# Optimizing a Trainium2 kernel written in Bass

```python
import numpy as np
import jax
import jax.numpy as jnp

def _softmax(x, axis=-1):
    return jax.nn.softmax(x, axis=axis)

def _gelu(x):
    return jax.nn.gelu(x, approximate=True)

def _silu(x):
    return jax.nn.silu(x)

def _sigmoid(x):
    return jax.nn.sigmoid(x)

def _layernorm(x, axis=-1, eps=1e-05):
    m = jnp.mean(x, axis=axis, keepdims=True)
    v = jnp.var(x, axis=axis, keepdims=True)
    return (x - m) / jnp.sqrt(v + eps)

def _scatter_add(tgt, idx, src, axis=0):
    return tgt.at[idx].add(src)

def _segment_sum(src, seg, n):
    return jax.ops.segment_sum(src, seg, n)
kernel_name = 'mk_recurrent_d2_jaxref_r8_a2236b'

def setup_inputs(seed: int=0):
    np.random.seed(seed)
    _w = jnp.asarray

    def _L0_attn_setup():
        import jax, jax.numpy as jnp
        import numpy as np
        key = jax.random.key(seed)
        ks = jax.random.split(key, 6)
        Bsz, S, H, N = (4, 512, 128, 32)
        return {'x': jax.random.normal(ks[0], (Bsz, S, H), jnp.float32), 'A': jax.random.normal(ks[1], (N, N), jnp.float32) * 0.01, 'Bm': jax.random.normal(ks[2], (N, N), jnp.float32) * 0.01, 'C': jax.random.normal(ks[3], (H, N), jnp.float32) * 0.01, 'D': jnp.full((H,), 0.01, jnp.float32), 'W_in': jax.random.normal(ks[4], (N, H), jnp.float32) / np.sqrt(H).astype(np.float32), 'b_in': jnp.zeros((N,), jnp.float32)}
    _L0_attn_in = _L0_attn_setup()

    def _L0_ffn_setup():
        import jax, jax.numpy as jnp
        import numpy as np
        B, S, D, H, E = (4, 256, 128, 512, 8)
        key = jax.random.key(seed)
        ks = jax.random.split(key, 8)
        s_d = 1.0 / np.sqrt(D)
        s_h = 1.0 / np.sqrt(H)
        return {'x': jax.random.normal(ks[0], (B, S, D), dtype=jnp.float32), 'gate_w': jax.random.uniform(ks[1], (E, D), jnp.float32, -s_d, s_d), 'gate_b': jax.random.uniform(ks[2], (E,), jnp.float32, -s_d, s_d), 'w1': jax.random.uniform(ks[3], (E, H, D), jnp.float32, -s_d, s_d), 'b1': jax.random.uniform(ks[4], (E, H), jnp.float32, -s_d, s_d), 'w2': jax.random.uniform(ks[5], (E, D, H), jnp.float32, -s_h, s_h), 'b2': jax.random.uniform(ks[6], (E, D), jnp.float32, -s_h, s_h)}
    _L0_ffn_in = _L0_ffn_setup()

    def _L1_attn_setup():
        import jax, jax.numpy as jnp
        import numpy as np
        import math
        EMBED_DIM = 128
        NHEAD = 16
        HEAD_DIM = 64
        BATCH = 2
        SEQ = 256
        key = jax.random.key(seed)
        k_in, k_wqkv, k_wo, k_g = jax.random.split(key, 4)
        std = math.sqrt(2.0 / EMBED_DIM)
        inputs = jax.random.normal(k_in, (BATCH, SEQ, EMBED_DIM), dtype=jnp.float32)
        Wqkv_w = jax.random.normal(k_wqkv, (3 * NHEAD * HEAD_DIM, EMBED_DIM), dtype=jnp.float32) * std
        Wqkv_b = jnp.zeros((3 * NHEAD * HEAD_DIM,), dtype=jnp.float32)
        Wo_w = jax.random.normal(k_wo, (EMBED_DIM, NHEAD * HEAD_DIM), dtype=jnp.float32) * std
        Wo_b = jnp.zeros((EMBED_DIM,), dtype=jnp.float32)
        ghost = jax.random.uniform(k_g, (NHEAD,), dtype=jnp.float32) * 0.1
        return {'inputs': inputs, 'Wqkv_w': Wqkv_w, 'Wqkv_b': Wqkv_b, 'Wo_w': Wo_w, 'Wo_b': Wo_b, 'ghost': ghost}
    _L1_attn_in = _L1_attn_setup()

    def _L1_ffn_setup():
        import jax, jax.numpy as jnp
        import numpy as np
        import math
        B, S, D = (4, 256, 128)
        H = 16
        E = 8
        K = 2
        F = 512

        def _layernorm(x, g, b, eps=1e-05):
            mu = jnp.mean(x, axis=-1, keepdims=True)
            var = jnp.mean(jnp.square(x - mu), axis=-1, keepdims=True)
            return (x - mu) * jax.lax.rsqrt(var + eps) * g + b

        def _attention(x, Wq, bq, Wk, bk, Wv, bv, Wo, bo):
            b, s, d = x.shape
            dh = d // H
            q = (x @ Wq + bq).reshape(b, s, H, dh)
            k = (x @ Wk + bk).reshape(b, s, H, dh)
            v = (x @ Wv + bv).reshape(b, s, H, dh)
            scores = jnp.einsum('bqhd,bkhd->bhqk', q, k) / math.sqrt(dh)
            attn = jax.nn.softmax(scores, axis=-1)
            out = jnp.einsum('bhqk,bkhd->bqhd', attn, v).reshape(b, s, d)
            return out @ Wo + bo

        def _moe(x, gate_w, gate_b, W1, b1, W2, b2):
            b, s, d = x.shape
            xt = x.reshape(b * s, d)
            probs = jax.nn.softmax(xt @ gate_w + gate_b, axis=-1)
            top_v, top_i = jax.lax.top_k(probs, K)
            combine = jnp.sum(jax.nn.one_hot(top_i, E, dtype=xt.dtype) * top_v[..., None], axis=1)
            out = jnp.zeros_like(xt)
            for e in range(E):
                h = jax.nn.gelu(xt @ W1[e] + b1[e], approximate=False) @ W2[e] + b2[e]
                out = out + combine[:, e:e + 1] * h
            return out.reshape(b, s, d)
        key = jax.random.key(seed)
        ks = jax.random.split(key, 16)
        s_d = 1.0 / math.sqrt(D)
        s_f = 1.0 / math.sqrt(F)
        return {'x': jax.random.normal(ks[0], (B, S, D), jnp.float32), 'Wq': jax.random.normal(ks[1], (D, D), jnp.float32) * s_d, 'Wk': jax.random.normal(ks[2], (D, D), jnp.float32) * s_d, 'Wv': jax.random.normal(ks[3], (D, D), jnp.float32) * s_d, 'Wo': jax.random.normal(ks[4], (D, D), jnp.float32) * s_d, 'bq': jnp.zeros((D,), jnp.float32), 'bk': jnp.zeros((D,), jnp.float32), 'bv': jnp.zeros((D,), jnp.float32), 'bo': jnp.zeros((D,), jnp.float32), 'ln1_g': jnp.ones((D,), jnp.float32), 'ln1_b': jnp.zeros((D,), jnp.float32), 'ln2_g': jnp.ones((D,), jnp.float32), 'ln2_b': jnp.zeros((D,), jnp.float32), 'gate_w': jax.random.normal(ks[5], (D, E), jnp.float32) * s_d, 'gate_b': jnp.zeros((E,), jnp.float32), 'W1': jax.random.normal(ks[6], (E, D, F), jnp.float32) * s_d, 'b1': jnp.zeros((E, F), jnp.float32), 'W2': jax.random.normal(ks[7], (E, F, D), jnp.float32) * s_f, 'b2': jnp.zeros((E, D), jnp.float32)}
    _L1_ffn_in = _L1_ffn_setup()
    _d = {'L0_attn_x': _L0_attn_in['x'], 'L0_attn_A': _L0_attn_in['A'], 'L0_attn_Bm': _L0_attn_in['Bm'], 'L0_attn_C': _L0_attn_in['C'], 'L0_attn_D': _L0_attn_in['D'], 'L0_attn_W_in': _L0_attn_in['W_in'], 'L0_attn_b_in': _L0_attn_in['b_in'], 'L0_ffn_gate_w': _L0_ffn_in['gate_w'], 'L0_ffn_gate_b': _L0_ffn_in['gate_b'], 'L0_ffn_w1': _L0_ffn_in['w1'], 'L0_ffn_b1': _L0_ffn_in['b1'], 'L0_ffn_w2': _L0_ffn_in['w2'], 'L0_ffn_b2': _L0_ffn_in['b2'], 'L1_attn_Wqkv_w': _L1_attn_in['Wqkv_w'], 'L1_attn_Wqkv_b': _L1_attn_in['Wqkv_b'], 'L1_attn_Wo_w': _L1_attn_in['Wo_w'], 'L1_attn_Wo_b': _L1_attn_in['Wo_b'], 'L1_attn_ghost': _L1_attn_in['ghost'], 'L1_ffn_Wq': _L1_ffn_in['Wq'], 'L1_ffn_bq': _L1_ffn_in['bq'], 'L1_ffn_Wk': _L1_ffn_in['Wk'], 'L1_ffn_bk': _L1_ffn_in['bk'], 'L1_ffn_Wv': _L1_ffn_in['Wv'], 'L1_ffn_bv': _L1_ffn_in['bv'], 'L1_ffn_Wo': _L1_ffn_in['Wo'], 'L1_ffn_bo': _L1_ffn_in['bo'], 'L1_ffn_ln1_g': _L1_ffn_in['ln1_g'], 'L1_ffn_ln1_b': _L1_ffn_in['ln1_b'], 'L1_ffn_ln2_g': _L1_ffn_in['ln2_g'], 'L1_ffn_ln2_b': _L1_ffn_in['ln2_b'], 'L1_ffn_gate_w': _L1_ffn_in['gate_w'], 'L1_ffn_gate_b': _L1_ffn_in['gate_b'], 'L1_ffn_W1': _L1_ffn_in['W1'], 'L1_ffn_b1': _L1_ffn_in['b1'], 'L1_ffn_W2': _L1_ffn_in['W2'], 'L1_ffn_b2': _L1_ffn_in['b2']}
    _x0 = _d['L0_attn_x']
    _d['L0_attn_x'] = jax.random.normal(jax.random.fold_in(jax.random.key(seed), 1), (32, 256, 128), dtype=_x0.dtype)
    del _x0
    return _d

def reference(L0_attn_x, L0_attn_A, L0_attn_Bm, L0_attn_C, L0_attn_D, L0_attn_W_in, L0_attn_b_in, L0_ffn_gate_w, L0_ffn_gate_b, L0_ffn_w1, L0_ffn_b1, L0_ffn_w2, L0_ffn_b2, L1_attn_Wqkv_w, L1_attn_Wqkv_b, L1_attn_Wo_w, L1_attn_Wo_b, L1_attn_ghost, L1_ffn_Wq, L1_ffn_bq, L1_ffn_Wk, L1_ffn_bk, L1_ffn_Wv, L1_ffn_bv, L1_ffn_Wo, L1_ffn_bo, L1_ffn_ln1_g, L1_ffn_ln1_b, L1_ffn_ln2_g, L1_ffn_ln2_b, L1_ffn_gate_w, L1_ffn_gate_b, L1_ffn_W1, L1_ffn_b1, L1_ffn_W2, L1_ffn_b2):

    def _L0_attn_ref(x, A, Bm, C, D, W_in, b_in):
        import jax, jax.numpy as jnp
        import numpy as np
        u = jnp.einsum('bsh,nh->bsn', x, W_in) + b_in
        uB = jnp.einsum('bsn,mn->bsm', u, Bm)

        def step(h, uB_t):
            h = h @ A + uB_t
            return (h, h)
        h0 = jnp.zeros((x.shape[0], A.shape[0]), x.dtype)
        _, hs = jax.lax.scan(step, h0, jnp.swapaxes(uB, 0, 1))
        hs = jnp.swapaxes(hs, 0, 1)
        return jnp.einsum('bsn,hn->bsh', hs, C) + D

    def _L0_ffn_ref(x, gate_w, gate_b, w1, b1, w2, b2):
        import jax, jax.numpy as jnp
        import numpy as np
        B, S, D, H, E = (4, 256, 128, 512, 8)
        b, s, d = x.shape
        xf = x.reshape(-1, d)
        logits = xf @ gate_w.T + gate_b
        top1 = jnp.argmax(logits, axis=-1)
        out = jnp.zeros_like(xf)
        n_experts = w1.shape[0]
        for e in range(n_experts):
            h = jax.nn.relu(xf @ w1[e].T + b1[e])
            y = h @ w2[e].T + b2[e]
            out = out + jnp.where((top1 == e)[:, None], y, jnp.zeros((), y.dtype))
        return out.reshape(b, s, d)

    def _L1_attn_ref(inputs, Wqkv_w, Wqkv_b, Wo_w, Wo_b, ghost):
        import jax, jax.numpy as jnp
        import numpy as np
        import math
        EMBED_DIM = 128
        NHEAD = 16
        HEAD_DIM = 64
        BATCH = 2
        SEQ = 256
        b, s, e = inputs.shape
        QKV = inputs @ Wqkv_w.T + Wqkv_b
        QKVh = QKV.reshape(b, s, 3, NHEAD, HEAD_DIM).transpose(0, 3, 2, 1, 4)
        Q, K, V = (QKVh[:, :, 0], QKVh[:, :, 1], QKVh[:, :, 2])
        scores = jnp.einsum('bhqd,bhkd->bhqk', Q, K) / math.sqrt(HEAD_DIM)
        row = jnp.arange(s)
        mask = jnp.where(row[None, :] > row[:, None], -jnp.inf, 0.0).astype(scores.dtype)
        scores = scores + mask[None, None]
        m = jnp.max(scores, axis=-1, keepdims=True)
        z = jnp.exp(scores - m)
        S = z / (jnp.sum(z, axis=-1, keepdims=True) + ghost.reshape(1, -1, 1, 1))
        A = jnp.einsum('bhqk,bhkd->bhqd', S, V)
        A = A.transpose(0, 2, 1, 3).reshape(b, s, NHEAD * HEAD_DIM)
        return A @ Wo_w.T + Wo_b

    def _L1_ffn_ref(x, Wq, bq, Wk, bk, Wv, bv, Wo, bo, ln1_g, ln1_b, ln2_g, ln2_b, gate_w, gate_b, W1, b1, W2, b2):
        import jax, jax.numpy as jnp
        import numpy as np
        import math
        B, S, D = (4, 256, 128)
        H = 16
        E = 8
        K = 2
        F = 512

        def _layernorm(x, g, b, eps=1e-05):
            mu = jnp.mean(x, axis=-1, keepdims=True)
            var = jnp.mean(jnp.square(x - mu), axis=-1, keepdims=True)
            return (x - mu) * jax.lax.rsqrt(var + eps) * g + b

        def _attention(x, Wq, bq, Wk, bk, Wv, bv, Wo, bo):
            b, s, d = x.shape
            dh = d // H
            q = (x @ Wq + bq).reshape(b, s, H, dh)
            k = (x @ Wk + bk).reshape(b, s, H, dh)
            v = (x @ Wv + bv).reshape(b, s, H, dh)
            scores = jnp.einsum('bqhd,bkhd->bhqk', q, k) / math.sqrt(dh)
            attn = jax.nn.softmax(scores, axis=-1)
            out = jnp.einsum('bhqk,bkhd->bqhd', attn, v).reshape(b, s, d)
            return out @ Wo + bo

        def _moe(x, gate_w, gate_b, W1, b1, W2, b2):
            b, s, d = x.shape
            xt = x.reshape(b * s, d)
            probs = jax.nn.softmax(xt @ gate_w + gate_b, axis=-1)
            top_v, top_i = jax.lax.top_k(probs, K)
            combine = jnp.sum(jax.nn.one_hot(top_i, E, dtype=xt.dtype) * top_v[..., None], axis=1)
            out = jnp.zeros_like(xt)
            for e in range(E):
                h = jax.nn.gelu(xt @ W1[e] + b1[e], approximate=False) @ W2[e] + b2[e]
                out = out + combine[:, e:e + 1] * h
            return out.reshape(b, s, d)
        x = x + _layernorm(_attention(x, Wq, bq, Wk, bk, Wv, bv, Wo, bo), ln1_g, ln1_b)
        x = x + _layernorm(_moe(x, gate_w, gate_b, W1, b1, W2, b2), ln2_g, ln2_b)
        return x
    x = L0_attn_x
    xn = _layernorm(x, axis=-1)
    s = _L0_attn_ref(xn, L0_attn_A, L0_attn_Bm, L0_attn_C, L0_attn_D, L0_attn_W_in, L0_attn_b_in)
    g = _silu(_L0_ffn_ref(xn, L0_ffn_gate_w, L0_ffn_gate_b, L0_ffn_w1, L0_ffn_b1, L0_ffn_w2, L0_ffn_b2))
    x = x + s * g
    xn = _layernorm(x, axis=-1)
    s = _L1_attn_ref(xn, L1_attn_Wqkv_w, L1_attn_Wqkv_b, L1_attn_Wo_w, L1_attn_Wo_b, L1_attn_ghost)
    g = _silu(_L1_ffn_ref(xn, L1_ffn_Wq, L1_ffn_bq, L1_ffn_Wk, L1_ffn_bk, L1_ffn_Wv, L1_ffn_bv, L1_ffn_Wo, L1_ffn_bo, L1_ffn_ln1_g, L1_ffn_ln1_b, L1_ffn_ln2_g, L1_ffn_ln2_b, L1_ffn_gate_w, L1_ffn_gate_b, L1_ffn_W1, L1_ffn_b1, L1_ffn_W2, L1_ffn_b2))
    x = x + s * g
    return x

_drawn_inputs = setup_inputs


def setup_inputs(seed=0):
    import zlib

    import numpy as np

    out = dict(_drawn_inputs(seed))
    spreads = {'L0_attn_D': (0.009999999776482582, 0.6),
     'L0_attn_b_in': (0.0, 0.8),
     'L1_attn_Wqkv_b': (0.0, 0.1),
     'L1_attn_Wo_b': (0.0, 0.521),
     'L1_ffn_bq': (0.0, 0.1),
     'L1_ffn_bk': (0.0, 2.0),
     'L1_ffn_bv': (0.0, 0.1),
     'L1_ffn_bo': (0.0, 0.1),
     'L1_ffn_ln1_g': (1.0, 0.2),
     'L1_ffn_ln1_b': (0.0, 0.1),
     'L1_ffn_ln2_g': (1.0, 0.2),
     'L1_ffn_ln2_b': (0.0, 0.4),
     'L1_ffn_gate_b': (0.0, 0.32),
     'L1_ffn_b1': (0.0, 0.581),
     'L1_ffn_b2': (0.0, 0.398)}
    factors = {'L0_attn_A': 8.0,
     'L0_attn_Bm': 7.626,
     'L0_attn_C': 8.0,
     'L0_attn_W_in': 7.721,
     'L0_ffn_gate_w': 4.108,
     'L0_ffn_gate_b': 8.0,
     'L0_ffn_w1': 5.539,
     'L0_ffn_b1': 8.0,
     'L0_ffn_w2': 4.763,
     'L0_ffn_b2': 8.0,
     'L1_attn_ghost': 13.051}
    for name, (base, spread) in spreads.items():
        noise = np.random.default_rng([zlib.crc32(name.encode()), seed]).standard_normal(out[name].shape)
        drawn = base * np.exp(spread * noise) if base else spread * noise
        out[name] = jnp.asarray(drawn.astype(out[name].dtype))
    for name, factor in factors.items():
        out[name] = (out[name] * factor).astype(out[name].dtype)
    return out
```

```python
from contextlib import ExitStack, contextmanager

import concourse.bass as bass
from concourse import mybir

ALU = mybir.AluOpType
ACT = mybir.ActivationFunctionType
F32 = mybir.dt.float32
BF16 = mybir.dt.bfloat16
I32 = mybir.dt.int32
AX_X = mybir.AxisListType.X

P = 128
BATCH, SEQ, D = 32, 256, 128
TOKENS = BATCH * SEQ
TILES = TOKENS // P
EXPERTS, HIDDEN = 8, 512
HC = HIDDEN // P
SLOTS = 256
EPS = 1e-5
CHUNKS = 4
CT = TILES // CHUNKS
N_STATE = 32
NEG = -1.0e30


def expert_tiles(assigned):
    n = assigned // SLOTS + EXPERTS - 1
    return n + n % 2


class Chain:

    def __init__(self, eng, sem):
        self.eng, self.sem, self.n = eng, sem, 0

    def __call__(self, ins):
        self.n += 1
        ins.then_inc(self.sem, 1)
        self.eng.wait_ge(self.sem, self.n)


def over(ap, n, axis):
    a = ap.unsqueeze(axis)
    shape = list(a.shape)
    shape[axis] = n
    return a.to_broadcast(shape)


@contextmanager
def semaphore(nc, t, name):
    t["semaphores"].append(nc.alloc_semaphore(name=name))
    yield t["semaphores"][-1]


def clear(nc, t):
    nc.clear_and_free_semaphores(t["semaphores"])
    nc.all_engine_barrier()
    t["semaphores"] = []


def constants(nc, t):
    with semaphore(nc, t, "const_step") as step, nc.Block() as block:

        @block.gpsimd
        def _(pool):
            link = Chain(pool, step)
            link(nc.gpsimd.memset(t["ident"][:], 0.0))
            link(nc.gpsimd.affine_select(out=t["ident"][:], in_=t["ident"][:], compare_op=ALU.not_equal,
                                         fill=1.0, base=0, pattern=[[-1, P]], channel_multiplier=1))
            link(nc.gpsimd.tensor_copy(t["ident_b"][:], t["ident"][:]))
            link(nc.gpsimd.memset(t["ones"][:], 1.0))
            link(nc.gpsimd.affine_select(out=t["before"][:], in_=t["ones"][:], compare_op=ALU.is_gt,
                                         fill=0.0, base=0, pattern=[[1, P]], channel_multiplier=-1))
            link(nc.gpsimd.memset(t["zero_b"][:], 0.0))
            link(nc.gpsimd.affine_select(out=t["future_q"][:], in_=t["zero_b"][:], compare_op=ALU.is_ge,
                                         fill=NEG, base=0, pattern=[[-1, P]], channel_multiplier=1))
            link(nc.gpsimd.affine_select(out=t["future_k"][:], in_=t["zero_b"][:], compare_op=ALU.is_ge,
                                         fill=NEG, base=0, pattern=[[1, P]], channel_multiplier=-1))
            link(nc.gpsimd.iota(t["rank8"][:], pattern=[[-1, EXPERTS]], base=EXPERTS, channel_multiplier=0,
                                allow_small_or_imprecise_dtypes=True))
            n = t["tile_no"].shape[1]
            link(nc.gpsimd.iota(t["tile_no"][:], pattern=[[1, n]], base=0, channel_multiplier=0,
                                allow_small_or_imprecise_dtypes=True))
            link(nc.gpsimd.memset(t["eps"][:], EPS))
            link(nc.gpsimd.memset(t["zeros"][:], 0.0))


class Norm:

    def __init__(self, nc, sem, sb, name):
        self.nc = nc
        self.step = sem(name + "_dve_step")
        self.centred, self.squared = sem(name + "_centred"), sem(name + "_squared")
        self.summed, self.rooted = sem(name + "_summed"), sem(name + "_rooted")
        self.sq = sb(name + "_sq", [P, CT, D], F32)
        self.mean = sb(name + "_mean", [P, CT], F32)
        self.var = sb(name + "_var", [P, CT], F32)
        self.std = sb(name + "_std", [P, CT], F32)
        self.rstd = sb(name + "_rstd", [P, CT], F32)

    def vector(self, link, c, src, out):
        nc = self.nc
        link(nc.vector.tensor_reduce(self.mean[:], src, AX_X, ALU.add))
        link(nc.vector.tensor_scalar(self.mean[:], self.mean[:], 1.0 / D, None, ALU.mult))
        nc.vector.tensor_tensor(out, src, over(self.mean[:], D, 2), ALU.subtract).then_inc(self.centred, 1)
        link.eng.wait_ge(self.squared, c + 1)
        nc.vector.tensor_reduce(self.var[:], self.sq[:], AX_X, ALU.add).then_inc(self.summed, 1)
        link.eng.wait_ge(self.rooted, c + 1)
        link(nc.vector.reciprocal(self.rstd[:], self.std[:]))
        link(nc.vector.tensor_tensor(out, out, over(self.rstd[:], D, 2), ALU.mult))

    def scalar(self, act, c, out, eps):
        nc = self.nc
        act.wait_ge(self.centred, c + 1)
        if c:
            act.wait_ge(self.summed, c)
        nc.scalar.activation(self.sq[:], out, ACT.Square).then_inc(self.squared, 1)
        act.wait_ge(self.summed, c + 1)
        nc.scalar.activation(self.std[:], self.var[:], ACT.Sqrt, bias=eps, scale=1.0 / D).then_inc(self.rooted, 1)


def first_of(nc, link, out, values, best, work, rank8, tiles):
    link(nc.vector.tensor_reduce(best, values, AX_X, ALU.max))
    link(nc.vector.tensor_tensor(work, values, over(best, EXPERTS, 2), ALU.is_ge))
    link(nc.vector.tensor_tensor(work, work, over(rank8, tiles, 1), ALU.mult))
    link(nc.vector.tensor_reduce(best, work, AX_X, ALU.max))
    link(nc.vector.tensor_tensor(out, work, over(best, EXPERTS, 2), ALU.is_ge))


def route(nc, dve, link, t, r, n_assign, n_tiles, counted, ready):
    n = n_assign * TILES
    dve.wait_ge(counted, 1)
    flat = lambda x: x[:].rearrange("p t e -> p (t e)")
    ps = lambda x: x[:, 0:n_assign, :].rearrange("p b n -> p (b n)")
    link(nc.vector.tensor_copy(flat(r["total"]), ps(r["ps_total"])))
    for e in range(EXPERTS):
        link(nc.vector.tensor_tensor_scan(r["upto"][:, :, e], t["ones"][:, 0:n] if n <= P else t["ones"][:],
                                          r["total"][:, :, e], 0.0, ALU.mult, ALU.add))
    link(nc.vector.tensor_copy(r["count"][:], r["upto"][:, n - 1, :]))
    link(nc.vector.tensor_tensor(flat(r["upto"]), flat(r["upto"]), flat(r["total"]), ALU.subtract))
    link(nc.vector.tensor_tensor(flat(r["upto"]), flat(r["upto"]), ps(r["ps_rank"]), ALU.add))
    link(nc.vector.tensor_scalar(r["count_i"][:], r["count"][:], float(SLOTS - 1), None, ALU.add))
    link(nc.vector.tensor_single_scalar(r["count_i"][:], r["count_i"][:], SLOTS.bit_length() - 1,
                                        ALU.arith_shift_right))
    link(nc.vector.tensor_copy(r["count"][:], r["count_i"][:]))
    link(nc.vector.tensor_tensor_scan(r["last"][:], t["ones"][:, 0:EXPERTS], r["count"][:], 0.0,
                                      ALU.mult, ALU.add))
    link(nc.vector.tensor_tensor(r["base"][:], r["last"][:], r["count"][:], ALU.subtract))
    link(nc.vector.tensor_scalar(r["base"][:], r["base"][:], float(SLOTS), None, ALU.mult))
    link(nc.vector.tensor_tensor(r["upto"][:], r["upto"][:], over(r["base"][:], n, 1), ALU.add))
    link(nc.vector.tensor_tensor(flat(r["upto"]), flat(r["upto"]), flat(r["chosen"]), ALU.mult))
    link(nc.vector.tensor_reduce(r["slot_f"][:], r["upto"][:], AX_X, ALU.add))
    link(nc.vector.tensor_copy(r["slot"][:], r["slot_f"][:]))
    link(nc.vector.tensor_tensor(r["ended"][:], over(t["tile_no"][0:1, 0:n_tiles], EXPERTS, 2),
                                 over(r["last"][0:1, :], n_tiles, 1), ALU.is_ge))
    link(nc.vector.tensor_reduce(r["expert_f"][:], r["ended"][:], AX_X, ALU.add))
    nc.vector.tensor_scalar(r["expert"][:], r["expert_f"][:], float(EXPERTS - 1), None,
                            ALU.min).then_inc(ready, 1)


def route_counts(nc, pe, t, r, n_assign, counted):
    flat = r["chosen"][:].rearrange("p t e -> p (t e)")
    for a in range(n_assign):
        part = flat[:, a * 512:(a + 1) * 512]
        nc.tensor.matmul(r["ps_rank"][:, a, :], t["before"][:], part, start=True, stop=True)
        last = nc.tensor.matmul(r["ps_total"][:, a, :], t["ones"][:], part, start=True, stop=True)
    last.then_inc(counted, 1)


def route_buffers(sb, pb, n_assign, n_tiles, keep, tag):
    n = n_assign * TILES
    return dict(
        keep,
        chosen=sb("chosen" + tag, [P, n, EXPERTS], F32), total=sb("total" + tag, [P, n, EXPERTS], F32),
        upto=sb("upto" + tag, [P, n, EXPERTS], F32), count=sb("count" + tag, [P, EXPERTS], F32),
        count_i=sb("count_i" + tag, [P, EXPERTS], I32), last=sb("last" + tag, [P, EXPERTS], F32),
        base=sb("base" + tag, [P, EXPERTS], F32), slot_f=sb("slot_f" + tag, [P, n], F32),
        ended=sb("ended" + tag, [1, n_tiles, EXPERTS], F32), expert_f=sb("expert_f" + tag, [1, n_tiles], F32),
        ps_rank=pb("ps_rank" + tag, [P, n_assign, 512], F32), ps_total=pb("ps_total" + tag, [P, n_assign, 512], F32))


def layer0_front(nc, t, d):
    with ExitStack() as ctx:
        def sb(name, shape, dt):
            return ctx.enter_context(nc.sbuf_tensor(name, shape, dt))

        def pb(name, shape, dt):
            return ctx.enter_context(nc.psum_tensor(name, shape, dt))

        def sem(name):
            return ctx.enter_context(semaphore(nc, t, name))

        x, xn, s = t["x"], t["xn"], t["s"]
        xnT = sb("xnT", [P, TOKENS], F32)
        win = sb("win", [P, N_STATE], F32)
        bd = sb("bd", [P, 2, P], F32)
        bdT = sb("bdT", [P, P], F32)
        pw = sb("pw", [P, 8, P], F32)
        pwT = sb("pwT", [P, 8, P], F32)
        cpad = sb("cpad", [P, 4, P], F32)
        b_in = sb("b_in", [P, 1], F32)
        d_bc = sb("d_bc", [P, D], F32)
        gw = sb("gw", [P, P], F32)
        gb = sb("gb", [P, EXPERTS], F32)
        u = sb("u", [P, 2048], F32)
        h = sb("h", [P, 8, SEQ], F32)
        logits = sb("logits", [P, TILES, EXPERTS], F32)
        best = sb("best", [P, TILES], F32)
        norm = Norm(nc, sem, sb, "n0")
        ps = pb("ps", [P, 6, 512], F32)
        n_tiles = expert_tiles(TOKENS)
        r = route_buffers(sb, pb, 1, n_tiles, dict(slot=t["slot0"], expert=t["expert0"]), "0")

        x_in = [sem(f"x_in{c}") for c in range(CHUNKS)]
        w_in, w_zero = sem("w_in"), sem("w_zero")
        zeroed, scattered = sem("zeroed"), sem("scattered")
        xn_ready, tr_done, xnT_ready = sem("xn_ready"), sem("tr_done"), sem("xnT_ready")
        u_done, u_ready, ub_done, h0_ready = sem("u_done"), sem("u_ready"), sem("ub_done"), sem("h0_ready")
        sq_done, pw_ready = sem("sq_done"), sem("pw_ready")
        step_done, h_ready = sem("step_done"), sem("h_ready")
        s_done, s_ready = sem("s_done"), sem("s_ready")
        g_done, g_ready = sem("g_done"), sem("g_ready")
        chosen_ready, counted, routed = sem("chosen_ready"), sem("counted"), sem("routed")
        dve_step = sem("dve_step")
        GROUPS = TILES // 4

        with nc.Block() as block:

            @block.sync
            def _(sp):
                for c in range(CHUNKS):
                    sp.dma_start(x[:, c * CT:(c + 1) * CT, :],
                                 d["x"].rearrange("(t p) d -> p t d", p=P)[:, c * CT:(c + 1) * CT, :])\
                      .then_inc(x_in[c], 16)
                sp.wait_ge(w_zero, 5)
                for g in range(4):
                    q = slice(32 * g, 32 * g + 32)
                    sp.dma_start(bd[q, 0, q], d["BmT"]).then_inc(w_in, 16)
                    sp.dma_start(bd[q, 1, q], d["A"]).then_inc(w_in, 16)
                    sp.dma_start(bdT[q, q], d["AT"]).then_inc(w_in, 16)
                    sp.dma_start(cpad[q, g, :], d["CT"]).then_inc(w_in, 16)
                    sp.dma_start(b_in[q, :], d["b_in"]).then_inc(w_in, 16)
                sp.dma_start(win[:], d["W_inT"]).then_inc(w_in, 16)
                sp.dma_start(gw[:, 0:EXPERTS], d["gate0T"]).then_inc(w_in, 16)
                sp.dma_start(gb[:], d["gate0_b"].to_broadcast([P, EXPERTS])).then_inc(w_in, 16)
                sp.dma_start(d_bc[:], d["D"].to_broadcast([P, D])).then_inc(w_in, 16)
                n = 0
                for name, tiles in (("rows0", n_tiles), ("rows1", expert_tiles(2 * TOKENS))):
                    out = d[name].rearrange("(q p) d -> p q d", p=P)
                    for q in range(0, 2 * tiles, 4):
                        sp.dma_start(out[:, q:q + 4, :],
                                     t["zeros"][:].rearrange("p (q d) -> p q d", d=D)).then_inc(zeroed, 16)
                        n += 16
                t["n_zeroed"] = n
                sp.wait_ge(zeroed, n)

            W_ALL = 16 * 24

            @block.gpsimd
            def _(pool):
                for m in (bd, bdT, cpad, gw):
                    nc.gpsimd.memset(m[:], 0.0).then_inc(w_zero, 1)
                nc.gpsimd.memset(norm.mean[:], 0.0).then_inc(w_zero, 1)
                pool.wait_ge(routed, 1)
                pool.wait_ge(zeroed, t["n_zeroed"])
                for i in range(TILES):
                    pool.indirect_dma_start(d["rows0"], bass.IndirectOffsetOnAxis(t["slot0"][:, i:i + 1], 0),
                                            xn[:, i, :], None).then_inc(scattered, 16)
                pool.wait_ge(scattered, 16 * TILES)

            @block.scalar
            def _(act):
                for c in range(CHUNKS):
                    norm.scalar(act, c, xn[:, c * CT:(c + 1) * CT, :], t["eps"][:])
                    for g in range(4 * c, 4 * c + 4):
                        act.wait_ge(tr_done, g + 1)
                        nc.scalar.activation(xnT[:, g * 512:(g + 1) * 512], ps[:, g % 2, :],
                                             ACT.Copy).then_inc(xnT_ready, 1)
                act.wait_ge(w_in, W_ALL)
                for c in range(4):
                    act.wait_ge(u_done, c + 1)
                    nc.scalar.activation(u[:, c * 512:(c + 1) * 512], ps[:, 2 + c % 2, :], ACT.Identity,
                                         bias=b_in[:, 0:1]).then_inc(u_ready, 1)
                hf = h[:].rearrange("p b t -> p (b t)")
                for c in range(4):
                    act.wait_ge(ub_done, c + 1)
                    nc.scalar.activation(hf[:, c * 512:(c + 1) * 512], ps[:, 4 + c % 2, :],
                                         ACT.Copy).then_inc(h0_ready, 1)
                for k in range(7):
                    act.wait_ge(sq_done, k + 1)
                    nc.scalar.activation(pw[:, k + 1, :], ps[:, k % 2, 0:P], ACT.Copy).then_inc(pw_ready, 1)
                    nc.scalar.activation(pwT[:, k + 1, :], ps[:, k % 2, P:2 * P], ACT.Copy).then_inc(pw_ready, 1)

            @block.tensor
            def _(pe):
                for g in range(GROUPS):
                    pe.wait_ge(xn_ready, g // 4 + 1)
                    if g >= 2:
                        pe.wait_ge(xnT_ready, g - 1)
                    for i in range(4):
                        last = nc.tensor.transpose(ps[:, g % 2, i * P:(i + 1) * P], xn[:, 4 * g + i, :], t["ident"][:])
                    last.then_inc(tr_done, 1)
                pe.wait_ge(xnT_ready, GROUPS)
                pe.wait_ge(w_in, W_ALL)
                for c in range(4):
                    if c >= 2:
                        pe.wait_ge(u_ready, c - 1)
                    for g in range(4):
                        last = nc.tensor.matmul(ps[32 * g:32 * g + 32, 2 + c % 2, :], win[:],
                                                xnT[:, g * 2048 + c * 512:g * 2048 + (c + 1) * 512],
                                                start=True, stop=True)
                    last.then_inc(u_done, 1)
                for c in range(4):
                    pe.wait_ge(u_ready, c + 1)
                    if c >= 2:
                        pe.wait_ge(h0_ready, c - 1)
                    nc.tensor.matmul(ps[:, 4 + c % 2, :], bd[:, 0, :], u[:, c * 512:(c + 1) * 512],
                                     start=True, stop=True).then_inc(ub_done, 1)
                for k in range(7):
                    if k:
                        pe.wait_ge(pw_ready, 2 * k)
                    a, aT = (pw[:, k, :], pwT[:, k, :]) if k else (bd[:, 1, :], bdT[:])
                    nc.tensor.matmul(ps[:, k % 2, 0:P], aT, a, start=True, stop=True)
                    nc.tensor.matmul(ps[:, k % 2, P:2 * P], a, aT, start=True, stop=True).then_inc(sq_done, 1)
                pe.wait_ge(h0_ready, 4)
                pe.wait_ge(pw_ready, 14)
                for k in range(8):
                    for c in range(4):
                        n = 4 * k + c
                        if k:
                            pe.wait_ge(h_ready, n - 3)
                        if n >= 2:
                            pe.wait_ge(h_ready, n - 1)
                        nc.tensor.matmul(ps[:, 2 + c % 2, :], pw[:, k, :] if k else bd[:, 1, :],
                                         h[:, 2 * c:2 * c + 2, :], start=True, stop=True).then_inc(step_done, 1)
                pe.wait_ge(h_ready, 32)
                for q in range(GROUPS):
                    if q >= 2:
                        pe.wait_ge(s_ready, q - 1)
                    for i in range(4):
                        n = 4 * q + i
                        b, half = n // 2, n % 2
                        last = nc.tensor.matmul(ps[:, 4 + q % 2, i * P:(i + 1) * P],
                                                h[:, b % 8, half * P:(half + 1) * P], cpad[:, b // 8, :],
                                                start=True, stop=True)
                    last.then_inc(s_done, 1)
                for q in range(GROUPS):
                    if q >= 2:
                        pe.wait_ge(g_ready, q - 1)
                    for i in range(4):
                        n = 4 * q + i
                        last = nc.tensor.matmul(ps[:, q % 2, i * P:(i + 1) * P], xnT[:, n * P:(n + 1) * P], gw[:],
                                                start=True, stop=True)
                    last.then_inc(g_done, 1)
                pe.wait_ge(chosen_ready, 1)
                route_counts(nc, pe, t, r, 1, counted)

            @block.vector
            def _(dve):
                link = Chain(dve, dve_step)
                dve.wait_ge(w_zero, 5)
                for c in range(CHUNKS):
                    q = slice(c * CT, (c + 1) * CT)
                    dve.wait_ge(x_in[c], 16)
                    norm.vector(link, c, x[:, q, :], xn[:, q, :])
                    nc.vector.tensor_copy(best[:, 0:1], t["eps"][:]).then_inc(xn_ready, 1)
                dve.wait_ge(w_in, W_ALL)
                for k in range(8):
                    d_ = 1 << k
                    for c in range(4):
                        n = 4 * k + c
                        dve.wait_ge(step_done, n + 1)
                        if k:
                            dve.wait_ge(h_ready, n - 3)
                        part = h[:, 2 * c:2 * c + 2, d_:SEQ]
                        psv = ps[:, 2 + c % 2, :].rearrange("p (b t) -> p b t", t=SEQ)[:, :, 0:SEQ - d_]
                        nc.vector.tensor_tensor(part, psv, part, ALU.add).then_inc(h_ready, 1)
                for q in range(GROUPS):
                    dve.wait_ge(s_done, q + 1)
                    nc.vector.tensor_tensor(s[:, 4 * q:4 * q + 4, :],
                                            ps[:, 4 + q % 2, :].rearrange("p (i d) -> p i d", d=D),
                                            over(d_bc[:], 4, 1), ALU.add).then_inc(s_ready, 1)
                for q in range(GROUPS):
                    dve.wait_ge(g_done, q + 1)
                    nc.vector.tensor_tensor(logits[:, 4 * q:4 * q + 4, :],
                                            ps[:, q % 2, :].rearrange("p (i d) -> p i d", d=P)[:, :, 0:EXPERTS],
                                            over(gb[:], 4, 1), ALU.add).then_inc(g_ready, 1)
                dve.wait_ge(g_ready, GROUPS)
                dve.wait_ge(xn_ready, CHUNKS)
                first_of(nc, link, r["chosen"][:], logits[:], best[:], r["total"][:], t["rank8"][:], TILES)
                nc.vector.tensor_copy(norm.mean[:, 0:1], t["eps"][:]).then_inc(chosen_ready, 1)
                route(nc, dve, link, t, r, 1, n_tiles, counted, routed)


def experts(nc, t, d, tag, n_tiles, act_fn, expert):
    with ExitStack() as ctx:
        def sb(name, shape, dt):
            return ctx.enter_context(nc.sbuf_tensor(name + tag, shape, dt))

        def pb(name, shape, dt):
            return ctx.enter_context(nc.psum_tensor(name + tag, shape, dt))

        def sem(name):
            return [ctx.enter_context(semaphore(nc, t, f"{name}{tag}_{b}")) for b in range(2)]

        rows, outs = d["rows" + tag], d["outs" + tag]
        W = HIDDEN + HIDDEN + HC
        w = [sb(f"w{b}", [P, W], F32) for b in range(2)]
        b2 = [sb(f"b2{b}", [P, D], F32) for b in range(2)]
        xr = [sb(f"xr{b}", [P, 2, D], F32) for b in range(2)]
        xT = [sb(f"xT{b}", [P, SLOTS], F32) for b in range(2)]
        hid = [sb(f"hid{b}", [P, HC, SLOTS], F32) for b in range(2)]
        y = [sb(f"y{b}", [P, 2, D], F32) for b in range(2)]
        ps_x = [pb(f"ps_x{b}", [P, 512], F32) for b in range(2)]
        ps_h = [pb(f"ps_h{b}", [P, 2, 512], F32) for b in range(2)]
        ps_y = [pb(f"ps_y{b}", [P, 512], F32) for b in range(2)]

        w_in, x_in, tr_done, xT_ready = sem("w_in"), sem("x_in"), sem("tr_done"), sem("xT_ready")
        up_a, up_b, hid_a, hid_b = sem("up_a"), sem("up_b"), sem("hid_a"), sem("hid_b")
        down, y_ready, stored = sem("down"), sem("y_ready"), sem("stored")
        last_a = n_tiles // 2
        relu = act_fn == ACT.Relu

        with nc.Block() as block:

            @block.sync
            def _(sp):
                def load(a, first):
                    for b in range(2):
                        n = 2 * a + b
                        if not first:
                            sp.wait_ge(tr_done[b], a)
                        sp.dma_start(xr[b][:], rows.rearrange("(n r p) d -> n p r d", p=P, r=2)[bass.ds(n, 1)]
                                     .rearrange("o p r d -> p (o r) d")).then_inc(x_in[b], 16)
                        e = sp.value_load(expert[0:1, bass.ds(n, 1)], min_val=0, max_val=EXPERTS - 1)
                        if not first:
                            sp.wait_ge(y_ready[b], a)
                        sp.dma_start(w[b][:], d["w" + tag][bass.ds(e, 1)].rearrange("o p n -> p (o n)"))\
                          .then_inc(w_in[b], 16)
                        sp.dma_start(b2[b][:], d["b2_" + tag][bass.ds(e, 1), :].to_broadcast([P, D]))\
                          .then_inc(w_in[b], 16)

                load(0, True)
                with sp.Fori(1, last_a) as a:
                    load(a, False)

            @block.gpsimd
            def _(pool):
                def store(a):
                    for b in range(2):
                        pool.wait_ge(y_ready[b], a + 1)
                        pool.dma_start(outs.rearrange("(n r p) d -> n p r d", p=P, r=2)[bass.ds(2 * a + b, 1)]
                                       .rearrange("o p r d -> p (o r) d"), y[b][:]).then_inc(stored[b], 16)

                with pool.Fori(0, last_a) as a:
                    store(a)
                for b in range(2):
                    pool.wait_ge(stored[b], 16 * last_a)

            @block.scalar
            def _(act):
                def hidden(a, b, first):
                    if not first:
                        act.wait_ge(down[b], a)
                    act.wait_ge(w_in[b], 32 * a + 32)
                    for c in range(2 if relu else HC):
                        if c == 0:
                            act.wait_ge(up_a[b], a + 1)
                        if c == 2:
                            act.wait_ge(up_b[b], a + 1)
                        ins = nc.scalar.activation(hid[b][:, c, :],
                                                   ps_h[b][:, c // 2, (c % 2) * SLOTS:(c % 2 + 1) * SLOTS],
                                                   act_fn, bias=w[b][:, 2 * HIDDEN + c:2 * HIDDEN + c + 1])
                        if c == 1:
                            ins.then_inc(hid_a[b], 1)
                        if c == 3:
                            ins.then_inc(hid_b[b], 1)

                for b in range(2):
                    hidden(0, b, True)
                with act.Fori(1, last_a) as a:
                    for b in range(2):
                        hidden(a, b, False)

            @block.vector
            def _(dve):
                def turn(a, b, first):
                    dve.wait_ge(tr_done[b], a + 1)
                    if not first:
                        dve.wait_ge(up_b[b], a)
                    nc.vector.tensor_copy(xT[b][:], ps_x[b][:, 0:SLOTS]).then_inc(xT_ready[b], 1)

                def hidden(a, b, first):
                    if not relu:
                        return
                    if not first:
                        dve.wait_ge(down[b], a)
                    dve.wait_ge(w_in[b], 32 * a + 32)
                    dve.wait_ge(up_b[b], a + 1)
                    for c in (2, 3):
                        ins = nc.vector.tensor_scalar(
                            hid[b][:, c, :], ps_h[b][:, 1, (c - 2) * SLOTS:(c - 1) * SLOTS],
                            w[b][:, 2 * HIDDEN + c:2 * HIDDEN + c + 1], 0.0, ALU.add, ALU.max)
                    ins.then_inc(hid_b[b], 1)

                def output(a, b, first):
                    dve.wait_ge(w_in[b], 32 * a + 32)
                    dve.wait_ge(down[b], a + 1)
                    if not first:
                        dve.wait_ge(stored[b], 16 * a)
                    nc.vector.tensor_tensor(y[b][:], ps_y[b][:, 0:2 * D].rearrange("p (r d) -> p r d", d=D),
                                            over(b2[b][:], 2, 1), ALU.add).then_inc(y_ready[b], 1)

                def step(a, first):
                    turn(a, 0, False)
                    hidden(a - 1, 1, first)
                    output(a - 1, 0, first)
                    turn(a, 1, False)
                    hidden(a, 0, False)
                    output(a - 1, 1, first)

                turn(0, 0, True)
                turn(0, 1, True)
                hidden(0, 0, True)
                step(1, True)
                with dve.Fori(2, last_a) as a:
                    step(a, False)
                hidden(last_a - 1, 1, False)
                output(last_a - 1, 0, False)
                output(last_a - 1, 1, False)

            @block.tensor
            def _(pe):
                def turn(a, b, first):
                    pe.wait_ge(x_in[b], 16 * a + 16)
                    if not first:
                        pe.wait_ge(xT_ready[b], a)
                    for r in range(2):
                        last = nc.tensor.transpose(ps_x[b][:, r * P:(r + 1) * P], xr[b][:, r, :], t["ident"][:])
                    last.then_inc(tr_done[b], 1)

                def up(a, b, first):
                    pe.wait_ge(xT_ready[b], a + 1)
                    pe.wait_ge(w_in[b], 32 * a + 32)
                    for c in range(HC):
                        if c == 0 and not first:
                            pe.wait_ge(hid_a[b], a)
                        if c == 2 and not first:
                            pe.wait_ge(hid_b[b], a)
                        last = nc.tensor.matmul(ps_h[b][:, c // 2, (c % 2) * SLOTS:(c % 2 + 1) * SLOTS],
                                                w[b][:, c * P:(c + 1) * P], xT[b][:], start=True, stop=True)
                        if c == 1:
                            last.then_inc(up_a[b], 1)
                    last.then_inc(up_b[b], 1)

                def down_(a, b, first):
                    pe.wait_ge(hid_a[b], a + 1)
                    pe.wait_ge(hid_b[b], a + 1)
                    if not first:
                        pe.wait_ge(y_ready[b], a)
                    for r in range(2):
                        for c in range(HC):
                            last = nc.tensor.matmul(ps_y[b][:, r * D:(r + 1) * D], hid[b][:, c, r * P:(r + 1) * P],
                                                    w[b][:, HIDDEN + c * D:HIDDEN + (c + 1) * D],
                                                    start=(c == 0), stop=(c == HC - 1))
                    last.then_inc(down[b], 1)

                def step(a, first):
                    turn(a, 0, False)
                    up(a - 1, 1, first)
                    down_(a - 1, 0, first)
                    turn(a, 1, False)
                    up(a, 0, False)
                    down_(a - 1, 1, first)

                turn(0, 0, True)
                turn(0, 1, True)
                up(0, 0, True)
                step(1, True)
                with pe.Fori(2, last_a) as a:
                    step(a, False)
                up(last_a - 1, 1, False)
                down_(last_a - 1, 0, False)
                down_(last_a - 1, 1, False)


def layer0_join(nc, t, d):
    with ExitStack() as ctx:
        def sb(name, shape, dt):
            return ctx.enter_context(nc.sbuf_tensor(name, shape, dt))

        def pb(name, shape, dt):
            return ctx.enter_context(nc.psum_tensor(name, shape, dt))

        def sem(name):
            return ctx.enter_context(semaphore(nc, t, name))

        x, xn, s = t["x"], t["xn"], t["s"]
        g = sb("g_rows", [P, TILES, D], F32)
        xnT = sb("xnT_b", [P, 4, 512], F32)
        norm = Norm(nc, sem, sb, "n1")
        ps = pb("ps_t", [P, 4, 512], F32)
        got = [sem(f"got{c}") for c in range(CHUNKS)]
        gated, xn_ready = sem("gated"), sem("xn1_ready")
        tr_done, xnT_ready, xnT_out = sem("tr1_done"), sem("xnT1_ready"), [sem(f"xnT_out{i}") for i in range(4)]
        dve_step, x_out = sem("dve1_step"), sem("x_out")
        GROUPS = TILES // 4

        with nc.Block() as block:

            @block.gpsimd
            def _(pool):
                for i in range(TILES):
                    pool.indirect_dma_start(g[:, i, :], None, d["outs0"],
                                            bass.IndirectOffsetOnAxis(t["slot0"][:, i:i + 1], 0))\
                        .then_inc(got[i // CT], 16)

            @block.scalar
            def _(act):
                def silu(c):
                    act.wait_ge(got[c], 16 * CT)
                    nc.scalar.activation(g[:, c * CT:(c + 1) * CT, :], g[:, c * CT:(c + 1) * CT, :],
                                         ACT.Silu).then_inc(gated, 1)

                silu(0)
                for c in range(CHUNKS):
                    if c + 1 < CHUNKS:
                        silu(c + 1)
                    norm.scalar(act, c, xn[:, c * CT:(c + 1) * CT, :], t["eps"][:])
                    for q in range(4 * c, 4 * c + 4):
                        act.wait_ge(tr_done, q + 1)
                        if q >= 4:
                            act.wait_ge(xnT_out[q % 4], 16 * (q // 4))
                        nc.scalar.activation(xnT[:, q % 4, :], ps[:, q % 4, :], ACT.Copy).then_inc(xnT_ready, 1)

            @block.tensor
            def _(pe):
                for q in range(GROUPS):
                    pe.wait_ge(xn_ready, q // 4 + 1)
                    if q >= 4:
                        pe.wait_ge(xnT_ready, q - 3)
                    for i in range(4):
                        last = nc.tensor.transpose(ps[:, q % 4, i * P:(i + 1) * P], xn[:, 4 * q + i, :], t["ident"][:])
                    last.then_inc(tr_done, 1)

            @block.sync
            def _(sp):
                for q in range(GROUPS):
                    sp.wait_ge(xnT_ready, q + 1)
                    sp.dma_start(d["xnT"][:, q * 512:(q + 1) * 512], xnT[:, q % 4, :]).then_inc(xnT_out[q % 4], 16)
                    if q % 4 == 3:
                        sp.dma_start(d["x_rows"].rearrange("(t p) d -> p t d", p=P)[:, 4 * q - 12:4 * q + 4, :],
                                     x[:, 4 * q - 12:4 * q + 4, :]).then_inc(x_out, 16)
                for i in range(4):
                    sp.wait_ge(xnT_out[i], 16 * GROUPS // 4)
                sp.wait_ge(x_out, 16 * CHUNKS)

            @block.vector
            def _(dve):
                link = Chain(dve, dve_step)
                for c in range(CHUNKS):
                    q = slice(c * CT, (c + 1) * CT)
                    dve.wait_ge(gated, c + 1)
                    link(nc.vector.tensor_tensor(g[:, q, :], g[:, q, :], s[:, q, :], ALU.mult))
                    link(nc.vector.tensor_tensor(x[:, q, :], x[:, q, :], g[:, q, :], ALU.add))
                    norm.vector(link, c, x[:, q, :], xn[:, q, :])
                    nc.vector.tensor_copy(norm.mean[:, 0:1], t["eps"][:]).then_inc(xn_ready, 1)


HEADS_B, DH_B = 16, 8
PAIRS = ((0, 0), (0, 1), (1, 0), (1, 1), (0, 2), (2, 0))
M_ROW = 64
STACK = M_ROW + 3


def wait(eng, sem, value):
    if not isinstance(value, int) or value > 0:
        eng.wait_ge(sem, value)


def pipelined(eng, count, step):
    step(0, 0, 2)
    step(1, 1, 2)
    with eng.Fori(1, count // 2 - 1) as i:
        step(2 * i, 0, 2)
        step(2 * i + 1, 1, 2)
    step(count - 2, 0, 1)
    step(count - 1, 1, 0)


def small_attention(nc, t, d):
    with ExitStack() as ctx:
        def sb(name, shape, dt):
            return ctx.enter_context(nc.sbuf_tensor("f_" + name, shape, dt))

        def pb(name, shape, dt):
            return ctx.enter_context(nc.psum_tensor("f_" + name, shape, dt))

        def sem(name):
            return ctx.enter_context(semaphore(nc, t, "f_" + name))

        def two(make, name, *more):
            return [make(f"{name}{b}", *more) for b in range(2)]

        H, T = HEADS_B, SEQ
        wq, wk, wv = (sb(n, [P, D], F32) for n in ("wq", "wk", "wv"))
        wo = sb("wo", [P, 4, D], F32)
        bq, bk = sb("bq", [P, 1], F32), sb("bk", [P, 1], F32)
        bv, bo = sb("bv", [P, D], F32), sb("bo", [P, D], F32)
        pick = sb("pick", [P, P], F32)
        slab = two(sb, "slab", [P, T], F32)
        qk = two(sb, "qk", [P, 2, T], F32)
        rest = sb("rest", [P, 2, T], F32)
        parts = two(sb, "parts", [P, 3, 2, T], BF16)
        qs, ks = two(sb, "qs", [STACK, H, T], BF16), two(sb, "ks", [STACK, H, T], BF16)
        v = two(sb, "v", [P, 2, H, 32], F32)
        nmax = two(sb, "nmax", [P, 2, H], F32)
        mrest = sb("mrest", [P, 2, H], F32)
        mparts = two(sb, "mparts", [P, 2, 3, H], BF16)
        mT = two(sb, "mT", [3 * H, T], BF16)
        prob = two(sb, "prob", [P, 4, 2 * T], F32)
        o = sb("o", [P, 4, T], F32)
        rec = two(sb, "rec", [P, T], F32)
        on = sb("on", [P, 4, T], F32)
        ps_s, ps_t, ps_o = (two(pb, n, [P, 2 * T], F32) for n in ("ps_s", "ps_t", "ps_o"))
        ps_q, ps_m = pb("ps_q", [P, 512], F32), pb("ps_m", [P, 512], F32)
        N = BATCH

        w_in, ready = sem("w_in"), sem("ready")
        slab_in, stack_in, max_in = two(sem, "slab_in"), two(sem, "stack_in"), two(sem, "max_in")
        qk_done, qk_ready, v_done, v_ready = sem("qk_done"), sem("qk_ready"), sem("v_done"), sem("v_ready")
        part0, rest1, part1, parts_ready = sem("part0"), sem("rest1"), sem("part1"), sem("parts_ready")
        mpart0, mrest1, mpart1, mparts_ready = sem("mpart0"), sem("mrest1"), sem("mpart1"), sem("mparts_ready")
        s_done, max_done, mT_done, mT_ready = sem("s_done"), sem("max_done"), sem("mT_done"), sem("mT_ready")
        st_done, exp_done, o_done, o_ready = sem("st_done"), sem("exp_done"), sem("o_done"), sem("o_ready")
        sum_done, rec_done, on_ready = sem("sum_done"), sem("rec_done"), sem("on_ready")
        z_done, z_ready = sem("z_done"), sem("z_ready")
        R = 11

        with nc.Block() as block:

            @block.sync
            def _(sp):
                def load(q, b):
                    wait(sp, v_done, q - 1)
                    sp.dma_start(slab[b][:], d["xnT"][:, bass.ds(q * T, T)]).then_inc(slab_in[b], 16)

                def stack(q, b, nth):
                    sp.wait_ge(parts_ready, q + 1)
                    for s_, pair in enumerate(PAIRS):
                        for z, (dst, part) in enumerate(zip((qs[b], ks[b]), pair)):
                            sp.dma_start(dst[8 * s_:8 * s_ + 8, :, :],
                                         parts[b][:, part, z, :])\
                              .then_inc(stack_in[b], 16)

                def maxima(q, b):
                    sp.wait_ge(mT_ready, q + 1)
                    sp.dma_start(qs[b][M_ROW:STACK, :, :], mT[b][:])\
                      .then_inc(max_in[b], 16)

                for w, n in ((wq, "Wq"), (wk, "Wk"), (wv, "Wv"), (bq, "bq"), (bk, "bk")):
                    sp.dma_start(w[:], d["f_" + n]).then_inc(w_in, 16)
                for w, n in ((bv, "bv"), (bo, "bo")):
                    sp.dma_start(w[:], d["f_" + n].to_broadcast([P, D])).then_inc(w_in, 16)
                sp.wait_ge(ready, R)
                for g in range(4):
                    for j in range(4):
                        h = 4 * g + j
                        sp.dma_start(wo[32 * j:32 * j + 8, g, :], d["f_Wo"][8 * h:8 * h + 8, :]).then_inc(w_in, 16)
                load(0, 0)
                load(1, 1)
                stack(0, 0, 0)
                load(2, 0)
                stack(1, 1, 1)
                load(3, 1)
                maxima(0, 0)

                def step(m, b, more):
                    if more >= 1:
                        maxima(m + 1, 1 - b)
                    if more >= 2:
                        stack(m + 2, b, 0)
                        if not (isinstance(m, int) and m + 4 >= N):
                            load(m + 4, b)

                step(0, 0, 2)
                step(1, 1, 2)
                with sp.Fori(1, N // 2 - 2) as i:
                    step(2 * i, 0, 2)
                    step(2 * i + 1, 1, 2)
                for m in range(N - 4, N):
                    step(m, m % 2, min(2, N - 1 - m))

            W_ALL = 16 * (5 + 2 + 16)

            @block.gpsimd
            def _(pool):
                fills = [(m[:], 0.0) for m in (*qs, *v, wo, pick)]
                fills += [(ks[b][0:M_ROW, :, :], 0.0) for b in range(2)]
                fills += [(ks[b][M_ROW:STACK, :, :], 1.0) for b in range(2)]
                for n, (m, value) in enumerate(fills):
                    nc.gpsimd.memset(m, value).then_inc(ready, 1)
                    pool.wait_ge(ready, n + 1)
                nc.gpsimd.affine_select(out=pick[:].rearrange("p (g c) -> p g c", c=32),
                                        in_=pick[:].rearrange("p (g c) -> p g c", c=32),
                                        compare_op=ALU.not_equal, fill=1.0, base=-8, pattern=[[-32, 4], [0, 32]],
                                        channel_multiplier=1).then_inc(ready, 1)

                def split(q, b):
                    pool.wait_ge(part0, q + 1)
                    wait(pool, parts_ready, q)
                    nc.gpsimd.tensor_tensor(rest[:], qk[b][:], parts[b][:, 0, :, :], ALU.subtract).then_inc(rest1, 1)
                    nc.gpsimd.tensor_tensor(parts[b][:, 1, :, :], qk[b][:], parts[b][:, 0, :, :],
                                            ALU.subtract).then_inc(part1, 1)
                    pool.wait_ge(rest1, q + 1)
                    pool.wait_ge(part1, q + 1)
                    nc.gpsimd.tensor_tensor(parts[b][:, 2, :, :], rest[:], parts[b][:, 1, :, :],
                                            ALU.subtract).then_inc(parts_ready, 1)

                def split_max(q, b):
                    pool.wait_ge(mpart0, q + 1)
                    wait(pool, mparts_ready, q)
                    nc.gpsimd.tensor_tensor(mrest[:], nmax[b][:], mparts[b][:, :, 0, :],
                                            ALU.subtract).then_inc(mrest1, 1)
                    nc.gpsimd.tensor_tensor(mparts[b][:, :, 1, :], nmax[b][:], mparts[b][:, :, 0, :],
                                            ALU.subtract).then_inc(mpart1, 1)
                    pool.wait_ge(mrest1, q + 1)
                    pool.wait_ge(mpart1, q + 1)
                    nc.gpsimd.tensor_tensor(mparts[b][:, :, 2, :], mrest[:], mparts[b][:, :, 1, :],
                                            ALU.subtract).then_inc(mparts_ready, 1)

                split(0, 0)
                split(1, 1)
                split_max(0, 0)

                def step(m, b, more):
                    if more >= 1:
                        split_max(m + 1, 1 - b)
                    if more >= 2:
                        split(m + 2, b)

                pipelined(pool, N, step)

            @block.scalar
            def _(act):
                def project(q, b):
                    act.wait_ge(qk_done, q + 1)
                    wait(act, parts_ready, q - 1)
                    nc.scalar.activation(qk[b][:, 0, :], ps_q[:, 0:T], ACT.Identity, bias=bq[:, 0:1],
                                         scale=DH_B ** -0.5).then_inc(qk_ready, 1)
                    nc.scalar.activation(qk[b][:, 1, :], ps_q[:, T:2 * T], ACT.Identity,
                                         bias=bk[:, 0:1]).then_inc(qk_ready, 1)

                def exps(m, g):
                    for j in range(4):
                        h = 4 * g + j
                        act.wait_ge(st_done, H * m + h + 1)
                        if j == 0:
                            wait(act, o_done, 4 * m + g - 1)
                        nc.scalar.activation(prob[g % 2][:, j, :], ps_t[h % 2][:], ACT.Exp).then_inc(exp_done, 1)

                def take(m, g):
                    act.wait_ge(o_done, 4 * m + g + 1)
                    wait(act, on_ready, 4 * m + g - 3)
                    nc.scalar.activation(o[:, g, :], ps_o[g % 2][:, 0:T], ACT.Copy).then_inc(o_ready, 1)

                def turned(q, b):
                    act.wait_ge(mT_done, q + 1)
                    wait(act, max_in[b], 16 * ((q - b) // 2) if isinstance(q, int) else 8 * (q - b))
                    nc.scalar.activation(mT[b][:], ps_m[0:3 * H, 0:T], ACT.Copy).then_inc(mT_ready, 1)

                act.wait_ge(w_in, W_ALL)
                act.wait_ge(ready, R)
                nc.scalar.activation(bq[:], bq[:], ACT.Copy, scale=DH_B ** -0.5).then_inc(ready, 1)
                act.wait_ge(ready, R + 1)
                project(0, 0)
                project(1, 1)
                turned(0, 0)

                def step(m, b, more):
                    exps(m, 0)
                    for g in range(1, 4):
                        exps(m, g)
                        take(m, g - 1)
                    if more >= 1:
                        turned(m + 1, 1 - b)
                    take(m, 3)
                    if more >= 2:
                        project(m + 2, b)

                pipelined(act, N, step)

            @block.vector
            def _(dve):
                def values(q, b):
                    dve.wait_ge(v_done, q + 1)
                    wait(dve, o_done, 4 * (q - 1))
                    for r in range(2):
                        last = nc.vector.tensor_tensor(v[b][:, r, :, 0:8],
                                                       ps_q[:, r * D:(r + 1) * D].rearrange("p (h c) -> p h c", c=8),
                                                       bv[:].rearrange("p (h c) -> p h c", c=8), ALU.add)
                    last.then_inc(v_ready, 1)

                def first_part(q, b):
                    dve.wait_ge(qk_ready, 2 * q + 2)
                    wait(dve, stack_in[b], 192 * ((q - b) // 2) if isinstance(q, int) else 96 * (q - b))
                    nc.vector.tensor_copy(parts[b][:, 0, :, :], qk[b][:]).then_inc(part0, 1)

                def first_max_part(q, b):
                    dve.wait_ge(max_done, H * (q + 1))
                    wait(dve, mT_done, q - 1)
                    nc.vector.tensor_copy(mparts[b][:, :, 0, :], nmax[b][:]).then_inc(mpart0, 1)

                def maxima(q, b, g):
                    for h in range(4 * g, 4 * g + 4):
                        dve.wait_ge(s_done, H * q + h + 1)
                        if h == 0:
                            wait(dve, mparts_ready, q - 1)
                        nc.vector.tensor_reduce(nmax[b][:, :, h], ps_s[h % 2][:].rearrange("p (r k) -> p r k", r=2),
                                                AX_X, ALU.max, negate=True).then_inc(max_done, 1)

                def divide(m, g):
                    dve.wait_ge(sum_done, 4 * m + g + 1)
                    wait(dve, on_ready, 4 * m + g - 1)
                    nc.vector.reciprocal(rec[g % 2][:], ps_m[:, 0:T]).then_inc(rec_done, 1)
                    dve.wait_ge(rec_done, 4 * m + g + 1)
                    wait(dve, z_done, m)
                    nc.vector.tensor_tensor(on[:, g, :], o[:, g, :], rec[g % 2][:], ALU.mult).then_inc(on_ready, 1)

                def output(m):
                    dve.wait_ge(z_done, m + 1)
                    nc.vector.tensor_tensor(t["s"][:, bass.ds(2 * m, 2), :],
                                            ps_m[:, 0:2 * D].rearrange("p (r c) -> p r c", c=D),
                                            over(bo[:], 2, 1), ALU.add).then_inc(z_ready, 1)

                dve.wait_ge(ready, R)
                for b in range(2):
                    last = nc.vector.memset(v[b][:, :, :, 8:9], 1.0)
                last.then_inc(ready, 1)
                dve.wait_ge(w_in, W_ALL)
                dve.wait_ge(ready, R + 2)
                for q in range(2):
                    first_part(q, q)
                    values(q, q)
                for g in range(4):
                    maxima(0, 0, g)
                first_max_part(0, 0)

                def step(m, b, more):
                    for g in range(4):
                        if more >= 1:
                            maxima(m + 1, 1 - b, g)
                        if g >= 2:
                            divide(m, g - 2)
                    if more >= 1:
                        first_max_part(m + 1, 1 - b)
                    divide(m, 2)
                    divide(m, 3)
                    output(m)
                    if more >= 2:
                        first_part(m + 2, b)
                        values(m + 2, b)

                pipelined(dve, N, step)

            @block.tensor
            def _(pe):
                def project(q, b):
                    pe.wait_ge(slab_in[b], 16 * ((q - b) // 2 + 1) if isinstance(q, int) else 8 * (q - b) + 16)
                    wait(pe, v_ready, q)
                    nc.tensor.matmul(ps_q[:, 0:T], wq[:], slab[b][:], start=True, stop=True)
                    nc.tensor.matmul(ps_q[:, T:2 * T], wk[:], slab[b][:], start=True, stop=True).then_inc(qk_done, 1)

                def values(q, b):
                    pe.wait_ge(qk_ready, 2 * q + 2)
                    for r in range(2):
                        last = nc.tensor.matmul(ps_q[:, r * D:(r + 1) * D], slab[b][:, r * P:(r + 1) * P], wv[:],
                                                start=True, stop=True)
                    last.then_inc(v_done, 1)

                def by_queries(q, b, h):
                    if h == 0:
                        pe.wait_ge(stack_in[b], 192 * ((q - b) // 2 + 1) if isinstance(q, int)
                                   else 96 * (q - b) + 192)
                    wait(pe, max_done, H * q + h - 1)
                    for r in range(2):
                        last = nc.tensor.matmul(ps_s[h % 2][:, r * T:(r + 1) * T], qs[b][0:M_ROW, h, r * P:(r + 1) * P],
                                                ks[b][0:M_ROW, h, :], start=True, stop=True)
                    last.then_inc(s_done, 1)

                def by_keys(m, b, h):
                    if h == 0:
                        pe.wait_ge(max_in[b], 16 * ((m - b) // 2 + 1) if isinstance(m, int) else 8 * (m - b) + 16)
                    wait(pe, exp_done, H * m + h - 1)
                    for r in range(2):
                        last = nc.tensor.matmul(ps_t[h % 2][:, r * T:(r + 1) * T], ks[b][:, h, r * P:(r + 1) * P],
                                                qs[b][:, h, :], start=True, stop=True)
                    last.then_inc(st_done, 1)

                def weigh(m, b, g):
                    pe.wait_ge(exp_done, H * m + 4 * g + 4)
                    pe.wait_ge(v_ready, m + 1)
                    wait(pe, o_ready, 4 * m + g - 1)
                    for r in range(2):
                        for j in range(4):
                            last = nc.tensor.matmul(ps_o[g % 2][32 * j:32 * j + 32, 0:T], v[b][:, r, 4 * g + j, :],
                                                    prob[g % 2][:, j, r * T:(r + 1) * T], start=(r == 0), stop=(r == 1))
                    last.then_inc(o_done, 1)

                def sums(m, g, after, value):
                    pe.wait_ge(o_ready, 4 * m + g + 1)
                    wait(pe, after, value)
                    nc.tensor.matmul(ps_m[:, 0:T], pick[:], o[:, g, :], start=True, stop=True).then_inc(sum_done, 1)

                def turn(q, b):
                    pe.wait_ge(mparts_ready, q + 1)
                    wait(pe, rec_done, 4 * q - 2)
                    for r in range(2):
                        last = nc.tensor.matmul(ps_m[0:3 * H, r * P:(r + 1) * P],
                                                mparts[b][:, r, :, :].rearrange("p a h -> p (a h)"),
                                                t["ident_b"][:], start=True, stop=True)
                    last.then_inc(mT_done, 1)

                def project_out(m):
                    pe.wait_ge(on_ready, 4 * m + 4)
                    for r in range(2):
                        for g in range(4):
                            last = nc.tensor.matmul(ps_m[:, r * D:(r + 1) * D], on[:, g, r * P:(r + 1) * P],
                                                    wo[:, g, :], start=(g == 0), stop=(g == 3))
                    last.then_inc(z_done, 1)

                pe.wait_ge(w_in, W_ALL)
                pe.wait_ge(ready, R + 2)
                project(0, 0)
                values(0, 0)
                project(1, 1)
                values(1, 1)
                for h in range(H):
                    by_queries(0, 0, h)
                turn(0, 0)

                def step(m, b, more):
                    for g in range(4):
                        for h in range(4 * g, 4 * g + 4):
                            by_keys(m, b, h)
                            if more >= 1:
                                by_queries(m + 1, 1 - b, h)
                        if g >= 1:
                            weigh(m, b, g - 1)
                        if g == 2:
                            sums(m, 0, z_ready, m)
                        if g == 3:
                            sums(m, 1, rec_done, 4 * m + 1)
                    if more >= 1:
                        turn(m + 1, 1 - b)
                    weigh(m, b, 3)
                    if more >= 1:
                        sums(m, 2, mT_ready, m + 2)
                    else:
                        sums(m, 2, rec_done, 4 * m + 2)
                    if more >= 2:
                        project(m + 2, b)
                    sums(m, 3, rec_done, 4 * m + 3)
                    project_out(m)
                    if more >= 2:
                        values(m + 2, b)

                pipelined(pe, N, step)


def layer1_route(nc, t, d):
    with ExitStack() as ctx:
        def sb(name, shape, dt):
            return ctx.enter_context(nc.sbuf_tensor(name, shape, dt))

        def pb(name, shape, dt):
            return ctx.enter_context(nc.psum_tensor(name, shape, dt))

        def sem(name):
            return ctx.enter_context(semaphore(nc, t, "r1_" + name))

        xn, s = t["xn"], t["s"]
        g1, b1 = sb("ln1_g", [P, D], F32), sb("ln1_b", [P, D], F32)
        gw, gb = sb("gw1", [P, P], F32), sb("gb1", [P, EXPERTS], F32)
        xT = sb("x1T", [P, 2, 512], F32)
        prob = sb("prob1", [P, TILES, EXPERTS], F32)
        best, total = sb("best1", [P, TILES], F32), sb("total1s", [P, TILES], F32)
        norm = Norm(nc, sem, sb, "n2")
        ps = pb("ps_x1", [P, 2, 512], F32)
        n_tiles = expert_tiles(2 * TOKENS)
        r = route_buffers(sb, pb, 2, n_tiles, dict(slot=t["slot1"], expert=t["expert1"]), "1")
        ps_g = pb("ps_g1", [P, 2, 512], F32)

        w_in, w_zero, x1_ready, x1_out = sem("w_in"), sem("w_zero"), sem("x1_ready"), sem("x1_out")
        tr_done, xT_ready, g_done, g_ready = sem("tr_done"), sem("xT_ready"), sem("g_done"), sem("g_ready")
        shifted, exp_ready = sem("shifted"), sem("exp_ready")
        chosen_ready, counted, routed, scattered = sem("chosen"), sem("counted"), sem("routed"), sem("scattered")
        dve_step = sem("dve_step")
        GROUPS = TILES // 4

        with nc.Block() as block:

            @block.sync
            def _(sp):
                sp.wait_ge(w_zero, 1)
                sp.dma_start(gw[:, 0:EXPERTS], d["gate1"]).then_inc(w_in, 16)
                for m, n in ((gb, "gate1_b"), (g1, "ln1_g"), (b1, "ln1_b")):
                    sp.dma_start(m[:], d[n].to_broadcast([P, m.shape[1]])).then_inc(w_in, 16)
                for c in range(CHUNKS):
                    sp.wait_ge(x1_ready, c + 1)
                    sp.dma_start(d["x1_rows"].rearrange("(t p) d -> p t d", p=P)[:, c * CT:(c + 1) * CT, :],
                                 xn[:, c * CT:(c + 1) * CT, :]).then_inc(x1_out, 16)
                sp.wait_ge(x1_out, 16 * CHUNKS)

            @block.gpsimd
            def _(pool):
                nc.gpsimd.memset(gw[:], 0.0).then_inc(w_zero, 1)
                pool.wait_ge(routed, 1)
                for i in range(2 * TILES):
                    pool.indirect_dma_start(d["rows1"], bass.IndirectOffsetOnAxis(t["slot1"][:, i:i + 1], 0),
                                            xn[:, i % TILES, :], None).then_inc(scattered, 16)
                pool.wait_ge(scattered, 16 * 2 * TILES)

            @block.scalar
            def _(act):
                for c in range(CHUNKS):
                    norm.scalar(act, c, s[:, c * CT:(c + 1) * CT, :], t["eps"][:])
                    for q in range(4 * c, 4 * c + 4):
                        act.wait_ge(tr_done, q + 1)
                        if q >= 2:
                            act.wait_ge(g_done, q - 1)
                        nc.scalar.activation(xT[:, q % 2, :], ps[:, q % 2, :], ACT.Copy).then_inc(xT_ready, 1)
                act.wait_ge(shifted, 1)
                nc.scalar.activation(prob[:], prob[:], ACT.Exp).then_inc(exp_ready, 1)

            @block.tensor
            def _(pe):
                pe.wait_ge(w_in, 64)
                pe.wait_ge(w_zero, 1)

                def gate(q):
                    pe.wait_ge(xT_ready, q + 1)
                    if q >= 2:
                        pe.wait_ge(g_ready, q - 1)
                    for i in range(4):
                        last = nc.tensor.matmul(ps_g[:, q % 2, i * P:(i + 1) * P], xT[:, q % 2, i * P:(i + 1) * P],
                                                gw[:], start=True, stop=True)
                    last.then_inc(g_done, 1)

                for q in range(GROUPS):
                    pe.wait_ge(x1_ready, q // 4 + 1)
                    if q >= 2:
                        pe.wait_ge(xT_ready, q - 1)
                    for i in range(4):
                        last = nc.tensor.transpose(ps[:, q % 2, i * P:(i + 1) * P], xn[:, 4 * q + i, :], t["ident"][:])
                    last.then_inc(tr_done, 1)
                    if q:
                        gate(q - 1)
                gate(GROUPS - 1)
                pe.wait_ge(chosen_ready, 1)
                route_counts(nc, pe, t, r, 2, counted)

            @block.vector
            def _(dve):
                link = Chain(dve, dve_step)
                dve.wait_ge(w_in, 64)

                def logits(q):
                    dve.wait_ge(g_done, q + 1)
                    nc.vector.tensor_tensor(prob[:, 4 * q:4 * q + 4, :],
                                            ps_g[:, q % 2, :].rearrange("p (i d) -> p i d", d=P)[:, :, 0:EXPERTS],
                                            over(gb[:], 4, 1), ALU.add).then_inc(g_ready, 1)

                for c in range(CHUNKS):
                    q = slice(c * CT, (c + 1) * CT)
                    norm.vector(link, c, s[:, q, :], s[:, q, :])
                    link(nc.vector.tensor_tensor(s[:, q, :], s[:, q, :], over(g1[:], CT, 1), ALU.mult))
                    link(nc.vector.tensor_tensor(s[:, q, :], s[:, q, :], over(b1[:], CT, 1), ALU.add))
                    nc.vector.tensor_tensor(xn[:, q, :], xn[:, q, :], s[:, q, :], ALU.add).then_inc(x1_ready, 1)
                    if c:
                        for g in range(4 * c - 4, 4 * c):
                            logits(g)
                for g in range(GROUPS - 4, GROUPS):
                    logits(g)
                dve.wait_ge(g_ready, GROUPS)
                link(nc.vector.tensor_reduce(best[:], prob[:], AX_X, ALU.max))
                nc.vector.tensor_tensor(prob[:], prob[:], over(best[:], EXPERTS, 2), ALU.subtract).then_inc(shifted, 1)
                dve.wait_ge(exp_ready, 1)
                link(nc.vector.tensor_reduce(total[:], prob[:], AX_X, ALU.add))
                link(nc.vector.reciprocal(total[:], total[:]))
                link(nc.vector.tensor_tensor(prob[:], prob[:], over(total[:], EXPERTS, 2), ALU.mult))
                first, second = r["chosen"][:, 0:TILES, :], r["chosen"][:, TILES:2 * TILES, :]
                work = r["total"][:, 0:TILES, :]
                first_of(nc, link, first, prob[:], best[:], work, t["rank8"][:], TILES)
                link(nc.vector.tensor_tensor(work, prob[:], first, ALU.mult))
                link(nc.vector.tensor_reduce(t["weight1"][:, 0:TILES], work, AX_X, ALU.add))
                rest = r["total"][:, TILES:2 * TILES, :]
                link(nc.vector.scalar_tensor_tensor(rest, first, -2.0, prob[:], ALU.mult, ALU.add))
                first_of(nc, link, second, rest, best[:], work, t["rank8"][:], TILES)
                link(nc.vector.tensor_tensor(work, prob[:], second, ALU.mult))
                link(nc.vector.tensor_reduce(t["weight1"][:, TILES:2 * TILES], work, AX_X, ALU.add))
                nc.vector.tensor_copy(best[:, 0:1], t["eps"][:]).then_inc(chosen_ready, 1)
                route(nc, dve, link, t, r, 2, n_tiles, counted, routed)


HEADS_A, DH_A = 16, 64
PAIRS_A = HEADS_A // 2
QKV = HEADS_A * DH_A


def causal_attention(nc, t, d):
    with ExitStack() as ctx:
        def sb(name, shape, dt):
            return ctx.enter_context(nc.sbuf_tensor("a_" + name, shape, dt))

        def pb(name, shape, dt):
            return ctx.enter_context(nc.psum_tensor("a_" + name, shape, dt))

        def sem(name):
            return ctx.enter_context(semaphore(nc, t, "a_" + name))

        def two(make, name, *more):
            return [make(f"{name}{b}", *more) for b in range(2)]

        H, T, N, HP = HEADS_A, SEQ, BATCH, PAIRS_A
        SC = DH_A ** -0.5
        w = sb("w", [P, 3 * QKV], F32)
        wo = sb("wo", [P, HP, D], F32)
        bq, bq_s, bk = sb("bq", [P, HP], F32), sb("bq_s", [P, HP], F32), sb("bk", [P, HP], F32)
        bv, bo = sb("bv", [P, QKV], F32), sb("bo", [P, D], F32)
        ghost = sb("ghost", [P, HP], F32)
        minus = sb("minus", [3, P], BF16)
        slab = two(sb, "slab", [P, T], F32)
        qT, kT = two(sb, "qT", [P, HP, T], F32), two(sb, "kT", [P, HP, T], F32)
        v = two(sb, "v", [P, 2, QKV], F32)
        blocks = two(sb, "blocks", [P, H, 3], F32)
        top = two(sb, "top", [P, 2, H], F32)
        mrest = sb("mrest", [P, 2, H], F32)
        mparts = two(sb, "mparts", [P, 2, 3, H], BF16)
        mT = two(sb, "mT", [3 * H, T], BF16)
        mrow = two(sb, "mrow", [3, H, T], BF16)
        prob = sb("prob", [P, 4, 3 * P], F32)
        o = two(sb, "o", [P, 2, T], F32)
        rec = two(sb, "rec", [P, T], F32)
        on = sb("on", [P, HP, T], F32)
        ps_s, ps_t, ps_o = (two(pb, n, [P, 512], F32) for n in ("ps_s", "ps_t", "ps_o"))
        ps_q, ps_m = pb("ps_q", [P, 512], F32), pb("ps_m", [P, 512], F32)

        w_in, ready = sem("w_in"), sem("ready")
        slab_in, max_in = two(sem, "slab_in"), two(sem, "max_in")
        qk_done, qk_act, qk_dve = sem("qk_done"), sem("qk_act"), sem("qk_dve")
        v_done, v_ready = sem("v_done"), sem("v_ready")
        s_done, max_done, first_top, top_ready = sem("s_done"), sem("max_done"), sem("first_top"), sem("top_ready")
        mpart0, mrest1, mpart1, mparts_ready = sem("mpart0"), sem("mrest1"), sem("mpart1"), sem("mparts_ready")
        mT_done, mT_ready = sem("mT_done"), sem("mT_ready")
        st_done, exp_done, o_done, o_ready = sem("st_done"), sem("exp_done"), sem("o_done"), sem("o_ready")
        rec_ready, on_ready, z_done, z_ready = sem("rec_ready"), sem("on_ready"), sem("z_done"), sem("z_ready")

        with nc.Block() as block:

            @block.sync
            def _(sp):
                def load(q, b):
                    wait(sp, v_done, 4 * (q - 1))
                    sp.dma_start(slab[b][:], d["xnT"][:, bass.ds(q * T, T)]).then_inc(slab_in[b], 16)

                def maxima(q, b):
                    sp.wait_ge(mT_ready, q + 1)
                    sp.dma_start(mrow[b][:], mT[b][:]).then_inc(max_in[b], 16)

                sp.dma_start(w[:], d["a_w"]).then_inc(w_in, 16)
                sp.dma_start(wo[:], d["a_wo"]).then_inc(w_in, 16)
                for m, n in ((bq, "a_bq"), (bk, "a_bk")):
                    sp.dma_start(m[:], d[n]).then_inc(w_in, 16)
                for m, n in ((bv, "a_bv"), (bo, "a_bo")):
                    sp.dma_start(m[:], d[n].to_broadcast([P, m.shape[1]])).then_inc(w_in, 16)
                for j in range(2):
                    sp.dma_start(ghost[64 * j:64 * j + 64, :], d["ghost"][j:j + 1, :].to_broadcast([64, HP]))\
                      .then_inc(w_in, 16)
                load(0, 0)
                load(1, 1)
                load(2, 0)
                load(3, 1)
                maxima(0, 0)

                def step(m, b, more, loads=True):
                    if more >= 1:
                        maxima(m + 1, 1 - b)
                    if loads:
                        load(m + 4, b)

                step(0, 0, 2)
                step(1, 1, 2)
                with sp.Fori(1, N // 2 - 2) as i:
                    step(2 * i, 0, 2)
                    step(2 * i + 1, 1, 2)
                for m in range(N - 4, N):
                    step(m, m % 2, N - 1 - m, False)

            W_ALL = 16 * 8

            @block.gpsimd
            def _(pool):
                nc.gpsimd.memset(minus[:], -1.0).then_inc(ready, 1)

                def split_max(q, b):
                    pool.wait_ge(mpart0, q + 1)
                    wait(pool, mparts_ready, q)
                    nc.gpsimd.tensor_tensor(mrest[:], top[b][:], mparts[b][:, :, 0, :], ALU.subtract).then_inc(mrest1, 1)
                    nc.gpsimd.tensor_tensor(mparts[b][:, :, 1, :], top[b][:], mparts[b][:, :, 0, :],
                                            ALU.subtract).then_inc(mpart1, 1)
                    pool.wait_ge(mrest1, q + 1)
                    pool.wait_ge(mpart1, q + 1)
                    nc.gpsimd.tensor_tensor(mparts[b][:, :, 2, :], mrest[:], mparts[b][:, :, 1, :],
                                            ALU.subtract).then_inc(mparts_ready, 1)

                def divide(m, p):
                    pool.wait_ge(rec_ready, HP * m + p + 1)
                    wait(pool, z_done, m)
                    nc.gpsimd.tensor_tensor(on[:, p, :], o[p % 2][:, 0, :], rec[p % 2][:], ALU.mult)\
                        .then_inc(on_ready, 1)

                split_max(0, 0)

                def step(m, b, more):
                    for p in range(HP - 1):
                        divide(m, p)
                    if more >= 1:
                        split_max(m + 1, 1 - b)
                    divide(m, HP - 1)

                pipelined(pool, N, step)

            @block.scalar
            def _(act):
                def project(q, b, p):
                    act.wait_ge(qk_done, HP * q + p + 1)
                    nc.scalar.activation(qT[b][:, p, :], ps_q[:, 0:T], ACT.Identity, bias=bq_s[:, p:p + 1], scale=SC)\
                      .then_inc(qk_act, 1)
                    nc.scalar.activation(kT[b][:, p, :], ps_q[:, T:2 * T], ACT.Identity, bias=bk[:, p:p + 1])\
                      .then_inc(qk_act, 1)

                def exps(m, p):
                    for h in (2 * p, 2 * p + 1):
                        act.wait_ge(st_done, H * m + h + 1)
                        if h % 2 == 0:
                            wait(act, o_done, HP * m + p - 1)
                        nc.scalar.activation(prob[:, h % 4, :], ps_t[h % 2][:, 0:3 * P], ACT.Exp).then_inc(exp_done, 1)

                def take(m, p):
                    act.wait_ge(o_done, HP * m + p + 1)
                    wait(act, on_ready, HP * m + p - 1)
                    nc.scalar.activation(o[p % 2][:, 0, :], ps_o[p % 2][:, 0:T], ACT.Copy).then_inc(o_ready, 1)
                    nc.scalar.activation(o[p % 2][:, 1, :], ps_o[p % 2][:, T:2 * T], ACT.Identity,
                                         bias=ghost[:, p:p + 1]).then_inc(o_ready, 1)

                def turned(q, b):
                    act.wait_ge(mT_done, q + 1)
                    wait(act, max_in[b], 16 * ((q - b) // 2) if isinstance(q, int) else 8 * (q - b))
                    nc.scalar.activation(mT[b][:], ps_m[0:3 * H, 0:T], ACT.Copy).then_inc(mT_ready, 1)

                act.wait_ge(w_in, W_ALL)
                nc.scalar.activation(bq_s[:], bq[:], ACT.Copy, scale=SC).then_inc(ready, 1)
                act.wait_ge(ready, 2)
                for q in range(2):
                    for p in range(0, HP, 2):
                        project(q, q, p)
                turned(0, 0)

                def step(m, b, more):
                    for p in range(HP):
                        exps(m, p)
                        if p:
                            take(m, p - 1)
                        if more >= 2 and p % 2 == 0:
                            project(m + 2, b, p)
                    if more >= 1:
                        turned(m + 1, 1 - b)
                    take(m, HP - 1)

                pipelined(act, N, step)

            @block.vector
            def _(dve):
                def project(q, b, p):
                    dve.wait_ge(qk_done, HP * q + p + 1)
                    nc.vector.tensor_scalar(qT[b][:, p, :], ps_q[:, 0:T], bq[:, p:p + 1], SC, ALU.add, ALU.mult)\
                      .then_inc(qk_dve, 1)
                    nc.vector.tensor_scalar(kT[b][:, p, :], ps_q[:, T:2 * T], bk[:, p:p + 1], None, ALU.add)\
                      .then_inc(qk_dve, 1)

                def values(q, b, n):
                    dve.wait_ge(v_done, 4 * q + n + 1)
                    wait(dve, o_done, HP * (q - 1))
                    cols = slice((n % 2) * 512, (n % 2 + 1) * 512)
                    nc.vector.tensor_tensor(v[b][:, n // 2, cols], ps_q[:], bv[:, cols], ALU.add).then_inc(v_ready, 1)

                def maximum(q, b, h):
                    dve.wait_ge(s_done, H * q + h + 1)
                    if h == 0:
                        wait(dve, top_ready, q - 1)
                    nc.vector.tensor_reduce(blocks[b][:, h, :], ps_s[h % 2][:, 0:3 * P].rearrange("p (n k) -> p n k", k=P),
                                            AX_X, ALU.max).then_inc(max_done, 1)

                def tops(q, b):
                    dve.wait_ge(max_done, H * (q + 1))
                    wait(dve, mparts_ready, q - 1)
                    nc.vector.tensor_copy(top[b][:, 0, :], blocks[b][:, :, 0]).then_inc(first_top, 1)
                    dve.wait_ge(first_top, q + 1)
                    nc.vector.tensor_tensor(top[b][:, 1, :], blocks[b][:, :, 1], blocks[b][:, :, 2], ALU.max)\
                      .then_inc(top_ready, 1)
                    dve.wait_ge(top_ready, q + 1)
                    wait(dve, mT_done, q - 1)
                    nc.vector.tensor_copy(mparts[b][:, :, 0, :], top[b][:]).then_inc(mpart0, 1)

                def invert(m, p):
                    dve.wait_ge(o_ready, 2 * (HP * m + p) + 2)
                    wait(dve, on_ready, HP * m + p - 1)
                    nc.vector.reciprocal(rec[p % 2][:], o[p % 2][:, 1, :]).then_inc(rec_ready, 1)

                def output(m):
                    dve.wait_ge(z_done, m + 1)
                    nc.vector.tensor_tensor(t["s"][:, bass.ds(2 * m, 2), :],
                                            ps_m[:, 0:2 * D].rearrange("p (r c) -> p r c", c=D),
                                            over(bo[:], 2, 1), ALU.add).then_inc(z_ready, 1)

                dve.wait_ge(w_in, W_ALL)
                for q in range(2):
                    for p in range(1, HP, 2):
                        project(q, q, p)
                    for n in range(4):
                        values(q, q, n)
                for h in range(H):
                    maximum(0, 0, h)
                tops(0, 0)

                def step(m, b, more):
                    for p in range(HP):
                        if more >= 1:
                            maximum(m + 1, 1 - b, 2 * p)
                            maximum(m + 1, 1 - b, 2 * p + 1)
                        if p:
                            invert(m, p - 1)
                        if more >= 2 and p % 2:
                            project(m + 2, b, p)
                    if more >= 1:
                        tops(m + 1, 1 - b)
                    invert(m, HP - 1)
                    if more >= 2:
                        values(m + 2, b, 0)
                    output(m)
                    if more >= 2:
                        for n in range(1, 4):
                            values(m + 2, b, n)

                pipelined(dve, N, step)

            @block.tensor
            def _(pe):
                def chunk_ready(q, p):
                    if p % 2 == 0:
                        pe.wait_ge(qk_act, HP * q + p + 2)
                    else:
                        pe.wait_ge(qk_dve, HP * q + p + 1)

                def project(q, b, p):
                    if p == 0:
                        pe.wait_ge(slab_in[b], 16 * ((q - b) // 2 + 1) if isinstance(q, int) else 8 * (q - b) + 16)
                        wait(pe, v_ready, 4 * q)
                    else:
                        chunk_ready(q, p - 1)
                    for z in range(2):
                        last = nc.tensor.matmul(ps_q[:, z * T:(z + 1) * T], w[:, z * QKV + p * P:z * QKV + (p + 1) * P],
                                                slab[b][:], start=True, stop=True)
                    last.then_inc(qk_done, 1)

                def values(q, b, n):
                    if n == 0:
                        chunk_ready(q, HP - 1)
                    else:
                        pe.wait_ge(v_ready, 4 * q + n)
                    r, half = n // 2, n % 2
                    nc.tensor.matmul(ps_q[:], slab[b][:, r * P:(r + 1) * P],
                                     w[:, 2 * QKV + half * 512:2 * QKV + (half + 1) * 512],
                                     start=True, stop=True).then_inc(v_done, 1)

                def by_queries(q, b, h):
                    chunk_ready(q, h // 2)
                    wait(pe, max_done, H * q + h - 1)
                    rows, out, p = slice(64 * (h % 2), 64 * (h % 2) + 64), ps_s[h % 2], h // 2
                    mask = lambda cols: nc.tensor.matmul(out[:, cols:cols + P], t["ident_b"][:], t["future_q"][:],
                                                         start=False, stop=True)
                    nc.tensor.matmul(out[:, 0:P], qT[b][rows, p, 0:P], kT[b][rows, p, 0:P], start=True, stop=False)
                    mask(0)
                    nc.tensor.matmul(out[:, P:3 * P], qT[b][rows, p, P:T], kT[b][rows, p, :], start=True, stop=False)
                    mask(2 * P).then_inc(s_done, 1)

                def by_keys(m, b, h):
                    if h == 0:
                        pe.wait_ge(max_in[b], 16 * ((m - b) // 2 + 1) if isinstance(m, int) else 8 * (m - b) + 16)
                    wait(pe, exp_done, H * m + h - 1)
                    rows, out, p = slice(64 * (h % 2), 64 * (h % 2) + 64), ps_t[h % 2], h // 2
                    for cols, keys, queries in ((slice(0, T), slice(0, P), slice(0, T)),
                                                (slice(T, 3 * P), slice(P, T), slice(P, T))):
                        nc.tensor.matmul(out[:, cols], kT[b][rows, p, keys], qT[b][rows, p, queries],
                                         start=True, stop=False)
                        nc.tensor.matmul(out[:, cols], minus[:], mrow[b][:, h, queries], start=False, stop=False)
                        last = nc.tensor.matmul(out[:, cols.start:cols.start + P], t["ident_b"][:], t["future_k"][:],
                                                start=False, stop=True)
                    last.then_inc(st_done, 1)

                def weigh(m, b, p):
                    pe.wait_ge(exp_done, H * m + 2 * p + 2)
                    if p == 0:
                        pe.wait_ge(v_ready, 4 * m + 4)
                    wait(pe, o_ready, 2 * (HP * m + p) - 2)
                    for z in range(2):
                        for keys in range(2):
                            for h in (2 * p, 2 * p + 1):
                                stat = t["ones"][:, 0:64] if z else v[b][:, keys, h * 64:(h + 1) * 64]
                                first = z * T + (P if keys else 0)
                                last = nc.tensor.matmul(
                                    ps_o[p % 2][64 * (h % 2):64 * (h % 2) + 64, first:(z + 1) * T], stat,
                                    prob[:, h % 4, 2 * P:3 * P] if keys else prob[:, h % 4, 0:T],
                                    start=(keys == 0), stop=(keys == 1))
                    last.then_inc(o_done, 1)

                def turn(q, b):
                    pe.wait_ge(mparts_ready, q + 1)
                    wait(pe, z_ready, q - 1)
                    for r in range(2):
                        last = nc.tensor.matmul(ps_m[0:3 * H, r * P:(r + 1) * P],
                                                mparts[b][:, r, :, :].rearrange("p a h -> p (a h)"),
                                                t["ident_b"][:], start=True, stop=True)
                    last.then_inc(mT_done, 1)

                def project_out(m, more):
                    pe.wait_ge(on_ready, HP * m + HP)
                    if more >= 1:
                        pe.wait_ge(mT_ready, m + 2)
                    for r in range(2):
                        for p in range(HP):
                            last = nc.tensor.matmul(ps_m[:, r * D:(r + 1) * D], on[:, p, r * P:(r + 1) * P],
                                                    wo[:, p, :], start=(p == 0), stop=(p == HP - 1))
                    last.then_inc(z_done, 1)

                pe.wait_ge(w_in, W_ALL)
                pe.wait_ge(ready, 2)
                for q in range(2):
                    for p in range(HP):
                        project(q, q, p)
                    for n in range(4):
                        values(q, q, n)
                for h in range(H):
                    by_queries(0, 0, h)
                turn(0, 0)

                def step(m, b, more):
                    for p in range(HP):
                        for h in (2 * p, 2 * p + 1):
                            by_keys(m, b, h)
                            if more >= 1:
                                by_queries(m + 1, 1 - b, h)
                        if p:
                            weigh(m, b, p - 1)
                        if more >= 2:
                            project(m + 2, b, p)
                    if more >= 1:
                        turn(m + 1, 1 - b)
                    weigh(m, b, HP - 1)
                    if more >= 2:
                        values(m + 2, b, 0)
                    project_out(m, more)
                    if more >= 2:
                        for n in range(1, 4):
                            values(m + 2, b, n)

                pipelined(pe, N, step)


def layer1_join(nc, t, d):
    with ExitStack() as ctx:
        def sb(name, shape, dt):
            return ctx.enter_context(nc.sbuf_tensor(name, shape, dt))

        def sem(name):
            return ctx.enter_context(semaphore(nc, t, "j1_" + name))

        s = t["s"]
        x, x1 = sb("x_again", [P, TILES, D], F32), sb("x1_again", [P, 2, CT, D], F32)
        y = [sb(f"y_best{a}", [P, TILES, D], F32) for a in range(2)]
        g2, b2 = sb("ln2_g", [P, D], F32), sb("ln2_b", [P, D], F32)
        norm = Norm(nc, sem, sb, "n3")
        w_in, x_in, x1_in = sem("w_in"), sem("x_in"), [sem("x1_in0"), sem("x1_in1")]
        got = [sem(f"got{c}") for c in range(CHUNKS)]
        inner, gated, done, out_done = sem("inner"), sem("gated"), sem("done"), sem("out_done")
        dve_step = sem("dve_step")

        def rows(name, c):
            return d[name].rearrange("(t p) d -> p t d", p=P)[:, c * CT:(c + 1) * CT, :]

        with nc.Block() as block:

            @block.sync
            def _(sp):
                for m, n in ((g2, "ln2_g"), (b2, "ln2_b")):
                    sp.dma_start(m[:], d[n].to_broadcast([P, D])).then_inc(w_in, 16)
                for c in range(CHUNKS):
                    sp.dma_start(x[:, c * CT:(c + 1) * CT, :], rows("x_rows", c)).then_inc(x_in, 16)
                for c in range(CHUNKS):
                    if c >= 2:
                        sp.wait_ge(inner, c - 1)
                    sp.dma_start(x1[:, c % 2, :, :], rows("x1_rows", c)).then_inc(x1_in[c % 2], 16)
                for c in range(CHUNKS):
                    sp.wait_ge(done, c + 1)
                    sp.dma_start(rows("out", c), x[:, c * CT:(c + 1) * CT, :]).then_inc(out_done, 16)
                sp.wait_ge(out_done, 16 * CHUNKS)

            @block.gpsimd
            def _(pool):
                for i in range(TILES):
                    for a in range(2):
                        n = a * TILES + i
                        pool.indirect_dma_start(y[a][:, i, :], None, d["outs1"],
                                                bass.IndirectOffsetOnAxis(t["slot1"][:, n:n + 1], 0))\
                            .then_inc(got[i // CT], 16)

            @block.scalar
            def _(act):
                for c in range(CHUNKS):
                    part = y[0][:, c * CT:(c + 1) * CT, :]
                    norm.scalar(act, c, part, t["eps"][:])
                    act.wait_ge(inner, c + 1)
                    nc.scalar.activation(part, part, ACT.Silu).then_inc(gated, 1)

            @block.vector
            def _(dve):
                link = Chain(dve, dve_step)
                dve.wait_ge(w_in, 32)
                dve.wait_ge(x_in, 16 * CHUNKS)
                for c in range(CHUNKS):
                    q = slice(c * CT, (c + 1) * CT)
                    dve.wait_ge(got[c], 32 * CT)
                    for a in range(2):
                        weight = t["weight1"][:, a * TILES + c * CT:a * TILES + (c + 1) * CT]
                        link(nc.vector.tensor_tensor(y[a][:, q, :], y[a][:, q, :], over(weight, D, 2), ALU.mult))
                    link(nc.vector.tensor_tensor(y[0][:, q, :], y[0][:, q, :], y[1][:, q, :], ALU.add))
                    norm.vector(link, c, y[0][:, q, :], y[0][:, q, :])
                    link(nc.vector.tensor_tensor(y[0][:, q, :], y[0][:, q, :], over(g2[:], CT, 1), ALU.mult))
                    link(nc.vector.tensor_tensor(y[0][:, q, :], y[0][:, q, :], over(b2[:], CT, 1), ALU.add))
                    dve.wait_ge(x1_in[c % 2], 16 * (c // 2 + 1))
                    nc.vector.tensor_tensor(y[0][:, q, :], y[0][:, q, :], x1[:, c % 2, :, :], ALU.add).then_inc(inner, 1)
                    dve.wait_ge(gated, c + 1)
                    link(nc.vector.tensor_tensor(y[0][:, q, :], y[0][:, q, :], s[:, q, :], ALU.mult))
                    nc.vector.tensor_tensor(x[:, q, :], x[:, q, :], y[0][:, q, :], ALU.add).then_inc(done, 1)


def shared(sb):
    return dict(
        semaphores=[], ident=sb("ident", [P, P], F32), ident_b=sb("ident_b", [P, P], BF16), ones=sb("ones", [P, P], F32),
        before=sb("before", [P, P], F32), zero_b=sb("zero_b", [P, P], BF16),
        future_q=sb("future_q", [P, P], BF16), future_k=sb("future_k", [P, P], BF16),
        rank8=sb("rank8", [P, EXPERTS], F32), tile_no=sb("tile_no", [1, expert_tiles(2 * TOKENS)], F32),
        eps=sb("eps", [P, 1], F32), zeros=sb("zeros", [P, 4 * D], F32),
        slot0=sb("slot0", [P, TILES], I32), expert0=sb("expert0", [1, expert_tiles(TOKENS)], I32),
        slot1=sb("slot1", [P, 2 * TILES], I32), expert1=sb("expert1", [1, expert_tiles(2 * TOKENS)], I32),
        weight1=sb("weight1", [P, 2 * TILES], F32), s=sb("s", [P, TILES, D], F32))


def program(nc, d):
    def dram(name, *shape):
        d[name] = nc.dram_tensor("scratch_" + name, shape, F32, kind="Internal").ap()

    dram("rows0", expert_tiles(TOKENS) * SLOTS, D)
    dram("outs0", expert_tiles(TOKENS) * SLOTS, D)
    dram("rows1", expert_tiles(2 * TOKENS) * SLOTS, D)
    dram("outs1", expert_tiles(2 * TOKENS) * SLOTS, D)
    dram("xnT", D, TOKENS)
    dram("x_rows", TOKENS, D)
    dram("x1_rows", TOKENS, D)
    with ExitStack() as ctx:
        def sb(name, shape, dt):
            return ctx.enter_context(nc.sbuf_tensor(name, shape, dt))

        t = shared(sb)
        constants(nc, t)
        with nc.sbuf_tensor("xn", [P, TILES, D], F32) as xn:
            t["xn"] = xn
            with nc.sbuf_tensor("x", [P, TILES, D], F32) as x:
                t["x"] = x
                layer0_front(nc, t, d)
                experts(nc, t, d, "0", expert_tiles(TOKENS), ACT.Relu, t["expert0"])
                layer0_join(nc, t, d)
                clear(nc, t)
            small_attention(nc, t, d)
            layer1_route(nc, t, d)
        causal_attention(nc, t, d)
        clear(nc, t)
        experts(nc, t, d, "1", expert_tiles(2 * TOKENS), ACT.Gelu, t["expert1"])
        layer1_join(nc, t, d)


def layout(i):
    import numpy as np

    def experts_pack(w1T, w2T, b1):
        e = w1T.shape[0]
        w2 = w2T.reshape(e, HC, P, D).transpose(0, 2, 1, 3).reshape(e, P, HC * D)
        return np.ascontiguousarray(np.concatenate([w1T, w2, b1.reshape(e, HC, P).transpose(0, 2, 1)], axis=2))

    def by_channel(a):
        return c(a.reshape(-1, HEADS_B, DH_B).transpose(0, 2, 1).reshape(a.shape[0], -1))

    c = np.ascontiguousarray
    return {
        "x": c(i["L0_attn_x"].reshape(TOKENS, D)),
        "A": c(i["L0_attn_A"]), "AT": c(i["L0_attn_A"].T), "BmT": c(i["L0_attn_Bm"].T),
        "CT": c(i["L0_attn_C"].T), "W_inT": c(i["L0_attn_W_in"].T), "b_in": c(i["L0_attn_b_in"].reshape(N_STATE, 1)),
        "D": c(i["L0_attn_D"].reshape(1, D)),
        "gate0T": c(i["L0_ffn_gate_w"].T), "gate0_b": c(i["L0_ffn_gate_b"].reshape(1, EXPERTS)),
        "w0": experts_pack(i["L0_ffn_w1"].transpose(0, 2, 1), i["L0_ffn_w2"].transpose(0, 2, 1), i["L0_ffn_b1"]),
        "b2_0": c(i["L0_ffn_b2"]),
        **{"f_" + n: by_channel(i["L1_ffn_" + n]) for n in ("Wq", "Wk")},
        **{"f_" + n: c(i["L1_ffn_" + n]) for n in ("Wv", "Wo")},
        "gate1": c(i["L1_ffn_gate_w"]), "gate1_b": c(i["L1_ffn_gate_b"].reshape(1, EXPERTS)),
        **{n: c(i["L1_ffn_" + n].reshape(1, D)) for n in ("ln1_g", "ln1_b", "ln2_g", "ln2_b")},
        "w1": experts_pack(i["L1_ffn_W1"], i["L1_ffn_W2"], i["L1_ffn_b1"]), "b2_1": c(i["L1_ffn_b2"]),
        "a_w": c(i["L1_attn_Wqkv_w"].T),
        "a_wo": c(i["L1_attn_Wo_w"].T.reshape(PAIRS_A, P, D).transpose(1, 0, 2)),
        "a_bq": c(i["L1_attn_Wqkv_b"][0:QKV].reshape(PAIRS_A, P).T),
        "a_bk": c(i["L1_attn_Wqkv_b"][QKV:2 * QKV].reshape(PAIRS_A, P).T),
        "a_bv": c(i["L1_attn_Wqkv_b"][2 * QKV:].reshape(1, QKV)), "a_bo": c(i["L1_attn_Wo_b"].reshape(1, D)),
        "ghost": c(i["L1_attn_ghost"].reshape(PAIRS_A, 2).T),
        **{"f_" + n: by_channel(i["L1_ffn_" + n].reshape(1, D)).reshape(D, 1) for n in ("bq", "bk")},
        "f_bv": c(i["L1_ffn_bv"].reshape(1, D)), "f_bo": c(i["L1_ffn_bo"].reshape(1, D)),
    }


def kernel(**inputs):
    import numpy as np
    import concourse.bacc as bacc
    from concourse.bass_utils import run_bass_kernel_spmd

    nc = bacc.Bacc("TRN2", target_bir_lowering=False, num_devices=1)
    arrays, d = {}, {}
    for name, a in layout(inputs).items():
        arrays["in_" + name] = a
        d[name] = nc.dram_tensor("in_" + name, a.shape, mybir.dt.from_np(a.dtype), kind="ExternalInput").ap()
    d["out"] = nc.dram_tensor("out_rows", (TOKENS, D), F32, kind="ExternalOutput").ap()
    program(nc, d)
    ran = run_bass_kernel_spmd(nc, [arrays], core_ids=[0])
    return ran.results[0]["out_rows"].reshape(BATCH, SEQ, D)
```

```python
from contextlib import ExitStack, contextmanager

import concourse.bass as bass
from concourse import mybir

ALU = mybir.AluOpType
ACT = mybir.ActivationFunctionType
F32 = mybir.dt.float32
BF16 = mybir.dt.bfloat16
I32 = mybir.dt.int32
AX_X = mybir.AxisListType.X

P = 128
BATCH, SEQ, D = 32, 256, 128
TOKENS = BATCH * SEQ
TILES = TOKENS // P
EXPERTS, HIDDEN = 8, 512
HC = HIDDEN // P
SLOTS = 256
EPS = 1e-5
CHUNKS = 4
CT = TILES // CHUNKS
N_STATE = 32
NEG = -1.0e30


NBUF = 4


def expert_tiles(assigned):
    n = assigned // SLOTS + EXPERTS - 1
    return -(-n // NBUF) * NBUF


class Chain:

    def __init__(self, eng, sem):
        self.eng, self.sem, self.n = eng, sem, 0

    def __call__(self, ins):
        self.n += 1
        ins.then_inc(self.sem, 1)
        self.eng.wait_ge(self.sem, self.n)


def over(ap, n, axis):
    a = ap.unsqueeze(axis)
    shape = list(a.shape)
    shape[axis] = n
    return a.to_broadcast(shape)


@contextmanager
def semaphore(nc, t, name):
    t["semaphores"].append(nc.alloc_semaphore(name=name))
    yield t["semaphores"][-1]


def clear(nc, t):
    nc.clear_and_free_semaphores(t["semaphores"])
    nc.all_engine_barrier()
    t["semaphores"] = []


def constants(nc, t):
    with semaphore(nc, t, "const_step") as step, nc.Block() as block:

        @block.gpsimd
        def _(pool):
            link = Chain(pool, step)
            link(nc.gpsimd.memset(t["ident"][:], 0.0))
            link(nc.gpsimd.affine_select(out=t["ident"][:], in_=t["ident"][:], compare_op=ALU.not_equal,
                                         fill=1.0, base=0, pattern=[[-1, P]], channel_multiplier=1))
            link(nc.gpsimd.tensor_copy(t["ident_b"][:], t["ident"][:]))
            link(nc.gpsimd.memset(t["ones"][:], 1.0))
            link(nc.gpsimd.affine_select(out=t["before"][:], in_=t["ones"][:], compare_op=ALU.is_gt,
                                         fill=0.0, base=0, pattern=[[1, P]], channel_multiplier=-1))
            link(nc.gpsimd.memset(t["zero_b"][:], 0.0))
            link(nc.gpsimd.affine_select(out=t["future_q"][:], in_=t["zero_b"][:], compare_op=ALU.is_ge,
                                         fill=NEG, base=0, pattern=[[-1, P]], channel_multiplier=1))
            link(nc.gpsimd.affine_select(out=t["future_k"][:], in_=t["zero_b"][:], compare_op=ALU.is_ge,
                                         fill=NEG, base=0, pattern=[[1, P]], channel_multiplier=-1))
            link(nc.gpsimd.iota(t["rank8"][:], pattern=[[-1, EXPERTS]], base=EXPERTS, channel_multiplier=0,
                                allow_small_or_imprecise_dtypes=True))
            n = t["tile_no"].shape[1]
            link(nc.gpsimd.iota(t["tile_no"][:], pattern=[[1, n]], base=0, channel_multiplier=0,
                                allow_small_or_imprecise_dtypes=True))
            link(nc.gpsimd.memset(t["eps"][:], EPS))
            link(nc.gpsimd.memset(t["zeros"][:], 0.0))


class Norm:

    def __init__(self, nc, sem, sb, name):
        self.nc = nc
        self.step = sem(name + "_dve_step")
        self.centred, self.squared = sem(name + "_centred"), sem(name + "_squared")
        self.summed, self.rooted = sem(name + "_summed"), sem(name + "_rooted")
        self.sq = sb(name + "_sq", [P, CT, D], F32)
        self.mean = sb(name + "_mean", [P, CT], F32)
        self.var = sb(name + "_var", [P, CT], F32)
        self.std = sb(name + "_std", [P, CT], F32)
        self.rstd = sb(name + "_rstd", [P, CT], F32)

    def vector(self, link, c, src, out):
        nc = self.nc
        link(nc.vector.tensor_reduce(self.mean[:], src, AX_X, ALU.add))
        link(nc.vector.tensor_scalar(self.mean[:], self.mean[:], 1.0 / D, None, ALU.mult))
        nc.vector.tensor_tensor(out, src, over(self.mean[:], D, 2), ALU.subtract).then_inc(self.centred, 1)
        link.eng.wait_ge(self.squared, c + 1)
        nc.vector.tensor_reduce(self.var[:], self.sq[:], AX_X, ALU.add).then_inc(self.summed, 1)
        link.eng.wait_ge(self.rooted, c + 1)
        link(nc.vector.reciprocal(self.rstd[:], self.std[:]))
        link(nc.vector.tensor_tensor(out, out, over(self.rstd[:], D, 2), ALU.mult))

    def scalar(self, act, c, out, eps):
        nc = self.nc
        act.wait_ge(self.centred, c + 1)
        if c:
            act.wait_ge(self.summed, c)
        nc.scalar.activation(self.sq[:], out, ACT.Square).then_inc(self.squared, 1)
        act.wait_ge(self.summed, c + 1)
        nc.scalar.activation(self.std[:], self.var[:], ACT.Sqrt, bias=eps, scale=1.0 / D).then_inc(self.rooted, 1)


def first_of(nc, link, out, values, best, work, rank8, tiles):
    link(nc.vector.tensor_reduce(best, values, AX_X, ALU.max))
    link(nc.vector.tensor_tensor(work, values, over(best, EXPERTS, 2), ALU.is_ge))
    link(nc.vector.tensor_tensor(work, work, over(rank8, tiles, 1), ALU.mult))
    link(nc.vector.tensor_reduce(best, work, AX_X, ALU.max))
    link(nc.vector.tensor_tensor(out, work, over(best, EXPERTS, 2), ALU.is_ge))


def route(nc, dve, link, t, r, n_assign, n_tiles, counted, ready):
    n = n_assign * TILES
    dve.wait_ge(counted, 1)
    flat = lambda x: x[:].rearrange("p t e -> p (t e)")
    ps = lambda x: x[:, 0:n_assign, :].rearrange("p b n -> p (b n)")
    link(nc.vector.tensor_copy(flat(r["total"]), ps(r["ps_total"])))
    for e in range(EXPERTS):
        link(nc.vector.tensor_tensor_scan(r["upto"][:, :, e], t["ones"][:, 0:n] if n <= P else t["ones"][:],
                                          r["total"][:, :, e], 0.0, ALU.mult, ALU.add))
    link(nc.vector.tensor_copy(r["count"][:], r["upto"][:, n - 1, :]))
    link(nc.vector.tensor_tensor(flat(r["upto"]), flat(r["upto"]), flat(r["total"]), ALU.subtract))
    link(nc.vector.tensor_tensor(flat(r["upto"]), flat(r["upto"]), ps(r["ps_rank"]), ALU.add))
    link(nc.vector.tensor_scalar(r["count_i"][:], r["count"][:], float(SLOTS - 1), None, ALU.add))
    link(nc.vector.tensor_single_scalar(r["count_i"][:], r["count_i"][:], SLOTS.bit_length() - 1,
                                        ALU.arith_shift_right))
    link(nc.vector.tensor_copy(r["count"][:], r["count_i"][:]))
    link(nc.vector.tensor_tensor_scan(r["last"][:], t["ones"][:, 0:EXPERTS], r["count"][:], 0.0,
                                      ALU.mult, ALU.add))
    link(nc.vector.tensor_tensor(r["base"][:], r["last"][:], r["count"][:], ALU.subtract))
    link(nc.vector.tensor_scalar(r["base"][:], r["base"][:], float(SLOTS), None, ALU.mult))
    link(nc.vector.tensor_tensor(r["upto"][:], r["upto"][:], over(r["base"][:], n, 1), ALU.add))
    link(nc.vector.tensor_tensor(flat(r["upto"]), flat(r["upto"]), flat(r["chosen"]), ALU.mult))
    link(nc.vector.tensor_reduce(r["slot_f"][:], r["upto"][:], AX_X, ALU.add))
    link(nc.vector.tensor_copy(r["slot"][:], r["slot_f"][:]))
    link(nc.vector.tensor_tensor(r["ended"][:], over(t["tile_no"][0:1, 0:n_tiles], EXPERTS, 2),
                                 over(r["last"][0:1, :], n_tiles, 1), ALU.is_ge))
    link(nc.vector.tensor_reduce(r["expert_f"][:], r["ended"][:], AX_X, ALU.add))
    nc.vector.tensor_scalar(r["expert"][:], r["expert_f"][:], float(EXPERTS - 1), None,
                            ALU.min).then_inc(ready, 1)


def route_counts(nc, pe, t, r, n_assign, counted):
    flat = r["chosen"][:].rearrange("p t e -> p (t e)")
    for a in range(n_assign):
        part = flat[:, a * 512:(a + 1) * 512]
        nc.tensor.matmul(r["ps_rank"][:, a, :], t["before"][:], part, start=True, stop=True)
        last = nc.tensor.matmul(r["ps_total"][:, a, :], t["ones"][:], part, start=True, stop=True)
    last.then_inc(counted, 1)


def route_buffers(sb, pb, n_assign, n_tiles, keep, tag):
    n = n_assign * TILES
    return dict(
        keep,
        chosen=sb("chosen" + tag, [P, n, EXPERTS], F32), total=sb("total" + tag, [P, n, EXPERTS], F32),
        upto=sb("upto" + tag, [P, n, EXPERTS], F32), count=sb("count" + tag, [P, EXPERTS], F32),
        count_i=sb("count_i" + tag, [P, EXPERTS], I32), last=sb("last" + tag, [P, EXPERTS], F32),
        base=sb("base" + tag, [P, EXPERTS], F32), slot_f=sb("slot_f" + tag, [P, n], F32),
        ended=sb("ended" + tag, [1, n_tiles, EXPERTS], F32), expert_f=sb("expert_f" + tag, [1, n_tiles], F32),
        ps_rank=pb("ps_rank" + tag, [P, n_assign, 512], F32), ps_total=pb("ps_total" + tag, [P, n_assign, 512], F32))


def layer0_front(nc, t, d):
    with ExitStack() as ctx:
        def sb(name, shape, dt):
            return ctx.enter_context(nc.sbuf_tensor(name, shape, dt))

        def pb(name, shape, dt):
            return ctx.enter_context(nc.psum_tensor(name, shape, dt))

        def sem(name):
            return ctx.enter_context(semaphore(nc, t, name))

        x, xn, s = t["x"], t["xn"], t["s"]
        xnT = sb("xnT", [P, TOKENS], F32)
        win = sb("win", [P, N_STATE], F32)
        bd = sb("bd", [P, 2, P], F32)
        bdT = sb("bdT", [P, P], F32)
        pw = sb("pw", [P, 8, P], F32)
        pwT = sb("pwT", [P, 8, P], F32)
        cpad = sb("cpad", [P, 4, P], F32)
        b_in = sb("b_in", [P, 1], F32)
        d_bc = sb("d_bc", [P, D], F32)
        gw = sb("gw", [P, P], F32)
        gb = sb("gb", [P, EXPERTS], F32)
        u = sb("u", [P, 2048], F32)
        h = sb("h", [P, 8, SEQ], F32)
        logits = sb("logits", [P, TILES, EXPERTS], F32)
        best = sb("best", [P, TILES], F32)
        norm = Norm(nc, sem, sb, "n0")
        ps = pb("ps", [P, 6, 512], F32)
        n_tiles = expert_tiles(TOKENS)
        r = route_buffers(sb, pb, 1, n_tiles, dict(slot=t["slot0"], expert=t["expert0"]), "0")

        x_in = [sem(f"x_in{c}") for c in range(CHUNKS)]
        w_in, w_zero = sem("w_in"), sem("w_zero")
        zeroed, scattered = sem("zeroed"), sem("scattered")
        xn_ready, tr_done, xnT_ready = sem("xn_ready"), sem("tr_done"), sem("xnT_ready")
        u_done, u_ready, ub_done, h0_ready = sem("u_done"), sem("u_ready"), sem("ub_done"), sem("h0_ready")
        sq_done, pw_ready = sem("sq_done"), sem("pw_ready")
        step_done, h_ready = sem("step_done"), sem("h_ready")
        s_done, s_ready = sem("s_done"), sem("s_ready")
        g_done, g_ready = sem("g_done"), sem("g_ready")
        chosen_ready, counted, routed = sem("chosen_ready"), sem("counted"), sem("routed")
        dve_step = sem("dve_step")
        GROUPS = TILES // 4

        with nc.Block() as block:

            @block.sync
            def _(sp):
                for c in range(CHUNKS):
                    sp.dma_start(x[:, c * CT:(c + 1) * CT, :],
                                 d["x"].rearrange("(t p) d -> p t d", p=P)[:, c * CT:(c + 1) * CT, :])\
                      .then_inc(x_in[c], 16)
                sp.wait_ge(w_zero, 5)
                for g in range(4):
                    q = slice(32 * g, 32 * g + 32)
                    sp.dma_start(bd[q, 0, q], d["BmT"]).then_inc(w_in, 16)
                    sp.dma_start(bd[q, 1, q], d["A"]).then_inc(w_in, 16)
                    sp.dma_start(bdT[q, q], d["AT"]).then_inc(w_in, 16)
                    sp.dma_start(cpad[q, g, :], d["CT"]).then_inc(w_in, 16)
                    sp.dma_start(b_in[q, :], d["b_in"]).then_inc(w_in, 16)
                sp.dma_start(win[:], d["W_inT"]).then_inc(w_in, 16)
                sp.dma_start(gw[:, 0:EXPERTS], d["gate0T"]).then_inc(w_in, 16)
                sp.dma_start(gb[:], d["gate0_b"].to_broadcast([P, EXPERTS])).then_inc(w_in, 16)
                sp.dma_start(d_bc[:], d["D"].to_broadcast([P, D])).then_inc(w_in, 16)
                n = 0
                for name, tiles in (("rows0", n_tiles), ("rows1", expert_tiles(2 * TOKENS))):
                    out = d[name].rearrange("(q p) d -> p q d", p=P)
                    for q in range(0, 2 * tiles, 4):
                        sp.dma_start(out[:, q:q + 4, :],
                                     t["zeros"][:].rearrange("p (q d) -> p q d", d=D)).then_inc(zeroed, 16)
                        n += 16
                t["n_zeroed"] = n
                sp.wait_ge(zeroed, n)

            W_ALL = 16 * 24

            @block.gpsimd
            def _(pool):
                for m in (bd, bdT, cpad, gw):
                    nc.gpsimd.memset(m[:], 0.0).then_inc(w_zero, 1)
                nc.gpsimd.memset(norm.mean[:], 0.0).then_inc(w_zero, 1)
                pool.wait_ge(routed, 1)
                pool.wait_ge(zeroed, t["n_zeroed"])
                for i in range(TILES):
                    pool.indirect_dma_start(d["rows0"], bass.IndirectOffsetOnAxis(t["slot0"][:, i:i + 1], 0),
                                            xn[:, i, :], None).then_inc(scattered, 16)
                pool.wait_ge(scattered, 16 * TILES)

            @block.scalar
            def _(act):
                for c in range(CHUNKS):
                    norm.scalar(act, c, xn[:, c * CT:(c + 1) * CT, :], t["eps"][:])
                    for g in range(4 * c, 4 * c + 4):
                        act.wait_ge(tr_done, g + 1)
                        nc.scalar.activation(xnT[:, g * 512:(g + 1) * 512], ps[:, g % 2, :],
                                             ACT.Copy).then_inc(xnT_ready, 1)
                act.wait_ge(w_in, W_ALL)
                for c in range(4):
                    act.wait_ge(u_done, c + 1)
                    nc.scalar.activation(u[:, c * 512:(c + 1) * 512], ps[:, 2 + c % 2, :], ACT.Identity,
                                         bias=b_in[:, 0:1]).then_inc(u_ready, 1)
                hf = h[:].rearrange("p b t -> p (b t)")
                for c in range(4):
                    act.wait_ge(ub_done, c + 1)
                    nc.scalar.activation(hf[:, c * 512:(c + 1) * 512], ps[:, 4 + c % 2, :],
                                         ACT.Copy).then_inc(h0_ready, 1)
                for k in range(7):
                    act.wait_ge(sq_done, k + 1)
                    nc.scalar.activation(pw[:, k + 1, :], ps[:, k % 2, 0:P], ACT.Copy).then_inc(pw_ready, 1)
                    nc.scalar.activation(pwT[:, k + 1, :], ps[:, k % 2, P:2 * P], ACT.Copy).then_inc(pw_ready, 1)

            @block.tensor
            def _(pe):
                for g in range(GROUPS):
                    pe.wait_ge(xn_ready, g // 4 + 1)
                    if g >= 2:
                        pe.wait_ge(xnT_ready, g - 1)
                    for i in range(4):
                        last = nc.tensor.transpose(ps[:, g % 2, i * P:(i + 1) * P], xn[:, 4 * g + i, :], t["ident"][:])
                    last.then_inc(tr_done, 1)
                pe.wait_ge(xnT_ready, GROUPS)
                pe.wait_ge(w_in, W_ALL)
                for c in range(4):
                    if c >= 2:
                        pe.wait_ge(u_ready, c - 1)
                    for g in range(4):
                        last = nc.tensor.matmul(ps[32 * g:32 * g + 32, 2 + c % 2, :], win[:],
                                                xnT[:, g * 2048 + c * 512:g * 2048 + (c + 1) * 512],
                                                start=True, stop=True)
                    last.then_inc(u_done, 1)
                for c in range(4):
                    pe.wait_ge(u_ready, c + 1)
                    if c >= 2:
                        pe.wait_ge(h0_ready, c - 1)
                    nc.tensor.matmul(ps[:, 4 + c % 2, :], bd[:, 0, :], u[:, c * 512:(c + 1) * 512],
                                     start=True, stop=True).then_inc(ub_done, 1)
                for k in range(7):
                    if k:
                        pe.wait_ge(pw_ready, 2 * k)
                    a, aT = (pw[:, k, :], pwT[:, k, :]) if k else (bd[:, 1, :], bdT[:])
                    nc.tensor.matmul(ps[:, k % 2, 0:P], aT, a, start=True, stop=True)
                    nc.tensor.matmul(ps[:, k % 2, P:2 * P], a, aT, start=True, stop=True).then_inc(sq_done, 1)
                pe.wait_ge(h0_ready, 4)
                pe.wait_ge(pw_ready, 14)
                for k in range(8):
                    for c in range(4):
                        n = 4 * k + c
                        if k:
                            pe.wait_ge(h_ready, n - 3)
                        if n >= 2:
                            pe.wait_ge(h_ready, n - 1)
                        nc.tensor.matmul(ps[:, 2 + c % 2, :], pw[:, k, :] if k else bd[:, 1, :],
                                         h[:, 2 * c:2 * c + 2, :], start=True, stop=True).then_inc(step_done, 1)
                pe.wait_ge(h_ready, 32)
                for q in range(GROUPS):
                    if q >= 2:
                        pe.wait_ge(s_ready, q - 1)
                    for i in range(4):
                        n = 4 * q + i
                        b, half = n // 2, n % 2
                        last = nc.tensor.matmul(ps[:, 4 + q % 2, i * P:(i + 1) * P],
                                                h[:, b % 8, half * P:(half + 1) * P], cpad[:, b // 8, :],
                                                start=True, stop=True)
                    last.then_inc(s_done, 1)
                for q in range(GROUPS):
                    if q >= 2:
                        pe.wait_ge(g_ready, q - 1)
                    for i in range(4):
                        n = 4 * q + i
                        last = nc.tensor.matmul(ps[:, q % 2, i * P:(i + 1) * P], xnT[:, n * P:(n + 1) * P], gw[:],
                                                start=True, stop=True)
                    last.then_inc(g_done, 1)
                pe.wait_ge(chosen_ready, 1)
                route_counts(nc, pe, t, r, 1, counted)

            @block.vector
            def _(dve):
                link = Chain(dve, dve_step)
                dve.wait_ge(w_zero, 5)
                for c in range(CHUNKS):
                    q = slice(c * CT, (c + 1) * CT)
                    dve.wait_ge(x_in[c], 16)
                    norm.vector(link, c, x[:, q, :], xn[:, q, :])
                    nc.vector.tensor_copy(best[:, 0:1], t["eps"][:]).then_inc(xn_ready, 1)
                dve.wait_ge(w_in, W_ALL)
                for k in range(8):
                    d_ = 1 << k
                    for c in range(4):
                        n = 4 * k + c
                        dve.wait_ge(step_done, n + 1)
                        if k:
                            dve.wait_ge(h_ready, n - 3)
                        part = h[:, 2 * c:2 * c + 2, d_:SEQ]
                        psv = ps[:, 2 + c % 2, :].rearrange("p (b t) -> p b t", t=SEQ)[:, :, 0:SEQ - d_]
                        nc.vector.tensor_tensor(part, psv, part, ALU.add).then_inc(h_ready, 1)
                for q in range(GROUPS):
                    dve.wait_ge(s_done, q + 1)
                    nc.vector.tensor_tensor(s[:, 4 * q:4 * q + 4, :],
                                            ps[:, 4 + q % 2, :].rearrange("p (i d) -> p i d", d=D),
                                            over(d_bc[:], 4, 1), ALU.add).then_inc(s_ready, 1)
                for q in range(GROUPS):
                    dve.wait_ge(g_done, q + 1)
                    nc.vector.tensor_tensor(logits[:, 4 * q:4 * q + 4, :],
                                            ps[:, q % 2, :].rearrange("p (i d) -> p i d", d=P)[:, :, 0:EXPERTS],
                                            over(gb[:], 4, 1), ALU.add).then_inc(g_ready, 1)
                dve.wait_ge(g_ready, GROUPS)
                dve.wait_ge(xn_ready, CHUNKS)
                first_of(nc, link, r["chosen"][:], logits[:], best[:], r["total"][:], t["rank8"][:], TILES)
                nc.vector.tensor_copy(norm.mean[:, 0:1], t["eps"][:]).then_inc(chosen_ready, 1)
                route(nc, dve, link, t, r, 1, n_tiles, counted, routed)


def wait(eng, sem, value):
    if not isinstance(value, int) or value > 0:
        eng.wait_ge(sem, value)


def loaded(eng, sems, n, j, each=16):
    eng.wait_ge(sems[j], each * (n // NBUF + 1) if isinstance(n, int) else each // NBUF * (n - j) + each)


def experts(nc, t, d, tag, n_tiles, act_fn, expert):
    with ExitStack() as ctx:
        def sb(name, shape, dt):
            return ctx.enter_context(nc.sbuf_tensor(name + tag, shape, dt))

        def pb(name, shape, dt):
            return ctx.enter_context(nc.psum_tensor(name + tag, shape, dt))

        def sem(name):
            return ctx.enter_context(semaphore(nc, t, name + tag))

        def many(n, make, name, *more):
            return [make(f"{name}{b}_", *more) for b in range(n)]

        rows, outs = d["rows" + tag], d["outs" + tag]
        B1, B2 = 2 * HIDDEN, 2 * HIDDEN + HC
        w = many(NBUF, sb, "w", [P, B2 + D], F32)
        xr = many(NBUF, sb, "xr", [P, 2, D], F32)
        y = many(NBUF, sb, "y", [P, 2, D], F32)
        xT = many(2, sb, "xT", [P, SLOTS], F32)
        hid = many(2, sb, "hid", [P, HC, SLOTS], F32)
        ps_x, ps_h, ps_y = (many(2, pb, n, s, F32) for n, s in (("ps_x", [P, 512]), ("ps_h", [P, 2, 512]),
                                                                ("ps_y", [P, 512])))
        w_in, x_in, stored = many(NBUF, sem, "w_in"), many(NBUF, sem, "x_in"), many(NBUF, sem, "stored")
        tr_done, xT_ready, up_a, up_b = sem("tr_done"), sem("xT_ready"), sem("up_a"), sem("up_b")
        hid_a, hid_b, down, y_ready = sem("hid_a"), sem("hid_b"), sem("down"), sem("y_ready")
        relu = act_fn == ACT.Relu
        groups = n_tiles // NBUF

        def exists(n):
            return not isinstance(n, int) or 0 <= n < n_tiles

        def loop(eng, step):
            for j in range(NBUF):
                step(j, j)
            with eng.Fori(1, groups - 1) as i:
                for j in range(NBUF):
                    step(NBUF * i + j, j)
            for j in range(NBUF):
                step(n_tiles - NBUF + j, j)

        with nc.Block() as block:

            @block.sync
            def _(sp):
                def load(n, j):
                    if not exists(n):
                        return
                    wait(sp, tr_done, n - NBUF + 1)
                    sp.dma_start(xr[j][:], rows.rearrange("(n r p) d -> n p r d", p=P, r=2)[bass.ds(n, 1)]
                                 .rearrange("o p r d -> p (o r) d")).then_inc(x_in[j], 16)
                    e = sp.value_load(expert[0:1, bass.ds(n, 1)], min_val=0, max_val=EXPERTS - 1)
                    wait(sp, y_ready, n - NBUF + 1)
                    sp.dma_start(w[j][:], d["w" + tag][bass.ds(e, 1)].rearrange("o p n -> p (o n)"))\
                      .then_inc(w_in[j], 16)

                for n in range(NBUF):
                    load(n, n)
                for j in range(NBUF):
                    load(NBUF + j, j)
                with sp.Fori(1, groups - 1) as i:
                    for j in range(NBUF):
                        load(NBUF * i + NBUF + j, j)

            @block.gpsimd
            def _(pool):
                def store(n, j):
                    pool.wait_ge(y_ready, n + 1)
                    pool.dma_start(outs.rearrange("(n r p) d -> n p r d", p=P, r=2)[bass.ds(n, 1)]
                                   .rearrange("o p r d -> p (o r) d"), y[j][:]).then_inc(stored[j], 16)

                loop(pool, store)
                for j in range(NBUF):
                    pool.wait_ge(stored[j], 16 * groups)

            @block.scalar
            def _(act):
                def hidden(n, j):
                    wait(act, down, n - 1)
                    loaded(act, w_in, n, j)
                    for c in range(2 if relu else HC):
                        if c == 0:
                            act.wait_ge(up_a, n + 1)
                        if c == 2:
                            act.wait_ge(up_b, n + 1)
                        ins = nc.scalar.activation(hid[j % 2][:, c, :],
                                                   ps_h[j % 2][:, c // 2, (c % 2) * SLOTS:(c % 2 + 1) * SLOTS],
                                                   act_fn, bias=w[j][:, B1 + c:B1 + c + 1])
                        if c == 1:
                            ins.then_inc(hid_a, 1)
                        if c == 3:
                            ins.then_inc(hid_b, 1)

                loop(act, hidden)

            @block.vector
            def _(dve):
                def turned(n, j):
                    dve.wait_ge(tr_done, n + 1)
                    wait(dve, up_b, n - 1)
                    nc.vector.tensor_copy(xT[j % 2][:], ps_x[j % 2][:, 0:SLOTS]).then_inc(xT_ready, 1)

                def hidden(n, j):
                    wait(dve, down, n - 1)
                    loaded(dve, w_in, n, j)
                    dve.wait_ge(up_b, n + 1)
                    for c in (2, 3):
                        ins = nc.vector.tensor_scalar(
                            hid[j % 2][:, c, :], ps_h[j % 2][:, 1, (c - 2) * SLOTS:(c - 1) * SLOTS],
                            w[j][:, B1 + c:B1 + c + 1], 0.0, ALU.add, ALU.max)
                    ins.then_inc(hid_b, 1)

                def output(n, j):
                    dve.wait_ge(down, n + 1)
                    before = n - NBUF
                    if not isinstance(n, int) or before >= 0:
                        loaded(dve, stored, before, j)
                    loaded(dve, w_in, n, j)
                    nc.vector.tensor_tensor(y[j][:], ps_y[j % 2][:, 0:2 * D].rearrange("p (r d) -> p r d", d=D),
                                            over(w[j][:, B2:B2 + D], 2, 1), ALU.add).then_inc(y_ready, 1)

                def step(n, j):
                    if exists(n + 2):
                        turned(n + 2, (j + 2) % NBUF)
                    if relu and exists(n + 1):
                        hidden(n + 1, (j + 1) % NBUF)
                    output(n, j)

                turned(0, 0)
                turned(1, 1)
                if relu:
                    hidden(0, 0)
                loop(dve, step)

            @block.tensor
            def _(pe):
                def turn(n, j):
                    loaded(pe, x_in, n, j)
                    wait(pe, xT_ready, n - 1)
                    for r in range(2):
                        last = nc.tensor.transpose(ps_x[j % 2][:, r * P:(r + 1) * P], xr[j][:, r, :], t["ident"][:])
                    last.then_inc(tr_done, 1)

                def up(n, j):
                    pe.wait_ge(xT_ready, n + 1)
                    loaded(pe, w_in, n, j)
                    for c in range(HC):
                        if c == 0:
                            wait(pe, hid_a, n - 1)
                        if c == 2:
                            wait(pe, hid_b, n - 1)
                        last = nc.tensor.matmul(ps_h[j % 2][:, c // 2, (c % 2) * SLOTS:(c % 2 + 1) * SLOTS],
                                                w[j][:, c * P:(c + 1) * P], xT[j % 2][:], start=True, stop=True)
                        if c == 1:
                            last.then_inc(up_a, 1)
                    last.then_inc(up_b, 1)

                def down_(n, j):
                    pe.wait_ge(hid_a, n + 1)
                    pe.wait_ge(hid_b, n + 1)
                    wait(pe, y_ready, n - 1)
                    for r in range(2):
                        for c in range(HC):
                            last = nc.tensor.matmul(ps_y[j % 2][:, r * D:(r + 1) * D], hid[j % 2][:, c, r * P:(r + 1) * P],
                                                    w[j][:, HIDDEN + c * D:HIDDEN + (c + 1) * D],
                                                    start=(c == 0), stop=(c == HC - 1))
                    last.then_inc(down, 1)

                def step(n, j):
                    if exists(n + 2):
                        turn(n + 2, (j + 2) % NBUF)
                    if exists(n + 1):
                        up(n + 1, (j + 1) % NBUF)
                    down_(n, j)

                turn(0, 0)
                turn(1, 1)
                up(0, 0)
                loop(pe, step)


def layer0_join(nc, t, d):
    with ExitStack() as ctx:
        def sb(name, shape, dt):
            return ctx.enter_context(nc.sbuf_tensor(name, shape, dt))

        def pb(name, shape, dt):
            return ctx.enter_context(nc.psum_tensor(name, shape, dt))

        def sem(name):
            return ctx.enter_context(semaphore(nc, t, name))

        x, xn, s = t["x"], t["xn"], t["s"]
        g = sb("g_rows", [P, TILES, D], F32)
        xnT = sb("xnT_b", [P, 4, 512], F32)
        norm = Norm(nc, sem, sb, "n1")
        ps = pb("ps_t", [P, 4, 512], F32)
        got = [sem(f"got{c}") for c in range(CHUNKS)]
        gated, xn_ready = sem("gated"), sem("xn1_ready")
        tr_done, xnT_ready, xnT_out = sem("tr1_done"), sem("xnT1_ready"), [sem(f"xnT_out{i}") for i in range(4)]
        dve_step, x_out = sem("dve1_step"), sem("x_out")
        GROUPS = TILES // 4

        with nc.Block() as block:

            @block.gpsimd
            def _(pool):
                for i in range(TILES):
                    pool.indirect_dma_start(g[:, i, :], None, d["outs0"],
                                            bass.IndirectOffsetOnAxis(t["slot0"][:, i:i + 1], 0))\
                        .then_inc(got[i // CT], 16)

            @block.scalar
            def _(act):
                def silu(c):
                    act.wait_ge(got[c], 16 * CT)
                    nc.scalar.activation(g[:, c * CT:(c + 1) * CT, :], g[:, c * CT:(c + 1) * CT, :],
                                         ACT.Silu).then_inc(gated, 1)

                silu(0)
                for c in range(CHUNKS):
                    if c + 1 < CHUNKS:
                        silu(c + 1)
                    norm.scalar(act, c, xn[:, c * CT:(c + 1) * CT, :], t["eps"][:])
                    for q in range(4 * c, 4 * c + 4):
                        act.wait_ge(tr_done, q + 1)
                        if q >= 4:
                            act.wait_ge(xnT_out[q % 4], 16 * (q // 4))
                        nc.scalar.activation(xnT[:, q % 4, :], ps[:, q % 4, :], ACT.Copy).then_inc(xnT_ready, 1)

            @block.tensor
            def _(pe):
                for q in range(GROUPS):
                    pe.wait_ge(xn_ready, q // 4 + 1)
                    if q >= 4:
                        pe.wait_ge(xnT_ready, q - 3)
                    for i in range(4):
                        last = nc.tensor.transpose(ps[:, q % 4, i * P:(i + 1) * P], xn[:, 4 * q + i, :], t["ident"][:])
                    last.then_inc(tr_done, 1)

            @block.sync
            def _(sp):
                for q in range(GROUPS):
                    sp.wait_ge(xnT_ready, q + 1)
                    sp.dma_start(d["xnT"][:, q * 512:(q + 1) * 512], xnT[:, q % 4, :]).then_inc(xnT_out[q % 4], 16)
                    if q % 4 == 3:
                        sp.dma_start(d["x_rows"].rearrange("(t p) d -> p t d", p=P)[:, 4 * q - 12:4 * q + 4, :],
                                     x[:, 4 * q - 12:4 * q + 4, :]).then_inc(x_out, 16)
                for i in range(4):
                    sp.wait_ge(xnT_out[i], 16 * GROUPS // 4)
                sp.wait_ge(x_out, 16 * CHUNKS)

            @block.vector
            def _(dve):
                link = Chain(dve, dve_step)
                for c in range(CHUNKS):
                    q = slice(c * CT, (c + 1) * CT)
                    dve.wait_ge(gated, c + 1)
                    link(nc.vector.tensor_tensor(g[:, q, :], g[:, q, :], s[:, q, :], ALU.mult))
                    link(nc.vector.tensor_tensor(x[:, q, :], x[:, q, :], g[:, q, :], ALU.add))
                    norm.vector(link, c, x[:, q, :], xn[:, q, :])
                    nc.vector.tensor_copy(norm.mean[:, 0:1], t["eps"][:]).then_inc(xn_ready, 1)


HEADS_B, DH_B = 16, 8
PAIRS = ((0, 0), (0, 1), (1, 0), (1, 1), (0, 2), (2, 0))
M_ROW = 64
STACK = M_ROW + 3


def pipelined(eng, count, step):
    step(0, 0, 2)
    step(1, 1, 2)
    with eng.Fori(1, count // 2 - 1) as i:
        step(2 * i, 0, 2)
        step(2 * i + 1, 1, 2)
    step(count - 2, 0, 1)
    step(count - 1, 1, 0)


def by_fours(eng, count, step, last=4):
    for m in range(4):
        step(m, m)
    with eng.Fori(1, (count - last) // 4) as i:
        for j in range(4):
            step(4 * i + j, j)
    for m in range(count - last, count):
        step(m, m % 4)


def small_attention(nc, t, d):
    with ExitStack() as ctx:
        def sb(name, shape, dt):
            return ctx.enter_context(nc.sbuf_tensor("f_" + name, shape, dt))

        def pb(name, shape, dt):
            return ctx.enter_context(nc.psum_tensor("f_" + name, shape, dt))

        def sem(name):
            return ctx.enter_context(semaphore(nc, t, "f_" + name))

        def many(n, make, name, *more):
            return [make(f"{name}{b}", *more) for b in range(n)]

        H, T, N = HEADS_B, SEQ, BATCH
        wq, wk, wv, wo = (sb(n, [P, D], F32) for n in ("wq", "wk", "wv", "wo"))
        bq, bk = sb("bq", [P, 1], F32), sb("bk", [P, 1], F32)
        bv, bo = sb("bv", [P, D], F32), sb("bo", [P, D], F32)
        slab = many(4, sb, "slab", [P, T], F32)
        qk = many(2, sb, "qk", [P, 2, T], F32)
        rest = sb("rest", [P, 2, T], F32)
        parts = many(2, sb, "parts", [P, 3, 2, T], BF16)
        qs, ks = many(4, sb, "qs", [STACK, H, T], BF16), many(4, sb, "ks", [STACK, H, T], BF16)
        v = many(2, sb, "v", [P, 2, H, 32], F32)
        nmax = many(2, sb, "nmax", [P, 2, H], F32)
        mrest = sb("mrest", [P, 2, H], F32)
        mparts = many(2, sb, "mparts", [P, 2, 3, H], BF16)
        mT = many(4, sb, "mT", [3 * H, T], BF16)
        prob = many(2, sb, "prob", [P, 4, 2 * T], F32)
        o = many(2, sb, "o", [P, 4, T], F32)
        rec = sb("rec", [P, 2, H], F32)
        on = sb("on", [P, 2, D], F32)
        onT = sb("onT", [P, T], F32)
        ps_s, ps_t = (many(2, pb, n, [P, 2 * T], F32) for n in ("ps_s", "ps_t"))
        ps_o, ps_r, ps_q, ps_m = (pb(n, [P, 512], F32) for n in ("ps_o", "ps_r", "ps_q", "ps_m"))

        w_in, filled, bq_scaled = sem("w_in"), sem("filled"), sem("bq_scaled")
        slab_in, stack_in, max_in = (many(4, sem, n) for n in ("slab_in", "stack_in", "max_in"))
        qk_done, qk_ready, v_done, v_ready = sem("qk_done"), sem("qk_ready"), sem("v_done"), sem("v_ready")
        part0, rest1, part1, parts_ready = sem("part0"), sem("rest1"), sem("part1"), sem("parts_ready")
        mpart0, mrest1, mpart1, mparts_ready = sem("mpart0"), sem("mrest1"), sem("mpart1"), sem("mparts_ready")
        s_done, max_done, mT_done, mT_ready = sem("s_done"), sem("max_done"), sem("mT_done"), sem("mT_ready")
        st_done, exp_done, o_done, o_ready = sem("st_done"), sem("exp_done"), sem("o_done"), sem("o_ready")
        oT_done, rec_done, on_ready = sem("oT_done"), sem("rec_done"), sem("on_ready")
        back_done, onT_ready, z_done, z_ready = sem("back_done"), sem("onT_ready"), sem("z_done"), sem("z_ready")
        STACKED = 16 * 2 * len(PAIRS)
        W_ALL, FILLS = 16 * 8, 4 * 3 + 2 * 2

        def exists(m):
            return not isinstance(m, int) or 0 <= m < N

        def stages(m, j):
            return lambda k: (m + k, (j + k) % 4)

        with nc.Block() as block:

            @block.sync
            def _(sp):
                def load(q, j):
                    wait(sp, v_done, q - 3)
                    sp.dma_start(slab[j][:], d["xnT"][:, bass.ds(q * T, T)]).then_inc(slab_in[j], 16)

                def stack(q, j):
                    sp.wait_ge(parts_ready, q + 1)
                    for s_, pair in enumerate(PAIRS):
                        for z, (dst, part) in enumerate(zip((qs[j], ks[j]), pair)):
                            sp.dma_start(dst[8 * s_:8 * s_ + 8, :, :], parts[j % 2][:, part, z, :])\
                              .then_inc(stack_in[j], 16)

                def maxima(q, j):
                    sp.wait_ge(mT_ready, q + 1)
                    sp.dma_start(qs[j][M_ROW:STACK, :, :], mT[j][:]).then_inc(max_in[j], 16)

                for w, n in ((wq, "Wq"), (wk, "Wk"), (wv, "Wv"), (bq, "bq"), (bk, "bk"), (wo, "Wo")):
                    sp.dma_start(w[:], d["f_" + n]).then_inc(w_in, 16)
                for w, n in ((bv, "bv"), (bo, "bo")):
                    sp.dma_start(w[:], d["f_" + n].to_broadcast([P, D])).then_inc(w_in, 16)
                for q in range(4):
                    load(q, q)
                sp.wait_ge(filled, FILLS)
                for q in range(4):
                    stack(q, q)
                maxima(0, 0)
                load(4, 0)

                def step(m, j):
                    if exists(m + 1):
                        maxima(m + 1, (j + 1) % 4)
                    if exists(m + 5):
                        load(m + 5, (j + 1) % 4)
                    elif exists(m + 4):
                        sp.wait_ge(v_done, m + 2)
                    if exists(m + 4):
                        stack(m + 4, j)

                by_fours(sp, N, step, 8)

            @block.gpsimd
            def _(pool):
                for m in ks:
                    nc.gpsimd.memset(m[M_ROW:STACK, :, :], 1.0).then_inc(filled, 1)
                for m in ks:
                    nc.gpsimd.memset(m[32:M_ROW, :, :], 0.0).then_inc(filled, 1)

                def split(q, j):
                    whole, part = qk[j % 2], parts[j % 2]
                    pool.wait_ge(part0, q + 1)
                    wait(pool, parts_ready, q)
                    nc.gpsimd.tensor_tensor(rest[:], whole[:], part[:, 0, :, :], ALU.subtract).then_inc(rest1, 1)
                    nc.gpsimd.tensor_tensor(part[:, 1, :, :], whole[:], part[:, 0, :, :], ALU.subtract)\
                        .then_inc(part1, 1)
                    pool.wait_ge(rest1, q + 1)
                    pool.wait_ge(part1, q + 1)
                    nc.gpsimd.tensor_tensor(part[:, 2, :, :], rest[:], part[:, 1, :, :], ALU.subtract)\
                        .then_inc(parts_ready, 1)

                def split_max(q, j):
                    whole, part = nmax[j % 2], mparts[j % 2]
                    pool.wait_ge(mpart0, q + 1)
                    wait(pool, mparts_ready, q)
                    nc.gpsimd.tensor_tensor(mrest[:], whole[:], part[:, :, 0, :], ALU.subtract).then_inc(mrest1, 1)
                    nc.gpsimd.tensor_tensor(part[:, :, 1, :], whole[:], part[:, :, 0, :], ALU.subtract)\
                        .then_inc(mpart1, 1)
                    pool.wait_ge(mrest1, q + 1)
                    pool.wait_ge(mpart1, q + 1)
                    nc.gpsimd.tensor_tensor(part[:, :, 2, :], mrest[:], part[:, :, 1, :], ALU.subtract)\
                        .then_inc(mparts_ready, 1)

                for q in range(4):
                    split(q, q)
                split_max(0, 0)

                def step(m, j):
                    if exists(m + 1):
                        split_max(m + 1, (j + 1) % 4)
                    if exists(m + 4):
                        split(m + 4, j)

                by_fours(pool, N, step)

            @block.scalar
            def _(act):
                def project(q, j):
                    act.wait_ge(qk_done, q + 1)
                    wait(act, parts_ready, q - 1)
                    nc.scalar.activation(qk[j % 2][:, 0, :], ps_q[:, 0:T], ACT.Identity, bias=bq[:, 0:1],
                                         scale=DH_B ** -0.5)
                    nc.scalar.activation(qk[j % 2][:, 1, :], ps_q[:, T:2 * T], ACT.Identity,
                                         bias=bk[:, 0:1]).then_inc(qk_ready, 1)

                def exps(m, g):
                    for k in range(4):
                        h = 4 * g + k
                        act.wait_ge(st_done, H * m + h + 1)
                        if k == 0:
                            wait(act, o_done, 4 * m + g - 1)
                        nc.scalar.activation(prob[g % 2][:, k, :], ps_t[h % 2][:], ACT.Exp).then_inc(exp_done, 1)

                def take(m, j, half):
                    act.wait_ge(o_done, 4 * m + 2 * half + 2)
                    wait(act, oT_done, 2 * (m - 1))
                    nc.scalar.activation(o[j % 2][:, 2 * half:2 * half + 2, :].rearrange("p g t -> p (g t)"), ps_o[:],
                                         ACT.Copy).then_inc(o_ready, 1)

                def turned(q, j):
                    act.wait_ge(mT_done, q + 1)
                    if exists(q - 4):
                        loaded(act, max_in, q - 4, j)
                    nc.scalar.activation(mT[j][:], ps_m[0:3 * H, 0:T], ACT.Copy).then_inc(mT_ready, 1)

                def back(m):
                    act.wait_ge(back_done, m + 1)
                    wait(act, z_done, m)
                    nc.scalar.activation(onT[:], ps_m[:, 0:T], ACT.Copy).then_inc(onT_ready, 1)

                act.wait_ge(w_in, W_ALL)
                nc.scalar.activation(bq[:], bq[:], ACT.Copy, scale=DH_B ** -0.5).then_inc(bq_scaled, 1)
                act.wait_ge(bq_scaled, 1)
                for q in range(4):
                    project(q, q)
                turned(0, 0)

                def step(m, j):
                    exps(m, 0)
                    if exists(m - 1):
                        take(m - 1, j + 1, 1)
                    exps(m, 1)
                    if exists(m + 1):
                        turned(m + 1, (j + 1) % 4)
                    exps(m, 2)
                    take(m, j, 0)
                    if exists(m + 4):
                        project(m + 4, j)
                    if exists(m - 1):
                        back(m - 1)
                    exps(m, 3)

                by_fours(act, N, step)
                take(N - 1, 1, 1)
                back(N - 1)

            @block.vector
            def _(dve):
                def values(q, j):
                    dve.wait_ge(v_done, q + 1)
                    wait(dve, o_done, 4 * (q - 1))
                    for r in range(2):
                        last = nc.vector.tensor_tensor(v[j % 2][:, r, :, 0:8],
                                                       ps_q[:, r * D:(r + 1) * D].rearrange("p (h c) -> p h c", c=8),
                                                       bv[:].rearrange("p (h c) -> p h c", c=8), ALU.add)
                    last.then_inc(v_ready, 1)

                def first_part(q, j):
                    dve.wait_ge(qk_ready, q + 1)
                    if exists(q - 2):
                        loaded(dve, stack_in, q - 2, (j + 2) % 4, STACKED)
                    nc.vector.tensor_copy(parts[j % 2][:, 0, :, :], qk[j % 2][:]).then_inc(part0, 1)

                def first_max_part(q, j):
                    dve.wait_ge(max_done, H * (q + 1))
                    wait(dve, mT_done, q - 1)
                    nc.vector.tensor_copy(mparts[j % 2][:, :, 0, :], nmax[j % 2][:]).then_inc(mpart0, 1)

                def maxima(q, j, g):
                    for h in range(4 * g, 4 * g + 4):
                        dve.wait_ge(s_done, H * q + h + 1)
                        if h == 0:
                            wait(dve, mparts_ready, q - 1)
                        nc.vector.tensor_reduce(nmax[j % 2][:, :, h], ps_s[h % 2][:].rearrange("p (r k) -> p r k", r=2),
                                                AX_X, ALU.max, negate=True).then_inc(max_done, 1)

                def divide(m, r):
                    rows = ps_r[:].rearrange("p (h c) -> p h c", c=32)
                    dve.wait_ge(oT_done, 2 * m + r + 1)
                    wait(dve, on_ready, 2 * m + r - 1)
                    nc.vector.reciprocal(rec[:, r, :], rows[:, :, 8]).then_inc(rec_done, 1)
                    dve.wait_ge(rec_done, 2 * m + r + 1)
                    wait(dve, back_done, m)
                    nc.vector.tensor_tensor(on[:, r, :].rearrange("p (h c) -> p h c", c=8), rows[:, :, 0:8],
                                            over(rec[:, r, :], 8, 2), ALU.mult).then_inc(on_ready, 1)

                def output(m):
                    dve.wait_ge(z_done, m + 1)
                    nc.vector.tensor_tensor(t["s"][:, bass.ds(2 * m, 2), :],
                                            ps_m[:, 0:2 * D].rearrange("p (r c) -> p r c", c=D),
                                            over(bo[:], 2, 1), ALU.add).then_inc(z_ready, 1)

                for m in qs:
                    nc.vector.memset(m[32:M_ROW, :, :], 0.0).then_inc(filled, 1)
                for m in v:
                    nc.vector.memset(m[:], 0.0).then_inc(filled, 1)
                dve.wait_ge(filled, FILLS - 2)
                for m in v:
                    nc.vector.memset(m[:, :, :, 8:9], 1.0).then_inc(filled, 1)
                dve.wait_ge(filled, FILLS)
                dve.wait_ge(w_in, W_ALL)
                for q in range(4):
                    first_part(q, q)
                values(0, 0)
                for q in range(2):
                    for g in range(4):
                        maxima(q, q, g)
                    if q == 0:
                        first_max_part(0, 0)

                def step(m, j):
                    near = stages(m, j)
                    for g in range(4):
                        if exists(m + 2):
                            maxima(*near(2), g)
                        if g == 0 and exists(m + 1):
                            first_max_part(*near(1))
                        if g in (1, 2) and exists(m - 1):
                            divide(m - 1, g - 1)
                        if g == 2 and exists(m + 4):
                            first_part(*near(4))
                    if exists(m + 1):
                        values(*near(1))
                    if exists(m - 1):
                        output(m - 1)

                by_fours(dve, N, step)
                for r in range(2):
                    divide(N - 1, r)
                output(N - 1)

            @block.tensor
            def _(pe):
                def project(q, j):
                    loaded(pe, slab_in, q, j)
                    nc.tensor.matmul(ps_q[:, 0:T], wq[:], slab[j][:], start=True, stop=True)
                    nc.tensor.matmul(ps_q[:, T:2 * T], wk[:], slab[j][:], start=True, stop=True).then_inc(qk_done, 1)

                def values(q, j):
                    for r in range(2):
                        last = nc.tensor.matmul(ps_q[:, r * D:(r + 1) * D], slab[j][:, r * P:(r + 1) * P], wv[:],
                                                start=True, stop=True)
                    last.then_inc(v_done, 1)

                def by_queries(q, j, h):
                    if h == 0:
                        loaded(pe, stack_in, q, j, STACKED)
                    wait(pe, max_done, H * q + h - 1)
                    for r in range(2):
                        last = nc.tensor.matmul(ps_s[h % 2][:, r * T:(r + 1) * T], qs[j][0:M_ROW, h, r * P:(r + 1) * P],
                                                ks[j][0:M_ROW, h, :], start=True, stop=True)
                    last.then_inc(s_done, 1)

                def by_keys(m, j, h):
                    if h == 0:
                        loaded(pe, max_in, m, j)
                    wait(pe, exp_done, H * m + h - 1)
                    for r in range(2):
                        last = nc.tensor.matmul(ps_t[h % 2][:, r * T:(r + 1) * T], ks[j][:, h, r * P:(r + 1) * P],
                                                qs[j][:, h, :], start=True, stop=True)
                    last.then_inc(st_done, 1)

                def weigh(m, j, g):
                    pe.wait_ge(exp_done, H * m + 4 * g + 4)
                    if g == 0:
                        pe.wait_ge(v_ready, m + 1)
                    if g % 2 == 0:
                        wait(pe, o_ready, 2 * m + g // 2)
                    first = (g % 2) * T
                    for r in range(2):
                        for k in range(4):
                            last = nc.tensor.matmul(ps_o[32 * k:32 * k + 32, first:first + T],
                                                    v[j % 2][:, r, 4 * g + k, :],
                                                    prob[g % 2][:, k, r * T:(r + 1) * T], start=(r == 0), stop=(r == 1))
                    last.then_inc(o_done, 1)

                def turn_o(m, j, r):
                    pe.wait_ge(o_ready, 2 * m + 2)
                    wait(pe, on_ready, 2 * m + r)
                    for g in range(4):
                        last = nc.tensor.transpose(ps_r[:, g * P:(g + 1) * P], o[j % 2][:, g, r * P:(r + 1) * P],
                                                   t["ident"][:])
                    last.then_inc(oT_done, 1)

                def turn_max(q, j):
                    pe.wait_ge(mparts_ready, q + 1)
                    wait(pe, z_ready, q - 2)
                    for r in range(2):
                        last = nc.tensor.matmul(ps_m[0:3 * H, r * P:(r + 1) * P],
                                                mparts[j % 2][:, r, :, :].rearrange("p a h -> p (a h)"),
                                                t["ident_b"][:], start=True, stop=True)
                    last.then_inc(mT_done, 1)

                def turn_back(m):
                    pe.wait_ge(on_ready, 2 * m + 2)
                    if exists(m + 2):
                        pe.wait_ge(mT_ready, m + 3)
                    else:
                        pe.wait_ge(z_ready, m)
                    for r in range(2):
                        last = nc.tensor.transpose(ps_m[:, r * P:(r + 1) * P], on[:, r, :], t["ident"][:])
                    last.then_inc(back_done, 1)

                def project_out(m):
                    pe.wait_ge(onT_ready, m + 1)
                    for r in range(2):
                        last = nc.tensor.matmul(ps_m[:, r * D:(r + 1) * D], onT[:, r * P:(r + 1) * P], wo[:],
                                                start=True, stop=True)
                    last.then_inc(z_done, 1)

                pe.wait_ge(w_in, W_ALL)
                pe.wait_ge(filled, FILLS)
                for q in range(4):
                    wait(pe, qk_ready, q)
                    project(q, q)
                pe.wait_ge(qk_ready, 4)
                values(0, 0)
                for q in range(2):
                    for h in range(H):
                        by_queries(q, q, h)
                    if q == 0:
                        turn_max(0, 0)

                def step(m, j):
                    near = stages(m, j)
                    for g in range(4):
                        for h in range(4 * g, 4 * g + 4):
                            by_keys(m, j, h)
                            if exists(m + 2):
                                by_queries(*near(2), h)
                        if g == 0 and exists(m - 1):
                            weigh(*near(-1), 3)
                        if g > 0:
                            weigh(m, j, g - 1)
                        if g in (1, 2) and exists(m - 1):
                            turn_o(*near(-1), g - 1)
                        if g == 1 and exists(m + 1):
                            turn_max(*near(1))
                        if g == 2 and exists(m + 4):
                            pe.wait_ge(v_ready, m + 1)
                            project(*near(4))
                        if g == 3:
                            if exists(m - 1):
                                project_out(m - 1)
                            if exists(m + 1):
                                if exists(m + 4):
                                    pe.wait_ge(qk_ready, m + 5)
                                else:
                                    pe.wait_ge(v_ready, m + 1)
                                values(*near(1))
                        if g == 2 and exists(m - 1):
                            turn_back(m - 1)

                by_fours(pe, N, step)
                weigh(N - 1, 3, 3)
                for r in range(2):
                    turn_o(N - 1, 3, r)
                turn_back(N - 1)
                project_out(N - 1)


def layer1_route(nc, t, d):
    with ExitStack() as ctx:
        def sb(name, shape, dt):
            return ctx.enter_context(nc.sbuf_tensor(name, shape, dt))

        def pb(name, shape, dt):
            return ctx.enter_context(nc.psum_tensor(name, shape, dt))

        def sem(name):
            return ctx.enter_context(semaphore(nc, t, "r1_" + name))

        xn, s = t["xn"], t["s"]
        g1, b1 = sb("ln1_g", [P, D], F32), sb("ln1_b", [P, D], F32)
        gw, gb = sb("gw1", [P, P], F32), sb("gb1", [P, EXPERTS], F32)
        xT = sb("x1T", [P, 2, 512], F32)
        prob = sb("prob1", [P, TILES, EXPERTS], F32)
        best, total = sb("best1", [P, TILES], F32), sb("total1s", [P, TILES], F32)
        norm = Norm(nc, sem, sb, "n2")
        ps = pb("ps_x1", [P, 2, 512], F32)
        n_tiles = expert_tiles(2 * TOKENS)
        r = route_buffers(sb, pb, 2, n_tiles, dict(slot=t["slot1"], expert=t["expert1"]), "1")
        ps_g = pb("ps_g1", [P, 2, 512], F32)

        w_in, w_zero, x1_ready, x1_out = sem("w_in"), sem("w_zero"), sem("x1_ready"), sem("x1_out")
        tr_done, xT_ready, g_done, g_ready = sem("tr_done"), sem("xT_ready"), sem("g_done"), sem("g_ready")
        shifted, exp_ready = sem("shifted"), sem("exp_ready")
        chosen_ready, counted, routed, scattered = sem("chosen"), sem("counted"), sem("routed"), sem("scattered")
        dve_step = sem("dve_step")
        GROUPS = TILES // 4

        with nc.Block() as block:

            @block.sync
            def _(sp):
                sp.wait_ge(w_zero, 1)
                sp.dma_start(gw[:, 0:EXPERTS], d["gate1"]).then_inc(w_in, 16)
                for m, n in ((gb, "gate1_b"), (g1, "ln1_g"), (b1, "ln1_b")):
                    sp.dma_start(m[:], d[n].to_broadcast([P, m.shape[1]])).then_inc(w_in, 16)
                for c in range(CHUNKS):
                    sp.wait_ge(x1_ready, c + 1)
                    sp.dma_start(d["x1_rows"].rearrange("(t p) d -> p t d", p=P)[:, c * CT:(c + 1) * CT, :],
                                 xn[:, c * CT:(c + 1) * CT, :]).then_inc(x1_out, 16)
                sp.wait_ge(x1_out, 16 * CHUNKS)

            @block.gpsimd
            def _(pool):
                nc.gpsimd.memset(gw[:], 0.0).then_inc(w_zero, 1)
                pool.wait_ge(routed, 1)
                for i in range(2 * TILES):
                    pool.indirect_dma_start(d["rows1"], bass.IndirectOffsetOnAxis(t["slot1"][:, i:i + 1], 0),
                                            xn[:, i % TILES, :], None).then_inc(scattered, 16)
                pool.wait_ge(scattered, 16 * 2 * TILES)

            @block.scalar
            def _(act):
                for c in range(CHUNKS):
                    norm.scalar(act, c, s[:, c * CT:(c + 1) * CT, :], t["eps"][:])
                    for q in range(4 * c, 4 * c + 4):
                        act.wait_ge(tr_done, q + 1)
                        if q >= 2:
                            act.wait_ge(g_done, q - 1)
                        nc.scalar.activation(xT[:, q % 2, :], ps[:, q % 2, :], ACT.Copy).then_inc(xT_ready, 1)
                act.wait_ge(shifted, 1)
                nc.scalar.activation(prob[:], prob[:], ACT.Exp).then_inc(exp_ready, 1)

            @block.tensor
            def _(pe):
                pe.wait_ge(w_in, 64)
                pe.wait_ge(w_zero, 1)

                def gate(q):
                    pe.wait_ge(xT_ready, q + 1)
                    if q >= 2:
                        pe.wait_ge(g_ready, q - 1)
                    for i in range(4):
                        last = nc.tensor.matmul(ps_g[:, q % 2, i * P:(i + 1) * P], xT[:, q % 2, i * P:(i + 1) * P],
                                                gw[:], start=True, stop=True)
                    last.then_inc(g_done, 1)

                for q in range(GROUPS):
                    pe.wait_ge(x1_ready, q // 4 + 1)
                    if q >= 2:
                        pe.wait_ge(xT_ready, q - 1)
                    for i in range(4):
                        last = nc.tensor.transpose(ps[:, q % 2, i * P:(i + 1) * P], xn[:, 4 * q + i, :], t["ident"][:])
                    last.then_inc(tr_done, 1)
                    if q:
                        gate(q - 1)
                gate(GROUPS - 1)
                pe.wait_ge(chosen_ready, 1)
                route_counts(nc, pe, t, r, 2, counted)

            @block.vector
            def _(dve):
                link = Chain(dve, dve_step)
                dve.wait_ge(w_in, 64)

                def logits(q):
                    dve.wait_ge(g_done, q + 1)
                    nc.vector.tensor_tensor(prob[:, 4 * q:4 * q + 4, :],
                                            ps_g[:, q % 2, :].rearrange("p (i d) -> p i d", d=P)[:, :, 0:EXPERTS],
                                            over(gb[:], 4, 1), ALU.add).then_inc(g_ready, 1)

                for c in range(CHUNKS):
                    q = slice(c * CT, (c + 1) * CT)
                    norm.vector(link, c, s[:, q, :], s[:, q, :])
                    link(nc.vector.tensor_tensor(s[:, q, :], s[:, q, :], over(g1[:], CT, 1), ALU.mult))
                    link(nc.vector.tensor_tensor(s[:, q, :], s[:, q, :], over(b1[:], CT, 1), ALU.add))
                    nc.vector.tensor_tensor(xn[:, q, :], xn[:, q, :], s[:, q, :], ALU.add).then_inc(x1_ready, 1)
                    if c:
                        for g in range(4 * c - 4, 4 * c):
                            logits(g)
                for g in range(GROUPS - 4, GROUPS):
                    logits(g)
                dve.wait_ge(g_ready, GROUPS)
                link(nc.vector.tensor_reduce(best[:], prob[:], AX_X, ALU.max))
                nc.vector.tensor_tensor(prob[:], prob[:], over(best[:], EXPERTS, 2), ALU.subtract).then_inc(shifted, 1)
                dve.wait_ge(exp_ready, 1)
                link(nc.vector.tensor_reduce(total[:], prob[:], AX_X, ALU.add))
                link(nc.vector.reciprocal(total[:], total[:]))
                link(nc.vector.tensor_tensor(prob[:], prob[:], over(total[:], EXPERTS, 2), ALU.mult))
                first, second = r["chosen"][:, 0:TILES, :], r["chosen"][:, TILES:2 * TILES, :]
                work = r["total"][:, 0:TILES, :]
                first_of(nc, link, first, prob[:], best[:], work, t["rank8"][:], TILES)
                link(nc.vector.tensor_tensor(work, prob[:], first, ALU.mult))
                link(nc.vector.tensor_reduce(t["weight1"][:, 0:TILES], work, AX_X, ALU.add))
                rest = r["total"][:, TILES:2 * TILES, :]
                link(nc.vector.scalar_tensor_tensor(rest, first, -2.0, prob[:], ALU.mult, ALU.add))
                first_of(nc, link, second, rest, best[:], work, t["rank8"][:], TILES)
                link(nc.vector.tensor_tensor(work, prob[:], second, ALU.mult))
                link(nc.vector.tensor_reduce(t["weight1"][:, TILES:2 * TILES], work, AX_X, ALU.add))
                nc.vector.tensor_copy(best[:, 0:1], t["eps"][:]).then_inc(chosen_ready, 1)
                route(nc, dve, link, t, r, 2, n_tiles, counted, routed)


HEADS_A, DH_A = 16, 64
PAIRS_A = HEADS_A // 2
QKV = HEADS_A * DH_A


def causal_attention(nc, t, d):
    with ExitStack() as ctx:
        def sb(name, shape, dt):
            return ctx.enter_context(nc.sbuf_tensor("a_" + name, shape, dt))

        def pb(name, shape, dt):
            return ctx.enter_context(nc.psum_tensor("a_" + name, shape, dt))

        def sem(name):
            return ctx.enter_context(semaphore(nc, t, "a_" + name))

        def many(n, make, name, *more):
            return [make(f"{name}{b}", *more) for b in range(n)]

        T, N, HP = SEQ, BATCH, PAIRS_A
        SC = DH_A ** -0.5
        w = sb("w", [P, 3 * QKV], F32)
        wo = sb("wo", [P, HP, D], F32)
        bq, bq_s, bk = sb("bq", [P, HP], F32), sb("bq_s", [P, HP], F32), sb("bk", [P, HP], F32)
        bv, bo = sb("bv", [P, QKV], F32), sb("bo", [P, D], F32)
        ghost = sb("ghost", [P, HEADS_A], F32)
        slab = many(2, sb, "slab", [P, T], F32)
        qT, kT = many(2, sb, "qT", [P, T], F32), many(2, sb, "kT", [P, T], F32)
        v = sb("v", [P, 2, QKV], F32)
        nmax, sums = many(2, sb, "nmax", [P, 2, 2], F32), many(2, sb, "sums", [P, 2, 2], F32)
        total, rec = sb("total", [P, 2, 2], F32), many(2, sb, "rec", [P, 2, 2], F32)
        prob, probT = many(4, sb, "prob", [P, 2, 3 * P], F32), many(2, sb, "probT", [P, 2, 3 * P], F32)
        o = many(2, sb, "o", [P, HP, T], F32)
        ps_s = many(2, pb, "ps_s", [P, 2, 512], F32)
        ps_q, ps_t, ps_o = pb("ps_q", [P, 512], F32), pb("ps_t", [P, 2, 512], F32), pb("ps_o", [P, 512], F32)

        w_in, scaled_bias, slab_in = sem("w_in"), sem("scaled_bias"), many(2, sem, "slab_in")
        qk_done, qk_ready = sem("qk_done"), sem("qk_ready")
        v_done, v_ready = sem("v_done"), sem("v_ready")
        s_done, max_ready, exp_ready = sem("s_done"), sem("max_ready"), sem("exp_ready")
        totalled, rec_ready, divided = sem("totalled"), sem("rec_ready"), sem("divided")
        t_done, probT_ready, o_done, o_ready = sem("t_done"), sem("probT_ready"), sem("o_done"), sem("o_ready")
        z_done, z_ready = sem("z_done"), sem("z_ready")
        W_ALL = 16 * 7
        TURN, WEIGH, OUT = 2, 3, 4

        def exists(m):
            return not isinstance(m, int) or 0 <= m < N

        def ago(m, b, p, k):
            return (m, b, p - k) if p >= k else (m - 1, 1 - b, p - k + HP)

        def loop(eng, pair):
            def step(m, b, more):
                for p in range(HP):
                    pair(m, b, p)

            pipelined(eng, N, step)
            for p in range(OUT + 1):
                pair(N, 0, p)

        def chunk_at(m, b, p):
            if p in (2, 3):
                return m, b, p
            if p in (6, 7):
                return m + 1, 1 - b, p - 6
            return -1, 0, 0

        with nc.Block() as block:

            @block.sync
            def _(sp):
                def load(q, b):
                    wait(sp, qk_done, HP * (q - 1))
                    sp.dma_start(slab[b][:], d["xnT"][:, bass.ds(q * T, T)]).then_inc(slab_in[b], 16)

                load(0, 0)
                sp.dma_start(w[:], d["a_w"]).then_inc(w_in, 16)
                for m, n in ((bq, "a_bq"), (bk, "a_bk"), (wo, "a_wo")):
                    sp.dma_start(m[:], d[n]).then_inc(w_in, 16)
                for m, n in ((bv, "a_bv"), (bo, "a_bo"), (ghost, "ghost")):
                    sp.dma_start(m[:], d[n].to_broadcast([P, m.shape[1]])).then_inc(w_in, 16)
                load(1, 1)

                def step(m, b, more):
                    if more >= 2:
                        load(m + 2, b)

                pipelined(sp, N, step)

            @block.gpsimd
            def _(pool):
                def divide(m, b, p):
                    pool.wait_ge(rec_ready, HP * m + p + 1)
                    for q in range(2):
                        cols = prob[p % 4][:, :, q * P:(2 * q + 1) * P]
                        last = nc.gpsimd.tensor_tensor(cols, cols, over(rec[p % 2][:, q, :], (q + 1) * P, 2), ALU.mult)
                    last.then_inc(divided, 1)

                loop(pool, lambda m, b, p: divide(m, b, p) if exists(m) else None)

            @block.scalar
            def _(act):
                def queries_keys(m, b, p):
                    act.wait_ge(qk_done, HP * m + p + 1)
                    wait(act, s_done, HP * m + p - 1)
                    nc.scalar.activation(qT[p % 2][:], ps_q[:, 0:T], ACT.Identity, bias=bq_s[:, p:p + 1], scale=SC)
                    nc.scalar.activation(kT[p % 2][:], ps_q[:, T:2 * T], ACT.Identity, bias=bk[:, p:p + 1])\
                      .then_inc(qk_ready, 1)

                def exps(m, b, p):
                    act.wait_ge(max_ready, HP * m + p + 1)
                    wait(act, t_done, HP * m + p - 3)
                    wait(act, totalled, HP * m + p - 1)
                    for h in range(2):
                        for q in range(2):
                            cols = slice(q * P, (2 * q + 1) * P)
                            last = nc.scalar.activation(prob[p % 4][:, h, cols], ps_s[p % 2][:, h, cols], ACT.Exp,
                                                        bias=nmax[p % 2][:, q, h:h + 1],
                                                        accum_out=sums[p % 2][:, q, h:h + 1])
                    last.then_inc(exp_ready, 1)

                def take(m, b, p):
                    act.wait_ge(o_done, HP * m + p + 1)
                    wait(act, z_done, m - 1)
                    nc.scalar.activation(o[b][:, p, :], ps_o[:, 0:T], ACT.Copy).then_inc(o_ready, 1)

                act.wait_ge(w_in, W_ALL)
                nc.scalar.activation(bq_s[:], bq[:], ACT.Copy, scale=SC).then_inc(scaled_bias, 1)
                act.wait_ge(scaled_bias, 1)
                queries_keys(0, 0, 0)

                def pair(m, b, p):
                    after, old = (m, b, p + 1) if p + 1 < HP else (m + 1, 1 - b, 0), ago(m, b, p, WEIGH)
                    if exists(after[0]):
                        queries_keys(*after)
                    if exists(m):
                        exps(m, b, p)
                    if exists(old[0]):
                        take(*old)

                loop(act, pair)

            @block.vector
            def _(dve):
                def values(m, b, n):
                    dve.wait_ge(v_done, 4 * m + n + 1)
                    wait(dve, o_done, HP * (m - 1) + 4 * (n // 2 + 1))
                    half, r = n // 2, n % 2
                    cols = slice(half * 512, (half + 1) * 512)
                    nc.vector.tensor_tensor(v[:, r, cols], ps_q[:], bv[:, cols], ALU.add).then_inc(v_ready, 1)

                def maxima(m, b, p):
                    dve.wait_ge(s_done, HP * m + p + 1)
                    wait(dve, exp_ready, HP * m + p - 1)
                    for q in range(2):
                        last = nc.vector.tensor_reduce(nmax[p % 2][:, q, :], ps_s[p % 2][:, :, q * P:(2 * q + 1) * P],
                                                       AX_X, ALU.max, negate=True)
                    last.then_inc(max_ready, 1)

                def invert(m, b, p):
                    dve.wait_ge(exp_ready, HP * m + p + 1)
                    wait(dve, rec_ready, HP * m + p)
                    nc.vector.tensor_tensor(total[:], sums[p % 2][:], over(ghost[:, 2 * p:2 * p + 2], 2, 1),
                                            ALU.add).then_inc(totalled, 1)
                    dve.wait_ge(totalled, HP * m + p + 1)
                    wait(dve, divided, HP * m + p - 1)
                    nc.vector.reciprocal(rec[p % 2][:], total[:]).then_inc(rec_ready, 1)

                def turned(m, b, p):
                    dve.wait_ge(t_done, HP * m + p + 1)
                    wait(dve, o_done, HP * m + p - 1)
                    nc.vector.tensor_copy(probT[p % 2][:], ps_t[:, :, 0:3 * P]).then_inc(probT_ready, 1)

                def output(m):
                    dve.wait_ge(z_done, m + 1)
                    nc.vector.tensor_tensor(t["s"][:, bass.ds(2 * m, 2), :],
                                            ps_q[:, 0:2 * D].rearrange("p (r c) -> p r c", c=D),
                                            over(bo[:], 2, 1), ALU.add).then_inc(z_ready, 1)

                dve.wait_ge(w_in, W_ALL)
                for n in range(2):
                    values(0, 0, n)

                def pair(m, b, p):
                    old = ago(m, b, p, TURN)
                    if exists(m):
                        maxima(m, b, p)
                    if exists(old[0]):
                        turned(*old)
                    if exists(m):
                        invert(m, b, p)
                    chunk = chunk_at(m, b, p)
                    if exists(chunk[0]):
                        values(*chunk)
                    if p == OUT and exists(m - 1):
                        output(m - 1)

                loop(dve, pair)

            @block.tensor
            def _(pe):
                def slab_wait(m, b):
                    pe.wait_ge(slab_in[b], 16 * ((m - b) // 2 + 1) if isinstance(m, int) else 8 * (m - b) + 16)

                def project(m, b, p):
                    for z in range(2):
                        last = nc.tensor.matmul(ps_q[:, z * T:(z + 1) * T], w[:, z * QKV + p * P:z * QKV + (p + 1) * P],
                                                slab[b][:], start=True, stop=True)
                    last.then_inc(qk_done, 1)

                def values(m, b, n):
                    half, r = n // 2, n % 2
                    nc.tensor.matmul(ps_q[:], slab[b][:, r * P:(r + 1) * P],
                                     w[:, 2 * QKV + half * 512:2 * QKV + (half + 1) * 512],
                                     start=True, stop=True).then_inc(v_done, 1)

                def scores(m, b, p):
                    pe.wait_ge(qk_ready, HP * m + p + 1)
                    wait(pe, exp_ready, HP * m + p - 1)
                    for h in range(2):
                        rows, out = slice(64 * h, 64 * h + 64), ps_s[p % 2]
                        for q in range(2):
                            nc.tensor.matmul(out[:, h, q * P:(2 * q + 1) * P], qT[p % 2][rows, q * P:(q + 1) * P],
                                             kT[p % 2][rows, 0:(q + 1) * P], start=True, stop=False)
                            last = nc.tensor.matmul(out[:, h, 2 * q * P:(2 * q + 1) * P], t["ident_b"][:],
                                                    t["future_q"][:], start=False, stop=True)
                    last.then_inc(s_done, 1)

                def turn(m, b, p):
                    pe.wait_ge(divided, HP * m + p + 1)
                    wait(pe, probT_ready, HP * m + p)
                    for h in range(2):
                        for n in range(3):
                            cols = slice(n * P, (n + 1) * P)
                            last = nc.tensor.transpose(ps_t[:, h, cols], prob[p % 4][:, h, cols], t["ident"][:])
                    last.then_inc(t_done, 1)

                def weigh(m, b, p):
                    pe.wait_ge(probT_ready, HP * m + p + 1)
                    if p % 4 == 0:
                        pe.wait_ge(v_ready, 4 * m + 2 + p // 2)
                    wait(pe, o_ready, HP * m + p)
                    for keys in range(2):
                        for h in range(2):
                            head = 2 * p + h
                            last = nc.tensor.matmul(ps_o[64 * h:64 * h + 64, keys * P:T],
                                                    v[:, keys, head * 64:(head + 1) * 64],
                                                    probT[p % 2][:, h, 2 * P:3 * P] if keys else probT[p % 2][:, h, 0:T],
                                                    start=(keys == 0), stop=(keys == 1))
                    last.then_inc(o_done, 1)

                def project_out(m, b):
                    pe.wait_ge(o_ready, HP * m + HP)
                    for r in range(2):
                        for p in range(HP):
                            last = nc.tensor.matmul(ps_q[:, r * D:(r + 1) * D], o[b][:, p, r * P:(r + 1) * P],
                                                    wo[:, p, :], start=(p == 0), stop=(p == HP - 1))
                    last.then_inc(z_done, 1)

                pe.wait_ge(w_in, W_ALL)
                slab_wait(0, 0)
                project(0, 0, 0)
                for n in range(2):
                    if n == 0:
                        pe.wait_ge(qk_ready, 1)
                    else:
                        pe.wait_ge(v_ready, 1)
                    values(0, 0, n)

                def pair(m, b, p):
                    after, before = (m, b, p + 1) if p + 1 < HP else (m + 1, 1 - b, 0), ago(m, b, p, 1)
                    if exists(m):
                        scores(m, b, p)
                    if exists(after[0]):
                        made = chunk_at(*before)
                        if isinstance(m, int) and (m, p) == (0, 0):
                            made = (0, 0, 1)
                        if exists(made[0]):
                            pe.wait_ge(v_ready, 4 * made[0] + made[2] + 1)
                        if before[2] == OUT:
                            wait(pe, z_ready, m)
                        project(*after)
                    turned, weighed = ago(m, b, p, TURN), ago(m, b, p, WEIGH)
                    if exists(turned[0]):
                        turn(*turned)
                    if exists(weighed[0]):
                        weigh(*weighed)
                    chunk = chunk_at(m, b, p)
                    if exists(chunk[0]):
                        pe.wait_ge(qk_ready, HP * m + p + 2)
                        if p == 6:
                            slab_wait(m + 1, 1 - b)
                        values(*chunk)
                    if p == OUT and exists(m - 1):
                        if exists(after[0]):
                            pe.wait_ge(qk_ready, HP * m + p + 2)
                        project_out(m - 1, 1 - b)

                loop(pe, pair)


def layer1_join(nc, t, d):
    with ExitStack() as ctx:
        def sb(name, shape, dt):
            return ctx.enter_context(nc.sbuf_tensor(name, shape, dt))

        def sem(name):
            return ctx.enter_context(semaphore(nc, t, "j1_" + name))

        s = t["s"]
        x, x1 = sb("x_again", [P, TILES, D], F32), sb("x1_again", [P, 2, CT, D], F32)
        y = [sb(f"y_best{a}", [P, TILES, D], F32) for a in range(2)]
        g2, b2 = sb("ln2_g", [P, D], F32), sb("ln2_b", [P, D], F32)
        norm = Norm(nc, sem, sb, "n3")
        w_in, x_in, x1_in = sem("w_in"), sem("x_in"), [sem("x1_in0"), sem("x1_in1")]
        got = [sem(f"got{c}") for c in range(CHUNKS)]
        inner, gated, done, out_done = sem("inner"), sem("gated"), sem("done"), sem("out_done")
        dve_step = sem("dve_step")

        def rows(name, c):
            return d[name].rearrange("(t p) d -> p t d", p=P)[:, c * CT:(c + 1) * CT, :]

        with nc.Block() as block:

            @block.sync
            def _(sp):
                for m, n in ((g2, "ln2_g"), (b2, "ln2_b")):
                    sp.dma_start(m[:], d[n].to_broadcast([P, D])).then_inc(w_in, 16)
                for c in range(CHUNKS):
                    sp.dma_start(x[:, c * CT:(c + 1) * CT, :], rows("x_rows", c)).then_inc(x_in, 16)
                for c in range(CHUNKS):
                    if c >= 2:
                        sp.wait_ge(inner, c - 1)
                    sp.dma_start(x1[:, c % 2, :, :], rows("x1_rows", c)).then_inc(x1_in[c % 2], 16)
                for c in range(CHUNKS):
                    sp.wait_ge(done, c + 1)
                    sp.dma_start(rows("out", c), x[:, c * CT:(c + 1) * CT, :]).then_inc(out_done, 16)
                sp.wait_ge(out_done, 16 * CHUNKS)

            @block.gpsimd
            def _(pool):
                for i in range(TILES):
                    for a in range(2):
                        n = a * TILES + i
                        pool.indirect_dma_start(y[a][:, i, :], None, d["outs1"],
                                                bass.IndirectOffsetOnAxis(t["slot1"][:, n:n + 1], 0))\
                            .then_inc(got[i // CT], 16)

            @block.scalar
            def _(act):
                for c in range(CHUNKS):
                    part = y[0][:, c * CT:(c + 1) * CT, :]
                    norm.scalar(act, c, part, t["eps"][:])
                    act.wait_ge(inner, c + 1)
                    nc.scalar.activation(part, part, ACT.Silu).then_inc(gated, 1)

            @block.vector
            def _(dve):
                link = Chain(dve, dve_step)
                dve.wait_ge(w_in, 32)
                dve.wait_ge(x_in, 16 * CHUNKS)
                for c in range(CHUNKS):
                    q = slice(c * CT, (c + 1) * CT)
                    dve.wait_ge(got[c], 32 * CT)
                    for a in range(2):
                        weight = t["weight1"][:, a * TILES + c * CT:a * TILES + (c + 1) * CT]
                        link(nc.vector.tensor_tensor(y[a][:, q, :], y[a][:, q, :], over(weight, D, 2), ALU.mult))
                    link(nc.vector.tensor_tensor(y[0][:, q, :], y[0][:, q, :], y[1][:, q, :], ALU.add))
                    norm.vector(link, c, y[0][:, q, :], y[0][:, q, :])
                    link(nc.vector.tensor_tensor(y[0][:, q, :], y[0][:, q, :], over(g2[:], CT, 1), ALU.mult))
                    link(nc.vector.tensor_tensor(y[0][:, q, :], y[0][:, q, :], over(b2[:], CT, 1), ALU.add))
                    dve.wait_ge(x1_in[c % 2], 16 * (c // 2 + 1))
                    nc.vector.tensor_tensor(y[0][:, q, :], y[0][:, q, :], x1[:, c % 2, :, :], ALU.add).then_inc(inner, 1)
                    dve.wait_ge(gated, c + 1)
                    link(nc.vector.tensor_tensor(y[0][:, q, :], y[0][:, q, :], s[:, q, :], ALU.mult))
                    nc.vector.tensor_tensor(x[:, q, :], x[:, q, :], y[0][:, q, :], ALU.add).then_inc(done, 1)


def shared(sb):
    return dict(
        semaphores=[], ident=sb("ident", [P, P], F32), ident_b=sb("ident_b", [P, P], BF16), ones=sb("ones", [P, P], F32),
        before=sb("before", [P, P], F32), zero_b=sb("zero_b", [P, P], BF16),
        future_q=sb("future_q", [P, P], BF16), future_k=sb("future_k", [P, P], BF16),
        rank8=sb("rank8", [P, EXPERTS], F32), tile_no=sb("tile_no", [1, expert_tiles(2 * TOKENS)], F32),
        eps=sb("eps", [P, 1], F32), zeros=sb("zeros", [P, 4 * D], F32),
        slot0=sb("slot0", [P, TILES], I32), expert0=sb("expert0", [1, expert_tiles(TOKENS)], I32),
        slot1=sb("slot1", [P, 2 * TILES], I32), expert1=sb("expert1", [1, expert_tiles(2 * TOKENS)], I32),
        weight1=sb("weight1", [P, 2 * TILES], F32), s=sb("s", [P, TILES, D], F32))


def program(nc, d):
    def dram(name, *shape):
        d[name] = nc.dram_tensor("scratch_" + name, shape, F32, kind="Internal").ap()

    dram("rows0", expert_tiles(TOKENS) * SLOTS, D)
    dram("outs0", expert_tiles(TOKENS) * SLOTS, D)
    dram("rows1", expert_tiles(2 * TOKENS) * SLOTS, D)
    dram("outs1", expert_tiles(2 * TOKENS) * SLOTS, D)
    dram("xnT", D, TOKENS)
    dram("x_rows", TOKENS, D)
    dram("x1_rows", TOKENS, D)
    with ExitStack() as ctx:
        def sb(name, shape, dt):
            return ctx.enter_context(nc.sbuf_tensor(name, shape, dt))

        t = shared(sb)
        constants(nc, t)
        with nc.sbuf_tensor("xn", [P, TILES, D], F32) as xn:
            t["xn"] = xn
            with nc.sbuf_tensor("x", [P, TILES, D], F32) as x:
                t["x"] = x
                layer0_front(nc, t, d)
                experts(nc, t, d, "0", expert_tiles(TOKENS), ACT.Relu, t["expert0"])
                layer0_join(nc, t, d)
                clear(nc, t)
            small_attention(nc, t, d)
            layer1_route(nc, t, d)
        causal_attention(nc, t, d)
        clear(nc, t)
        experts(nc, t, d, "1", expert_tiles(2 * TOKENS), ACT.Gelu, t["expert1"])
        layer1_join(nc, t, d)


def layout(i):
    import numpy as np

    def experts_pack(w1T, w2T, b1, b2):
        e = w1T.shape[0]
        w2 = w2T.reshape(e, HC, P, D).transpose(0, 2, 1, 3).reshape(e, P, HC * D)
        return np.ascontiguousarray(np.concatenate(
            [w1T, w2, b1.reshape(e, HC, P).transpose(0, 2, 1), np.broadcast_to(b2[:, None, :], (e, P, D))], axis=2))

    def by_channel(a):
        return c(a.reshape(-1, HEADS_B, DH_B).transpose(0, 2, 1).reshape(a.shape[0], -1))

    c = np.ascontiguousarray
    return {
        "x": c(i["L0_attn_x"].reshape(TOKENS, D)),
        "A": c(i["L0_attn_A"]), "AT": c(i["L0_attn_A"].T), "BmT": c(i["L0_attn_Bm"].T),
        "CT": c(i["L0_attn_C"].T), "W_inT": c(i["L0_attn_W_in"].T), "b_in": c(i["L0_attn_b_in"].reshape(N_STATE, 1)),
        "D": c(i["L0_attn_D"].reshape(1, D)),
        "gate0T": c(i["L0_ffn_gate_w"].T), "gate0_b": c(i["L0_ffn_gate_b"].reshape(1, EXPERTS)),
        "w0": experts_pack(i["L0_ffn_w1"].transpose(0, 2, 1), i["L0_ffn_w2"].transpose(0, 2, 1), i["L0_ffn_b1"],
                           i["L0_ffn_b2"]),
        **{"f_" + n: by_channel(i["L1_ffn_" + n]) for n in ("Wq", "Wk")},
        **{"f_" + n: c(i["L1_ffn_" + n]) for n in ("Wv", "Wo")},
        "gate1": c(i["L1_ffn_gate_w"]), "gate1_b": c(i["L1_ffn_gate_b"].reshape(1, EXPERTS)),
        **{n: c(i["L1_ffn_" + n].reshape(1, D)) for n in ("ln1_g", "ln1_b", "ln2_g", "ln2_b")},
        "w1": experts_pack(i["L1_ffn_W1"], i["L1_ffn_W2"], i["L1_ffn_b1"], i["L1_ffn_b2"]),
        "a_w": c(i["L1_attn_Wqkv_w"].T),
        "a_wo": c(i["L1_attn_Wo_w"].T.reshape(PAIRS_A, P, D).transpose(1, 0, 2)),
        "a_bq": c(i["L1_attn_Wqkv_b"][0:QKV].reshape(PAIRS_A, P).T),
        "a_bk": c(i["L1_attn_Wqkv_b"][QKV:2 * QKV].reshape(PAIRS_A, P).T),
        "a_bv": c(i["L1_attn_Wqkv_b"][2 * QKV:].reshape(1, QKV)), "a_bo": c(i["L1_attn_Wo_b"].reshape(1, D)),
        "ghost": c(i["L1_attn_ghost"].reshape(1, HEADS_A)),
        **{"f_" + n: by_channel(i["L1_ffn_" + n].reshape(1, D)).reshape(D, 1) for n in ("bq", "bk")},
        "f_bv": c(i["L1_ffn_bv"].reshape(1, D)), "f_bo": c(i["L1_ffn_bo"].reshape(1, D)),
    }


def kernel(**inputs):
    import numpy as np
    import concourse.bacc as bacc
    from concourse.bass_utils import run_bass_kernel_spmd

    nc = bacc.Bacc("TRN2", target_bir_lowering=False, num_devices=1)
    arrays, d = {}, {}
    for name, a in layout(inputs).items():
        arrays["in_" + name] = a
        d[name] = nc.dram_tensor("in_" + name, a.shape, mybir.dt.from_np(a.dtype), kind="ExternalInput").ap()
    d["out"] = nc.dram_tensor("out_rows", (TOKENS, D), F32, kind="ExternalOutput").ap()
    program(nc, d)
    ran = run_bass_kernel_spmd(nc, [arrays], core_ids=[0])
    return ran.results[0]["out_rows"].reshape(BATCH, SEQ, D)
```

```python
from contextlib import ExitStack, contextmanager

import concourse.bass as bass
from concourse import mybir

ALU = mybir.AluOpType
ACT = mybir.ActivationFunctionType
F32 = mybir.dt.float32
BF16 = mybir.dt.bfloat16
F32R = mybir.dt.float32r
I32 = mybir.dt.int32
AX_X = mybir.AxisListType.X

P = 128
BATCH, SEQ, D = 32, 256, 128
TOKENS = BATCH * SEQ
TILES = TOKENS // P
EXPERTS, HIDDEN = 8, 512
HC = HIDDEN // P
SLOTS = 256
EPS = 1e-5
CHUNKS = 4
CT = TILES // CHUNKS
N_STATE = 32
NEG = -1.0e30
PLACE, WEIGHT, ROW = D, D + 1, D + 2


NBUF = 4


def expert_tiles(assigned):
    n = assigned // SLOTS + EXPERTS - 1
    return -(-n // NBUF) * NBUF


class Chain:

    def __init__(self, eng, sem):
        self.eng, self.sem, self.n = eng, sem, 0

    def __call__(self, ins):
        self.n += 1
        ins.then_inc(self.sem, 1)
        self.eng.wait_ge(self.sem, self.n)


def over(ap, n, axis):
    a = ap.unsqueeze(axis)
    shape = list(a.shape)
    shape[axis] = n
    return a.to_broadcast(shape)


@contextmanager
def semaphore(nc, t, name):
    t["semaphores"].append(nc.alloc_semaphore(name=name))
    yield t["semaphores"][-1]


def clear(nc, t):
    nc.clear_and_free_semaphores(t["semaphores"])
    nc.all_engine_barrier()
    t["semaphores"] = []


def constants(nc, t):
    with semaphore(nc, t, "const_step") as step, nc.Block() as block:

        @block.gpsimd
        def _(pool):
            link = Chain(pool, step)
            link(nc.gpsimd.memset(t["ident"][:], 0.0))
            link(nc.gpsimd.affine_select(out=t["ident"][:], in_=t["ident"][:], compare_op=ALU.not_equal,
                                         fill=1.0, base=0, pattern=[[-1, P]], channel_multiplier=1))
            link(nc.gpsimd.tensor_copy(t["ident_b"][:], t["ident"][:]))
            link(nc.gpsimd.memset(t["ones"][:], 1.0))
            link(nc.gpsimd.affine_select(out=t["before"][:], in_=t["ones"][:], compare_op=ALU.is_gt,
                                         fill=0.0, base=0, pattern=[[1, P]], channel_multiplier=-1))
            link(nc.gpsimd.memset(t["zero_b"][:], 0.0))
            link(nc.gpsimd.affine_select(out=t["future_q"][:], in_=t["zero_b"][:], compare_op=ALU.is_ge,
                                         fill=NEG, base=0, pattern=[[-1, P]], channel_multiplier=1))
            link(nc.gpsimd.affine_select(out=t["future_k"][:], in_=t["zero_b"][:], compare_op=ALU.is_ge,
                                         fill=NEG, base=0, pattern=[[1, P]], channel_multiplier=-1))
            link(nc.gpsimd.iota(t["rank8"][:], pattern=[[-1, EXPERTS]], base=EXPERTS, channel_multiplier=0,
                                allow_small_or_imprecise_dtypes=True))
            n = t["tile_no"].shape[1]
            link(nc.gpsimd.iota(t["tile_no"][:], pattern=[[1, n]], base=0, channel_multiplier=0,
                                allow_small_or_imprecise_dtypes=True))
            link(nc.gpsimd.memset(t["eps"][:], EPS))
            link(nc.gpsimd.memset(t["zero_i"][:], 0))
            link(nc.gpsimd.memset(t["zero_f"][:], 0.0))


class Norm:

    def __init__(self, nc, sem, sb, name):
        self.nc = nc
        self.mean_ready, self.std_ready = sem(name + "_mean_ready"), sem(name + "_std_ready")
        self.summed = sem(name + "_summed")
        self.sq = sb(name + "_sq", [P, CT, D], F32)
        self.mean = sb(name + "_mean", [P, TILES], F32)
        self.var = sb(name + "_var", [P, TILES], F32)
        self.std = sb(name + "_std", [P, TILES], F32)
        self.rstd = sb(name + "_rstd", [P, TILES], F32)

    def begin(self, link, c, src):
        q = slice(c * CT, (c + 1) * CT)
        link(self.nc.vector.tensor_reduce(self.mean[:, q], src, AX_X, ALU.add))
        self.nc.vector.tensor_scalar(self.mean[:, q], self.mean[:, q], -1.0 / D, None, ALU.mult)\
            .then_inc(self.mean_ready, 1)

    def scalar(self, act, c, src, eps):
        q = slice(c * CT, (c + 1) * CT)
        act.wait_ge(self.mean_ready, c + 1)
        if c:
            act.wait_ge(self.std_ready, c)
        for i in range(CT):
            n = c * CT + i
            last = self.nc.scalar.activation(self.sq[:, i, :], src[:, i, :], ACT.Square, bias=self.mean[:, n:n + 1],
                                             accum_out=self.var[:, n:n + 1])
        last.then_inc(self.summed, 1)
        act.wait_ge(self.summed, c + 1)
        self.nc.scalar.activation(self.std[:, q], self.var[:, q], ACT.Sqrt, bias=eps, scale=1.0 / D)\
            .then_inc(self.std_ready, 1)

    def finish(self, link, c, src, out, sem):
        q = slice(c * CT, (c + 1) * CT)
        link.eng.wait_ge(self.mean_ready, c + 1)
        link.eng.wait_ge(self.std_ready, c + 1)
        link(self.nc.vector.reciprocal(self.rstd[:, q], self.std[:, q]))
        for i in range(CT):
            n = c * CT + i
            last = self.nc.vector.tensor_scalar(out[:, i, :], src[:, i, :], self.mean[:, n:n + 1],
                                                self.rstd[:, n:n + 1], ALU.add, ALU.mult)
        last.then_inc(sem, 1)


def first_of(nc, link, out, values, best, work, rank8, tiles, ready=None):
    link(nc.vector.tensor_reduce(best, values, AX_X, ALU.max))
    link(nc.vector.tensor_tensor(work, values, over(best, EXPERTS, 2), ALU.is_ge))
    link(nc.vector.tensor_tensor(work, work, over(rank8, tiles, 1), ALU.mult))
    link(nc.vector.tensor_reduce(best, work, AX_X, ALU.max))
    last = nc.vector.tensor_tensor(out, work, over(best, EXPERTS, 2), ALU.is_ge)
    if ready is None:
        link(last)
    else:
        last.then_inc(ready, 1)
        link.eng.wait_ge(ready, 1)


def route(nc, dve, link, t, r, n_assign, n_tiles, counted, ready):
    n = n_assign * TILES
    dve.wait_ge(counted, 1)
    flat = lambda x: x[:].rearrange("p t e -> p (t e)")
    ps = lambda x: x[:, 0:n_assign, :].rearrange("p b n -> p (b n)")
    link(nc.vector.tensor_copy(flat(r["total"]), ps(r["ps_total"])))
    for e in range(EXPERTS):
        link(nc.vector.tensor_tensor_scan(r["upto"][:, :, e], t["ones"][:, 0:n] if n <= P else t["ones"][:],
                                          r["total"][:, :, e], 0.0, ALU.mult, ALU.add))
    link(nc.vector.tensor_copy(r["count"][:], r["upto"][:, n - 1, :]))
    link(nc.vector.tensor_tensor(flat(r["upto"]), flat(r["upto"]), flat(r["total"]), ALU.subtract))
    link(nc.vector.tensor_tensor(flat(r["upto"]), flat(r["upto"]), ps(r["ps_rank"]), ALU.add))
    link(nc.vector.tensor_scalar(r["count_i"][:], r["count"][:], float(SLOTS - 1), None, ALU.add))
    link(nc.vector.tensor_single_scalar(r["count_i"][:], r["count_i"][:], SLOTS.bit_length() - 1,
                                        ALU.arith_shift_right))
    link(nc.vector.tensor_copy(r["count"][:], r["count_i"][:]))
    link(nc.vector.tensor_tensor_scan(r["last"][:], t["ones"][:, 0:EXPERTS], r["count"][:], 0.0,
                                      ALU.mult, ALU.add))
    link(nc.vector.tensor_tensor(r["base"][:], r["last"][:], r["count"][:], ALU.subtract))
    link(nc.vector.tensor_scalar(r["base"][:], r["base"][:], float(SLOTS), None, ALU.mult))
    link(nc.vector.tensor_tensor(r["upto"][:], r["upto"][:], over(r["base"][:], n, 1), ALU.add))
    link(nc.vector.tensor_tensor(flat(r["upto"]), flat(r["upto"]), flat(r["chosen"]), ALU.mult))
    link(nc.vector.tensor_reduce(r["slot_f"][:], r["upto"][:], AX_X, ALU.add))
    link(nc.vector.tensor_copy(r["slot"][:], r["slot_f"][:]))
    link(nc.vector.tensor_tensor(r["ended"][:], over(t["tile_no"][0:1, 0:n_tiles], EXPERTS, 2),
                                 over(r["last"][0:1, :], n_tiles, 1), ALU.is_ge))
    link(nc.vector.tensor_reduce(r["expert_f"][:], r["ended"][:], AX_X, ALU.add))
    nc.vector.tensor_scalar(r["expert"][:], r["expert_f"][:], float(EXPERTS - 1), None,
                            ALU.min).then_inc(ready, 1)


def route_counts(nc, pe, t, r, n_assign, counted):
    flat = r["chosen"][:].rearrange("p t e -> p (t e)")
    for a in range(n_assign):
        part = flat[:, a * 512:(a + 1) * 512]
        nc.tensor.matmul(r["ps_rank"][:, a, :], t["before"][:], part, start=True, stop=True)
        last = nc.tensor.matmul(r["ps_total"][:, a, :], t["ones"][:], part, start=True, stop=True)
    last.then_inc(counted, 1)


def route_buffers(sb, pb, n_assign, n_tiles, keep, tag):
    n = n_assign * TILES
    return dict(
        keep,
        chosen=sb("chosen" + tag, [P, n, EXPERTS], F32), total=sb("total" + tag, [P, n, EXPERTS], F32),
        upto=sb("upto" + tag, [P, n, EXPERTS], F32), count=sb("count" + tag, [P, EXPERTS], F32),
        count_i=sb("count_i" + tag, [P, EXPERTS], I32), last=sb("last" + tag, [P, EXPERTS], F32),
        base=sb("base" + tag, [P, EXPERTS], F32), slot_f=sb("slot_f" + tag, [P, n], F32),
        ended=sb("ended" + tag, [1, n_tiles, EXPERTS], F32), expert_f=sb("expert_f" + tag, [1, n_tiles], F32),
        ps_rank=pb("ps_rank" + tag, [P, n_assign, 512], F32), ps_total=pb("ps_total" + tag, [P, n_assign, 512], F32))


def layer0_front(nc, t, d):
    with ExitStack() as ctx:
        def sb(name, shape, dt):
            return ctx.enter_context(nc.sbuf_tensor(name, shape, dt))

        def pb(name, shape, dt):
            return ctx.enter_context(nc.psum_tensor(name, shape, dt))

        def sem(name):
            return ctx.enter_context(semaphore(nc, t, name))

        x, xn, s = t["x"], t["xn"], t["s"]
        xnT = sb("xnT", [P, TOKENS], F32)
        win = sb("win", [P, N_STATE], F32)
        bd = sb("bd", [P, 2, P], F32)
        bdT = sb("bdT", [P, P], F32)
        pw = sb("pw", [P, 8, P], F32)
        pwT = sb("pwT", [P, 8, P], F32)
        cpad = sb("cpad", [P, 4, P], F32)
        b_in = sb("b_in", [P, 1], F32)
        d_bc = sb("d_bc", [P, D], F32)
        gw = sb("gw", [P, P], F32)
        gb = sb("gb", [P, EXPERTS], F32)
        u = sb("u", [P, 2048], F32)
        h = sb("h", [P, 8, SEQ], F32)
        logits = sb("logits", [P, TILES, EXPERTS], F32)
        best = sb("best", [P, TILES], F32)
        norm = Norm(nc, sem, sb, "n0")
        ps = pb("ps", [P, 6, 512], F32)
        PAD = 8
        pad = [sb(f"pad{b}", [P, PAD, ROW], F32) for b in range(2)]
        pads = [(name, q, rows + q * P) for name, rows in (("rows0", TOKENS), ("rows1", 2 * TOKENS))
                for q in range(0, 2 * expert_tiles(rows), PAD)]
        n_tiles = expert_tiles(TOKENS)
        r = route_buffers(sb, pb, 1, n_tiles, dict(slot=t["slot0"], expert=t["expert0"]), "0")

        x_in = [sem(f"x_in{c}") for c in range(CHUNKS)]
        w_in, w_zero = sem("w_in"), sem("w_zero")
        placed, pad_made, padded, scattered = sem("placed"), sem("pad_made"), [sem("padded0"), sem("padded1")], sem("scattered")
        xn_ready, tr_done, xnT_ready = sem("xn_ready"), sem("tr_done"), sem("xnT_ready")
        u_done, u_ready, ub_done, h0_ready = sem("u_done"), sem("u_ready"), sem("ub_done"), sem("h0_ready")
        sq_done, pw_ready = sem("sq_done"), sem("pw_ready")
        step_done, h_ready = sem("step_done"), sem("h_ready")
        s_done, s_ready = sem("s_done"), sem("s_ready")
        g_done, g_ready = sem("g_done"), sem("g_ready")
        chosen_ready, counted, routed = sem("chosen_ready"), sem("counted"), sem("routed")
        dve_step = sem("dve_step")
        GROUPS = TILES // 4

        with nc.Block() as block:

            @block.sync
            def _(sp):
                for c in range(CHUNKS):
                    sp.dma_start(x[:, c * CT:(c + 1) * CT, :],
                                 d["x"].rearrange("(t p) d -> p t d", p=P)[:, c * CT:(c + 1) * CT, :])\
                      .then_inc(x_in[c], 16)
                sp.wait_ge(w_zero, 4)
                for g in range(4):
                    q = slice(32 * g, 32 * g + 32)
                    sp.dma_start(bd[q, 0, q], d["BmT"]).then_inc(w_in, 16)
                    sp.dma_start(bd[q, 1, q], d["A"]).then_inc(w_in, 16)
                    sp.dma_start(bdT[q, q], d["AT"]).then_inc(w_in, 16)
                    sp.dma_start(cpad[q, g, :], d["CT"]).then_inc(w_in, 16)
                    sp.dma_start(b_in[q, :], d["b_in"]).then_inc(w_in, 16)
                sp.dma_start(win[:], d["W_inT"]).then_inc(w_in, 16)
                sp.dma_start(gw[:, 0:EXPERTS], d["gate0T"]).then_inc(w_in, 16)
                sp.dma_start(gb[:], d["gate0_b"].to_broadcast([P, EXPERTS])).then_inc(w_in, 16)
                sp.dma_start(d_bc[:], d["D"].to_broadcast([P, D])).then_inc(w_in, 16)
                for n, (name, q, place) in enumerate(pads):
                    sp.wait_ge(pad_made, n + 1)
                    sp.dma_start(d[name].rearrange("(q p) d -> p q d", p=P)[:, q:q + PAD, :], pad[n % 2][:])\
                      .then_inc(padded[n % 2], 16)

            W_ALL = 16 * 24

            @block.gpsimd
            def _(pool):
                for m in (bd, bdT, cpad, gw):
                    nc.gpsimd.memset(m[:], 0.0).then_inc(w_zero, 1)
                nc.gpsimd.iota(t["row"][:, :, PLACE].bitcast(I32), pattern=[[P, TILES]], base=0, channel_multiplier=1)\
                    .then_inc(placed, 1)
                nc.gpsimd.memset(t["row"][:, :, WEIGHT], 1.0).then_inc(placed, 1)
                for b in range(2):
                    nc.gpsimd.memset(pad[b][:], 0.0).then_inc(placed, 1)
                pool.wait_ge(placed, 4)
                for n, (name, q, place) in enumerate(pads):
                    if n >= 2:
                        pool.wait_ge(padded[n % 2], 16 * (n // 2))
                    nc.gpsimd.iota(pad[n % 2][:, :, PLACE].bitcast(I32), pattern=[[P, PAD]], base=place,
                                   channel_multiplier=1).then_inc(pad_made, 1)
                pool.wait_ge(routed, 1)
                for b in range(2):
                    pool.wait_ge(padded[b], 16 * (len(pads) // 2))
                for i in range(TILES):
                    pool.indirect_dma_start(d["rows0"], bass.IndirectOffsetOnAxis(t["slot0"][:, i:i + 1], 0),
                                            t["row"][:, i, :], None).then_inc(scattered, 16)
                pool.wait_ge(scattered, 16 * TILES)

            @block.scalar
            def _(act):
                for c in range(CHUNKS):
                    norm.scalar(act, c, x[:, c * CT:(c + 1) * CT, :], t["eps"][:])
                    for g in range(4 * c, 4 * c + 4):
                        act.wait_ge(tr_done, g + 1)
                        nc.scalar.activation(xnT[:, g * 512:(g + 1) * 512], ps[:, g % 2, :],
                                             ACT.Copy).then_inc(xnT_ready, 1)
                act.wait_ge(w_in, W_ALL)
                for c in range(4):
                    act.wait_ge(u_done, c + 1)
                    nc.scalar.activation(u[:, c * 512:(c + 1) * 512], ps[:, 2 + c % 2, :], ACT.Identity,
                                         bias=b_in[:, 0:1]).then_inc(u_ready, 1)
                hf = h[:].rearrange("p b t -> p (b t)")
                for c in range(4):
                    act.wait_ge(ub_done, c + 1)
                    nc.scalar.activation(hf[:, c * 512:(c + 1) * 512], ps[:, 4 + c % 2, :],
                                         ACT.Copy).then_inc(h0_ready, 1)
                for k in range(7):
                    act.wait_ge(sq_done, k + 1)
                    nc.scalar.activation(pw[:, k + 1, :], ps[:, k % 2, 0:P], ACT.Copy).then_inc(pw_ready, 1)
                    nc.scalar.activation(pwT[:, k + 1, :], ps[:, k % 2, P:2 * P], ACT.Copy).then_inc(pw_ready, 1)

            @block.tensor
            def _(pe):
                pe.wait_ge(w_zero, 4)

                def gate(q):
                    pe.wait_ge(xnT_ready, q + 1)
                    if q == 0:
                        pe.wait_ge(w_in, W_ALL)
                    if q >= 2:
                        pe.wait_ge(g_ready, q - 1)
                    for i in range(4):
                        n = 4 * q + i
                        last = nc.tensor.matmul(ps[:, 2 + q % 2, i * P:(i + 1) * P], xnT[:, n * P:(n + 1) * P], gw[:],
                                                start=True, stop=True)
                    last.then_inc(g_done, 1)

                for g in range(GROUPS):
                    pe.wait_ge(xn_ready, g // 4 + 1)
                    if g >= 2:
                        pe.wait_ge(xnT_ready, g - 1)
                    for i in range(4):
                        last = nc.tensor.transpose(ps[:, g % 2, i * P:(i + 1) * P], xn[:, 4 * g + i, :], t["ident"][:])
                    last.then_inc(tr_done, 1)
                    if g:
                        gate(g - 1)
                gate(GROUPS - 1)
                pe.wait_ge(g_ready, GROUPS)
                for c in range(4):
                    if c >= 2:
                        pe.wait_ge(u_ready, c - 1)
                    for g in range(4):
                        last = nc.tensor.matmul(ps[32 * g:32 * g + 32, 2 + c % 2, :], win[:],
                                                xnT[:, g * 2048 + c * 512:g * 2048 + (c + 1) * 512],
                                                start=True, stop=True)
                    last.then_inc(u_done, 1)
                for c in range(4):
                    pe.wait_ge(u_ready, c + 1)
                    if c >= 2:
                        pe.wait_ge(h0_ready, c - 1)
                    nc.tensor.matmul(ps[:, 4 + c % 2, :], bd[:, 0, :], u[:, c * 512:(c + 1) * 512],
                                     start=True, stop=True).then_inc(ub_done, 1)
                pe.wait_ge(chosen_ready, 1)
                route_counts(nc, pe, t, r, 1, counted)
                for k in range(7):
                    if k:
                        pe.wait_ge(pw_ready, 2 * k)
                    a, aT = (pw[:, k, :], pwT[:, k, :]) if k else (bd[:, 1, :], bdT[:])
                    nc.tensor.matmul(ps[:, k % 2, 0:P], aT, a, start=True, stop=True)
                    nc.tensor.matmul(ps[:, k % 2, P:2 * P], a, aT, start=True, stop=True).then_inc(sq_done, 1)
                pe.wait_ge(h0_ready, 4)
                pe.wait_ge(pw_ready, 14)
                for k in range(8):
                    for c in range(4):
                        n = 4 * k + c
                        if k:
                            pe.wait_ge(h_ready, n - 3)
                        if n >= 2:
                            pe.wait_ge(h_ready, n - 1)
                        nc.tensor.matmul(ps[:, 2 + c % 2, :], pw[:, k, :] if k else bd[:, 1, :],
                                         h[:, 2 * c:2 * c + 2, :], start=True, stop=True).then_inc(step_done, 1)
                pe.wait_ge(h_ready, 32)
                for q in range(GROUPS):
                    if q >= 2:
                        pe.wait_ge(s_ready, q - 1)
                    for i in range(4):
                        n = 4 * q + i
                        b, half = n // 2, n % 2
                        last = nc.tensor.matmul(ps[:, 4 + q % 2, i * P:(i + 1) * P],
                                                h[:, b % 8, half * P:(half + 1) * P], cpad[:, b // 8, :],
                                                start=True, stop=True)
                    last.then_inc(s_done, 1)

            @block.vector
            def _(dve):
                link = Chain(dve, dve_step)

                def logit(q):
                    dve.wait_ge(g_done, q + 1)
                    nc.vector.tensor_tensor(logits[:, 4 * q:4 * q + 4, :],
                                            ps[:, 2 + q % 2, :].rearrange("p (i d) -> p i d", d=P)[:, :, 0:EXPERTS],
                                            over(gb[:], 4, 1), ALU.add).then_inc(g_ready, 1)

                part = lambda a, c: a[:, c * CT:(c + 1) * CT, :]
                dve.wait_ge(x_in[0], 16)
                norm.begin(link, 0, part(x, 0))
                for c in range(CHUNKS):
                    if c + 1 < CHUNKS:
                        dve.wait_ge(x_in[c + 1], 16)
                        norm.begin(link, c + 1, part(x, c + 1))
                    norm.finish(link, c, part(x, c), part(xn, c), xn_ready)
                    if c == 1:
                        dve.wait_ge(w_in, W_ALL)
                    if c:
                        for q in range(4 * c - 4, 4 * c):
                            logit(q)
                for q in range(GROUPS - 4, GROUPS):
                    logit(q)
                dve.wait_ge(g_ready, GROUPS)
                first_of(nc, link, r["chosen"][:], logits[:], best[:], r["total"][:], t["rank8"][:], TILES,
                         chosen_ready)
                route(nc, dve, link, t, r, 1, n_tiles, counted, routed)
                for k in range(8):
                    d_ = 1 << k
                    for c in range(4):
                        n = 4 * k + c
                        dve.wait_ge(step_done, n + 1)
                        if k:
                            dve.wait_ge(h_ready, n - 3)
                        part = h[:, 2 * c:2 * c + 2, d_:SEQ]
                        psv = ps[:, 2 + c % 2, :].rearrange("p (b t) -> p b t", t=SEQ)[:, :, 0:SEQ - d_]
                        nc.vector.tensor_tensor(part, psv, part, ALU.add).then_inc(h_ready, 1)
                for q in range(GROUPS):
                    dve.wait_ge(s_done, q + 1)
                    nc.vector.tensor_tensor(s[:, 4 * q:4 * q + 4, :],
                                            ps[:, 4 + q % 2, :].rearrange("p (i d) -> p i d", d=D),
                                            over(d_bc[:], 4, 1), ALU.add).then_inc(s_ready, 1)


def wait(eng, sem, value):
    if not isinstance(value, int) or value > 0:
        eng.wait_ge(sem, value)


def loaded(eng, sems, n, j, each=16):
    eng.wait_ge(sems[j], each * (n // NBUF + 1) if isinstance(n, int) else each // NBUF * (n - j) + each)


def three_passes(nc, out, a_hi, a_lo, b_hi, b_lo):
    nc.tensor.matmul(out, a_hi, b_hi, start=True, stop=False)
    nc.tensor.matmul(out, a_hi, b_lo, start=False, stop=False)
    return nc.tensor.matmul(out, a_lo, b_hi, start=False, stop=True)


def experts(nc, t, d, tag, n_tiles, act_fn, expert, weighted):
    with ExitStack() as ctx:
        def sb(name, shape, dt):
            return ctx.enter_context(nc.sbuf_tensor(name + tag, shape, dt))

        def pb(name, shape, dt):
            return ctx.enter_context(nc.psum_tensor(name + tag, shape, dt))

        def sem(name):
            return ctx.enter_context(semaphore(nc, t, name + tag))

        def many(n, make, name, *more):
            return [make(f"{name}{b}_", *more) for b in range(n)]

        rows, outs = d["rows" + tag], d["outs" + tag]
        B1, B2 = 2 * HIDDEN, 2 * HIDDEN + HC
        w = many(NBUF, sb, "w", [P, B2 + D], F32)
        xr = many(NBUF, sb, "xr", [P, 2, ROW], F32)
        places = many(NBUF, sb, "places", [P, 2], I32)
        y = many(NBUF, sb, "y", [P, 2, D], F32)
        xT_hi, xT_lo = many(2, sb, "xT_hi", [P, SLOTS], F32R), many(2, sb, "xT_lo", [P, SLOTS], F32R)
        w1_hi, w1_lo = many(2, sb, "w1_hi", [P, HIDDEN], F32R), many(2, sb, "w1_lo", [P, HIDDEN], F32R)
        hid = many(2, sb, "hid", [P, HC, SLOTS], F32)
        ps_x, ps_h, ps_y = (many(2, pb, n, s, F32) for n, s in (("ps_x", [P, 512]), ("ps_h", [P, 2, 512]),
                                                                ("ps_y", [P, 512])))
        w_in, x_in, stored = many(NBUF, sem, "w_in"), many(NBUF, sem, "x_in"), many(NBUF, sem, "stored")
        tr_done, xT_ready, up_a, up_b = sem("tr_done"), sem("xT_ready"), sem("up_a"), sem("up_b")
        hid_a, hid_b, down, y_ready = sem("hid_a"), sem("hid_b"), sem("down"), sem("y_ready")
        places_ready, xT_hi_ready = sem("places_ready"), sem("xT_hi_ready")
        biased = sem("biased")
        w1_hi_ready, w1_lo_ready = sem("w1_hi_ready"), sem("w1_lo_ready")
        relu = act_fn == ACT.Relu
        groups = n_tiles // NBUF

        def exists(n):
            return not isinstance(n, int) or 0 <= n < n_tiles

        def loop(eng, step):
            for j in range(NBUF):
                step(j, j)
            with eng.Fori(1, groups - 1) as i:
                for j in range(NBUF):
                    step(NBUF * i + j, j)
            for j in range(NBUF):
                step(n_tiles - NBUF + j, j)

        with nc.Block() as block:

            @block.sync
            def _(sp):
                def load(n, j):
                    if not exists(n):
                        return
                    wait(sp, tr_done, n - NBUF + 1)
                    wait(sp, places_ready, n - NBUF + 1)
                    if weighted:
                        wait(sp, y_ready, n - NBUF + 1)
                    sp.dma_start(xr[j][:], rows.rearrange("(n r p) d -> n p r d", p=P, r=2)[bass.ds(n, 1)]
                                 .rearrange("o p r d -> p (o r) d")).then_inc(x_in[j], 16)
                    e = sp.value_load(expert[0:1, bass.ds(n, 1)], min_val=0, max_val=EXPERTS - 1)
                    wait(sp, y_ready, n - NBUF + 1)
                    sp.dma_start(w[j][:], d["w" + tag][bass.ds(e, 1)].rearrange("o p n -> p (o n)"))\
                      .then_inc(w_in[j], 16)

                for n in range(NBUF):
                    load(n, n)
                for j in range(NBUF):
                    load(NBUF + j, j)
                with sp.Fori(1, groups - 1) as i:
                    for j in range(NBUF):
                        load(NBUF * i + NBUF + j, j)

            @block.gpsimd
            def _(pool):
                def place(n, j):
                    loaded(pool, x_in, n, j)
                    if exists(n - NBUF):
                        loaded(pool, stored, n - NBUF, j, 32)
                    nc.gpsimd.tensor_tensor(places[j][:], xr[j][:, :, PLACE].bitcast(I32), t["zero_i"][:], ALU.add)\
                        .then_inc(places_ready, 1)

                def store(n, j):
                    pool.wait_ge(places_ready, n + 1)
                    pool.wait_ge(y_ready, n + 1)
                    if exists(n + 1):
                        place(n + 1, (j + 1) % NBUF)
                    for r in range(2):
                        pool.indirect_dma_start(outs, bass.IndirectOffsetOnAxis(places[j][:, r:r + 1], 0),
                                                y[j][:, r, :], None).then_inc(stored[j], 16)

                place(0, 0)
                loop(pool, store)
                for j in range(NBUF):
                    pool.wait_ge(stored[j], 32 * groups)

            @block.scalar
            def _(act):
                def hidden(n, j):
                    wait(act, down, n - 1)
                    loaded(act, w_in, n, j)
                    for c in range(2 if relu else HC):
                        if c == 0:
                            act.wait_ge(up_a, n + 1)
                        if c == 2:
                            act.wait_ge(up_b, n + 1)
                        ins = nc.scalar.activation(hid[j % 2][:, c, :],
                                                   ps_h[j % 2][:, c // 2, (c % 2) * SLOTS:(c % 2 + 1) * SLOTS],
                                                   act_fn, bias=w[j][:, B1 + c:B1 + c + 1])
                        if c == 1:
                            ins.then_inc(hid_a, 1)
                        if c == 3:
                            ins.then_inc(hid_b, 1)

                def high_part(n, j):
                    loaded(act, w_in, n, j)
                    wait(act, up_b, n - 1)
                    nc.scalar.activation(w1_hi[j % 2][:], w[j][:, 0:HIDDEN], ACT.Copy).then_inc(w1_hi_ready, 1)

                def step(n, j):
                    hidden(n, j)
                    if exists(n + 2):
                        high_part(n + 2, (j + 2) % NBUF)

                high_part(0, 0)
                high_part(1, 1)
                loop(act, step)

            @block.vector
            def _(dve):
                def turned(n, j):
                    dve.wait_ge(tr_done, n + 1)
                    wait(dve, up_b, n - 1)
                    nc.vector.tensor_copy(xT_hi[j % 2][:], ps_x[j % 2][:, 0:SLOTS]).then_inc(xT_hi_ready, 1)
                    dve.wait_ge(xT_hi_ready, n + 1)
                    nc.vector.tensor_tensor(xT_lo[j % 2][:], ps_x[j % 2][:, 0:SLOTS], xT_hi[j % 2][:],
                                            ALU.subtract).then_inc(xT_ready, 1)

                def low_part(n, j):
                    dve.wait_ge(w1_hi_ready, n + 1)
                    nc.vector.tensor_tensor(w1_lo[j % 2][:], w[j][:, 0:HIDDEN], w1_hi[j % 2][:],
                                            ALU.subtract).then_inc(w1_lo_ready, 1)

                def hidden(n, j):
                    wait(dve, down, n - 1)
                    loaded(dve, w_in, n, j)
                    dve.wait_ge(up_b, n + 1)
                    for c in (2, 3):
                        ins = nc.vector.tensor_scalar(
                            hid[j % 2][:, c, :], ps_h[j % 2][:, 1, (c - 2) * SLOTS:(c - 1) * SLOTS],
                            w[j][:, B1 + c:B1 + c + 1], 0.0, ALU.add, ALU.max)
                    ins.then_inc(hid_b, 1)

                def output(n, j):
                    dve.wait_ge(down, n + 1)
                    if exists(n - NBUF):
                        loaded(dve, stored, n - NBUF, j, 32)
                    loaded(dve, w_in, n, j)
                    out = nc.vector.tensor_tensor(y[j][:], ps_y[j % 2][:, 0:2 * D].rearrange("p (r d) -> p r d", d=D),
                                                  over(w[j][:, B2:B2 + D], 2, 1), ALU.add)
                    if not weighted:
                        out.then_inc(y_ready, 1)
                        return
                    out.then_inc(biased, 1)
                    dve.wait_ge(biased, n + 1)
                    for r in range(2):
                        out = nc.vector.tensor_scalar(y[j][:, r, :], y[j][:, r, :], xr[j][:, r, WEIGHT:WEIGHT + 1],
                                                      None, ALU.mult)
                    out.then_inc(y_ready, 1)

                def step(n, j):
                    if exists(n + 2):
                        turned(n + 2, (j + 2) % NBUF)
                        low_part(n + 2, (j + 2) % NBUF)
                    if relu and exists(n + 1):
                        hidden(n + 1, (j + 1) % NBUF)
                    output(n, j)

                turned(0, 0)
                turned(1, 1)
                low_part(0, 0)
                low_part(1, 1)
                if relu:
                    hidden(0, 0)
                loop(dve, step)

            @block.tensor
            def _(pe):
                def turn(n, j):
                    loaded(pe, x_in, n, j)
                    wait(pe, xT_ready, n - 1)
                    for r in range(2):
                        last = nc.tensor.transpose(ps_x[j % 2][:, r * P:(r + 1) * P], xr[j][:, r, 0:D], t["ident"][:])
                    last.then_inc(tr_done, 1)

                def up(n, j):
                    pe.wait_ge(xT_ready, n + 1)
                    pe.wait_ge(w1_lo_ready, n + 1)
                    for c in range(HC):
                        if c == 0:
                            wait(pe, hid_a, n - 1)
                        if c == 2:
                            wait(pe, hid_b, n - 1)
                        cols = slice(c * P, (c + 1) * P)
                        last = three_passes(nc, ps_h[j % 2][:, c // 2, (c % 2) * SLOTS:(c % 2 + 1) * SLOTS],
                                            w1_hi[j % 2][:, cols], w1_lo[j % 2][:, cols],
                                            xT_hi[j % 2][:], xT_lo[j % 2][:])
                        if c == 1:
                            last.then_inc(up_a, 1)
                    last.then_inc(up_b, 1)

                def down_(n, j):
                    pe.wait_ge(hid_a, n + 1)
                    pe.wait_ge(hid_b, n + 1)
                    loaded(pe, w_in, n, j)
                    wait(pe, y_ready, n - 1)
                    for r in range(2):
                        for c in range(HC):
                            last = nc.tensor.matmul(ps_y[j % 2][:, r * D:(r + 1) * D], hid[j % 2][:, c, r * P:(r + 1) * P],
                                                    w[j][:, HIDDEN + c * D:HIDDEN + (c + 1) * D],
                                                    start=(c == 0), stop=(c == HC - 1))
                    last.then_inc(down, 1)

                def step(n, j):
                    if exists(n + 2):
                        turn(n + 2, (j + 2) % NBUF)
                    if exists(n + 1):
                        up(n + 1, (j + 1) % NBUF)
                    down_(n, j)

                turn(0, 0)
                turn(1, 1)
                up(0, 0)
                loop(pe, step)


def layer0_join(nc, t, d):
    with ExitStack() as ctx:
        def sb(name, shape, dt):
            return ctx.enter_context(nc.sbuf_tensor(name, shape, dt))

        def pb(name, shape, dt):
            return ctx.enter_context(nc.psum_tensor(name, shape, dt))

        def sem(name):
            return ctx.enter_context(semaphore(nc, t, name))

        x, xn, s = t["x"], t["xn"], t["s"]
        g = sb("g_rows", [P, TILES, D], F32)
        xnT = sb("xnT_b", [P, 4, 512], F32)
        norm = Norm(nc, sem, sb, "n1")
        ps = pb("ps_t", [P, 4, 512], F32)
        got = [sem(f"got{c}") for c in range(CHUNKS)]
        gated, product, xn_ready = sem("gated"), sem("product"), sem("xn1_ready")
        tr_done, xnT_ready, xnT_out = sem("tr1_done"), sem("xnT1_ready"), [sem(f"xnT_out{i}") for i in range(4)]
        dve_step, x_out = sem("dve1_step"), sem("x_out")
        GROUPS = TILES // 4

        with nc.Block() as block:

            @block.gpsimd
            def _(pool):
                for c in range(CHUNKS):
                    q = slice(c * CT, (c + 1) * CT)
                    pool.wait_ge(gated, c + 1)
                    nc.gpsimd.tensor_tensor(g[:, q, :], g[:, q, :], s[:, q, :], ALU.mult).then_inc(product, 1)

            @block.scalar
            def _(act):
                def silu(c):
                    act.wait_ge(got[c], 16)
                    nc.scalar.activation(g[:, c * CT:(c + 1) * CT, :], g[:, c * CT:(c + 1) * CT, :],
                                         ACT.Silu).then_inc(gated, 1)

                for c in range(CHUNKS):
                    silu(c)
                for c in range(CHUNKS):
                    norm.scalar(act, c, x[:, c * CT:(c + 1) * CT, :], t["eps"][:])
                    for q in range(4 * c, 4 * c + 4):
                        act.wait_ge(tr_done, q + 1)
                        if q >= 4:
                            act.wait_ge(xnT_out[q % 4], 16 * (q // 4))
                        nc.scalar.activation(xnT[:, q % 4, :], ps[:, q % 4, :], ACT.Copy).then_inc(xnT_ready, 1)

            @block.tensor
            def _(pe):
                for q in range(GROUPS):
                    pe.wait_ge(xn_ready, q // 4 + 1)
                    if q >= 4:
                        pe.wait_ge(xnT_ready, q - 3)
                    for i in range(4):
                        last = nc.tensor.transpose(ps[:, q % 4, i * P:(i + 1) * P], xn[:, 4 * q + i, :], t["ident"][:])
                    last.then_inc(tr_done, 1)

            @block.sync
            def _(sp):
                for c in range(CHUNKS):
                    sp.dma_start(g[:, c * CT:(c + 1) * CT, :],
                                 d["outs0"][0:TOKENS, :].rearrange("(t p) d -> p t d", p=P)[:, c * CT:(c + 1) * CT, :])\
                      .then_inc(got[c], 16)
                for q in range(GROUPS):
                    sp.wait_ge(xnT_ready, q + 1)
                    sp.dma_start(d["xnT"][:, q * 512:(q + 1) * 512], xnT[:, q % 4, :]).then_inc(xnT_out[q % 4], 16)
                    if q % 4 == 3:
                        sp.dma_start(d["x_rows"].rearrange("(t p) d -> p t d", p=P)[:, 4 * q - 12:4 * q + 4, :],
                                     x[:, 4 * q - 12:4 * q + 4, :]).then_inc(x_out, 16)
                for i in range(4):
                    sp.wait_ge(xnT_out[i], 16 * GROUPS // 4)
                sp.wait_ge(x_out, 16 * CHUNKS)

            @block.vector
            def _(dve):
                link = Chain(dve, dve_step)
                part = lambda a, c: a[:, c * CT:(c + 1) * CT, :]

                def join(c):
                    dve.wait_ge(product, c + 1)
                    link(nc.vector.tensor_tensor(part(x, c), part(x, c), part(g, c), ALU.add))
                    norm.begin(link, c, part(x, c))

                join(0)
                for c in range(CHUNKS):
                    if c + 1 < CHUNKS:
                        join(c + 1)
                    norm.finish(link, c, part(x, c), part(xn, c), xn_ready)


HEADS_B, DH_B = 16, 8
PAIRS = ((0, 0), (0, 1), (1, 0), (1, 1), (0, 2), (2, 0))
M_ROW = 65
STACK = M_ROW + 3


def pipelined(eng, count, step):
    step(0, 0, 2)
    step(1, 1, 2)
    with eng.Fori(1, count // 2 - 1) as i:
        step(2 * i, 0, 2)
        step(2 * i + 1, 1, 2)
    step(count - 2, 0, 1)
    step(count - 1, 1, 0)


def by_fours(eng, count, step, last=4):
    for m in range(4):
        step(m, m)
    with eng.Fori(1, (count - last) // 4) as i:
        for j in range(4):
            step(4 * i + j, j)
    for m in range(count - last, count):
        step(m, m % 4)


PAIR_OF_ONES = 1.0 + 0x3F80 / 2 ** 23


def small_attention(nc, t, d):
    with ExitStack() as ctx:
        def sb(name, shape, dt):
            return ctx.enter_context(nc.sbuf_tensor("f_" + name, shape, dt))

        def pb(name, shape, dt):
            return ctx.enter_context(nc.psum_tensor("f_" + name, shape, dt))

        def sem(name):
            return ctx.enter_context(semaphore(nc, t, "f_" + name))

        def many(n, make, name, *more):
            return [make(f"{name}{b}", *more) for b in range(n)]

        H, T, N = HEADS_B, SEQ, BATCH
        wq, wk, wv, wo = (sb(n, [P, D], F32) for n in ("wq", "wk", "wv", "wo"))
        bq, bk = sb("bq", [P, 1], F32), sb("bk", [P, 1], F32)
        bv, bo = sb("bv", [P, D], F32), sb("bo", [P, D], F32)
        slab = many(4, sb, "slab", [P, T], F32)
        qk = many(2, sb, "qk", [P, 2, T], F32)
        rest = sb("rest", [P, 2, T], F32)
        parts = many(2, sb, "parts", [P, 3, 2, T], BF16)
        qs, ks = many(4, sb, "qs", [STACK, H, T], BF16), many(4, sb, "ks", [STACK, H, T], BF16)
        v = many(2, sb, "v", [P, 2, H, 32], F32)
        nmax = many(2, sb, "nmax", [P, 2, H], F32)
        mrest = sb("mrest", [P, 2, H], F32)
        mparts = many(2, sb, "mparts", [P, 2, 3, H], BF16)
        mT = many(4, sb, "mT", [3 * H, T], BF16)
        prob = many(2, sb, "prob", [P, 4, 2 * T], F32)
        o = many(2, sb, "o", [P, 4, T], F32)
        rec = sb("rec", [P, 2, H], F32)
        on = sb("on", [P, 2, D], F32)
        onT = sb("onT", [P, T], F32)
        ps_s, ps_t = (many(2, pb, n, [P, 2 * T], F32) for n in ("ps_s", "ps_t"))
        ps_o = many(2, pb, "ps_o", [P, 512], F32)
        ps_q, ps_m = pb("ps_q", [P, 512], F32), pb("ps_m", [P, 512], F32)

        w_in, filled, bq_scaled, v_zeroed = sem("w_in"), sem("filled"), sem("bq_scaled"), sem("v_zeroed")
        ones_filled = sem("ones_filled")
        slab_in, stack_in, max_in = (many(4, sem, n) for n in ("slab_in", "stack_in", "max_in"))
        qk_done, qk_ready, v_done, v_ready = sem("qk_done"), sem("qk_ready"), sem("v_done"), sem("v_ready")
        part0, rest1, part1, parts_ready = sem("part0"), sem("rest1"), sem("part1"), sem("parts_ready")
        mpart0, mrest1, mpart1, mparts_ready = sem("mpart0"), sem("mrest1"), sem("mpart1"), sem("mparts_ready")
        s_done, max_done, mT_done, mT_ready = sem("s_done"), sem("max_done"), sem("mT_done"), sem("mT_ready")
        st_done, exp_done, o_done, o_ready = sem("st_done"), sem("exp_done"), sem("o_done"), sem("o_ready")
        oT_done, rec_done, on_ready = sem("oT_done"), sem("rec_done"), sem("on_ready")
        back_done, onT_ready, z_done, z_ready = sem("back_done"), sem("onT_ready"), sem("z_done"), sem("z_ready")
        STACKED = 16 * 2 * len(PAIRS)
        W_ALL, FILLS = 16 * 8, 3 * 4 + 2

        def exists(m):
            return not isinstance(m, int) or 0 <= m < N

        def in_pairs(rows):
            return rows.rearrange("p h t -> p (h t)").bitcast(F32)

        def rounds(eng, step):
            by_fours(eng, N, step)
            for m in (N, N + 1):
                step(m, m % 4)

        def stages(m, j):
            return lambda k: (m + k, (j + k) % 4)

        with nc.Block() as block:

            @block.sync
            def _(sp):
                def load(q, j):
                    wait(sp, v_done, q - 3)
                    sp.dma_start(slab[j][:], d["xnT"][:, bass.ds(q * T, T)]).then_inc(slab_in[j], 16)

                def stack(q, j):
                    sp.wait_ge(parts_ready, q + 1)
                    for s_, pair in enumerate(PAIRS):
                        for z, (dst, part) in enumerate(zip((qs[j], ks[j]), pair)):
                            sp.dma_start(dst[8 * s_:8 * s_ + 8, :, :], parts[j % 2][:, part, z, :])\
                              .then_inc(stack_in[j], 16)

                def maxima(q, j):
                    sp.wait_ge(mT_ready, q + 1)
                    sp.dma_start(qs[j][M_ROW:STACK, :, :], mT[j][:]).then_inc(max_in[j], 16)

                for w, n in ((wq, "Wq"), (wk, "Wk"), (wv, "Wv"), (bq, "bq"), (bk, "bk"), (wo, "Wo")):
                    sp.dma_start(w[:], d["f_" + n]).then_inc(w_in, 16)
                for w, n in ((bv, "bv"), (bo, "bo")):
                    sp.dma_start(w[:], d["f_" + n].to_broadcast([P, D])).then_inc(w_in, 16)
                for q in range(4):
                    load(q, q)
                sp.wait_ge(filled, FILLS)
                sp.wait_ge(ones_filled, 4)
                for q in range(4):
                    stack(q, q)
                maxima(0, 0)
                load(4, 0)

                def step(m, j):
                    if exists(m + 1):
                        maxima(m + 1, (j + 1) % 4)
                    if exists(m + 5):
                        load(m + 5, (j + 1) % 4)
                    elif exists(m + 4):
                        sp.wait_ge(v_done, m + 2)
                    if exists(m + 4):
                        stack(m + 4, j)

                by_fours(sp, N, step, 8)

            @block.gpsimd
            def _(pool):
                for m in ks:
                    nc.gpsimd.memset(in_pairs(m[64:STACK, :, :]), PAIR_OF_ONES).then_inc(ones_filled, 1)
                pool.wait_ge(ones_filled, 4)
                def split(q, j):
                    whole, part = qk[j % 2], parts[j % 2]
                    pool.wait_ge(part0, q + 1)
                    wait(pool, parts_ready, q)
                    nc.gpsimd.tensor_tensor(rest[:], whole[:], part[:, 0, :, :], ALU.subtract).then_inc(rest1, 1)
                    nc.gpsimd.tensor_tensor(part[:, 1, :, :], whole[:], part[:, 0, :, :], ALU.subtract)\
                        .then_inc(part1, 1)
                    pool.wait_ge(rest1, q + 1)
                    pool.wait_ge(part1, q + 1)
                    nc.gpsimd.tensor_tensor(part[:, 2, :, :], rest[:], part[:, 1, :, :], ALU.subtract)\
                        .then_inc(parts_ready, 1)

                def split_max(q, j):
                    whole, part = nmax[j % 2], mparts[j % 2]
                    pool.wait_ge(mpart0, q + 1)
                    wait(pool, mparts_ready, q)
                    nc.gpsimd.tensor_tensor(mrest[:], whole[:], part[:, :, 0, :], ALU.subtract).then_inc(mrest1, 1)
                    nc.gpsimd.tensor_tensor(part[:, :, 1, :], whole[:], part[:, :, 0, :], ALU.subtract)\
                        .then_inc(mpart1, 1)
                    pool.wait_ge(mrest1, q + 1)
                    pool.wait_ge(mpart1, q + 1)
                    nc.gpsimd.tensor_tensor(part[:, :, 2, :], mrest[:], part[:, :, 1, :], ALU.subtract)\
                        .then_inc(mparts_ready, 1)

                for q in range(4):
                    split(q, q)
                split_max(0, 0)

                def step(m, j):
                    if exists(m + 1):
                        split_max(m + 1, (j + 1) % 4)
                    if exists(m + 4):
                        split(m + 4, j)

                by_fours(pool, N, step)

            @block.scalar
            def _(act):
                def project(q, j):
                    act.wait_ge(qk_done, q + 1)
                    wait(act, parts_ready, q - 1)
                    nc.scalar.activation(qk[j % 2][:, 0, :], ps_q[:, 0:T], ACT.Identity, bias=bq[:, 0:1],
                                         scale=DH_B ** -0.5)
                    nc.scalar.activation(qk[j % 2][:, 1, :], ps_q[:, T:2 * T], ACT.Identity,
                                         bias=bk[:, 0:1]).then_inc(qk_ready, 1)

                def exp(m, g, k):
                    h = 4 * g + k
                    act.wait_ge(st_done, H * m + h + 1)
                    if k == 0:
                        wait(act, o_done, 4 * m + g - 1)
                    nc.scalar.activation(prob[g % 2][:, k, :], ps_t[h % 2][:], ACT.Exp).then_inc(exp_done, 1)

                def take(m, j, half):
                    act.wait_ge(o_done, 4 * m + 2 * half + 2)
                    wait(act, oT_done, 2 * (m - 1))
                    nc.scalar.activation(o[j % 2][:, 2 * half:2 * half + 2, :].rearrange("p g t -> p (g t)"), ps_o[half][:],
                                         ACT.Copy).then_inc(o_ready, 1)

                def turned(q, j):
                    act.wait_ge(mT_done, q + 1)
                    if exists(q - 4):
                        loaded(act, max_in, q - 4, j)
                    nc.scalar.activation(mT[j][:], ps_m[0:3 * H, 0:T], ACT.Copy).then_inc(mT_ready, 1)

                def back(m):
                    act.wait_ge(back_done, m + 1)
                    wait(act, z_done, m)
                    nc.scalar.activation(onT[:], ps_m[:, 0:T], ACT.Copy).then_inc(onT_ready, 1)

                for m in ks[0:2]:
                    nc.scalar.activation(in_pairs(m[32:64, :, :]), t["zero_f"][32:64, 0:1].to_broadcast([32, H * T // 2]),
                                         ACT.Copy)\
                      .then_inc(filled, 1)
                act.wait_ge(w_in, W_ALL)
                nc.scalar.activation(bq[:], bq[:], ACT.Copy, scale=DH_B ** -0.5).then_inc(bq_scaled, 1)
                act.wait_ge(bq_scaled, 1)
                for q in range(4):
                    project(q, q)
                turned(0, 0)

                def step(m, j):
                    for g in range(4):
                        for k in range(4):
                            if exists(m):
                                exp(m, g, k)
                            if (g, k) == (0, 1) and exists(m - 2):
                                back(m - 2)
                            if (g, k) == (1, 0) and exists(m + 4):
                                project(m + 4, j)
                            if (g, k) == (1, 1) and exists(m - 1):
                                take(m - 1, j + 1, 1)
                            if (g, k) == (2, 1) and exists(m + 1):
                                turned(m + 1, (j + 1) % 4)
                            if (g, k) == (3, 1) and exists(m):
                                take(m, j, 0)

                rounds(act, step)

            @block.vector
            def _(dve):
                def values(q, j):
                    dve.wait_ge(v_done, q + 1)
                    wait(dve, o_done, 4 * (q - 1))
                    for r in range(2):
                        last = nc.vector.tensor_tensor(v[j % 2][:, r, :, 0:8],
                                                       ps_q[:, r * D:(r + 1) * D].rearrange("p (h c) -> p h c", c=8),
                                                       bv[:].rearrange("p (h c) -> p h c", c=8), ALU.add)
                    last.then_inc(v_ready, 1)

                def first_part(q, j):
                    dve.wait_ge(qk_ready, q + 1)
                    if exists(q - 2):
                        loaded(dve, stack_in, q - 2, (j + 2) % 4, STACKED)
                    nc.vector.tensor_copy(parts[j % 2][:, 0, :, :], qk[j % 2][:]).then_inc(part0, 1)

                def first_max_part(q, j):
                    dve.wait_ge(max_done, H * (q + 1))
                    wait(dve, mT_done, q - 1)
                    nc.vector.tensor_copy(mparts[j % 2][:, :, 0, :], nmax[j % 2][:]).then_inc(mpart0, 1)

                def maximum(q, j, h):
                    dve.wait_ge(s_done, H * q + h + 1)
                    if h == 0:
                        wait(dve, mparts_ready, q - 1)
                    nc.vector.tensor_reduce(nmax[j % 2][:, :, h], ps_s[h % 2][:].rearrange("p (r k) -> p r k", r=2),
                                            AX_X, ALU.max, negate=True).then_inc(max_done, 1)

                def divide(m, r):
                    rows = ps_q[:].rearrange("p (h c) -> p h c", c=32)
                    dve.wait_ge(oT_done, 2 * m + r + 1)
                    wait(dve, on_ready, 2 * m + r - 1)
                    nc.vector.reciprocal(rec[:, r, :], rows[:, :, 8]).then_inc(rec_done, 1)
                    dve.wait_ge(rec_done, 2 * m + r + 1)
                    wait(dve, back_done, m)
                    nc.vector.tensor_tensor(on[:, r, :].rearrange("p (h c) -> p h c", c=8), rows[:, :, 0:8],
                                            over(rec[:, r, :], 8, 2), ALU.mult).then_inc(on_ready, 1)

                def output(m):
                    dve.wait_ge(z_done, m + 1)
                    nc.vector.tensor_tensor(t["s"][:, bass.ds(2 * m, 2), :],
                                            ps_m[:, 0:2 * D].rearrange("p (r c) -> p r c", c=D),
                                            over(bo[:], 2, 1), ALU.add).then_inc(z_ready, 1)

                for m in v:
                    nc.vector.memset(m[:], 0.0).then_inc(v_zeroed, 1)
                dve.wait_ge(v_zeroed, 2)
                for m in v:
                    nc.vector.memset(m[:, :, :, 8:9], 1.0).then_inc(filled, 1)
                for m in [m[32:64, :, :] for m in (*qs, *ks[2:4])] + [m[64:M_ROW, :, :] for m in qs]:
                    nc.vector.memset(in_pairs(m), 0.0).then_inc(filled, 1)
                dve.wait_ge(w_in, W_ALL)
                for q in range(4):
                    first_part(q, q)
                values(0, 0)
                for q in range(2):
                    for h in range(H):
                        maximum(q, q, h)
                    if q == 0:
                        first_max_part(0, 0)

                def step(m, j):
                    near = stages(m, j)
                    for g in range(4):
                        for k in range(4):
                            if exists(m + 2):
                                maximum(*near(2), 4 * g + k)
                            if (g, k) == (0, 0) and exists(m + 1):
                                first_max_part(*near(1))
                            if (g, k) == (1, 2) and exists(m + 4):
                                first_part(*near(4))
                            if (g, k) == (1, 3) and exists(m - 2):
                                output(m - 2)
                            if g in (2, 3) and k == 1 and exists(m - 1):
                                divide(m - 1, g - 2)
                    if exists(m + 1):
                        values(*near(1))

                rounds(dve, step)

            @block.tensor
            def _(pe):
                def project(q, j):
                    loaded(pe, slab_in, q, j)
                    nc.tensor.matmul(ps_q[:, 0:T], wq[:], slab[j][:], start=True, stop=True)
                    nc.tensor.matmul(ps_q[:, T:2 * T], wk[:], slab[j][:], start=True, stop=True).then_inc(qk_done, 1)

                def values(q, j):
                    for r in range(2):
                        last = nc.tensor.matmul(ps_q[:, r * D:(r + 1) * D], slab[j][:, r * P:(r + 1) * P], wv[:],
                                                start=True, stop=True)
                    last.then_inc(v_done, 1)

                def by_queries(q, j, h):
                    if h == 0:
                        loaded(pe, stack_in, q, j, STACKED)
                    wait(pe, max_done, H * q + h - 1)
                    for r in range(2):
                        last = nc.tensor.matmul(ps_s[h % 2][:, r * T:(r + 1) * T], qs[j][0:M_ROW, h, r * P:(r + 1) * P],
                                                ks[j][0:M_ROW, h, :], start=True, stop=True)
                    last.then_inc(s_done, 1)

                def by_keys(m, j, h):
                    if h == 0:
                        loaded(pe, max_in, m, j)
                    wait(pe, exp_done, H * m + h - 1)
                    for r in range(2):
                        last = nc.tensor.matmul(ps_t[h % 2][:, r * T:(r + 1) * T], ks[j][:, h, r * P:(r + 1) * P],
                                                qs[j][:, h, :], start=True, stop=True)
                    last.then_inc(st_done, 1)

                def weigh(m, j, g, r):
                    if r == 0:
                        pe.wait_ge(exp_done, H * m + 4 * g + 4)
                        if g == 0:
                            pe.wait_ge(v_ready, m + 1)
                        if g % 2 == 0:
                            wait(pe, o_ready, 2 * m - 1 + g // 2)
                    first = (g % 2) * T
                    for k in range(4):
                        last = nc.tensor.matmul(ps_o[g // 2][32 * k:32 * k + 32, first:first + T],
                                                v[j % 2][:, r, 4 * g + k, :],
                                                prob[g % 2][:, k, r * T:(r + 1) * T], start=(r == 0), stop=(r == 1))
                    if r == 1:
                        last.then_inc(o_done, 1)

                def turn_o(m, j, r):
                    pe.wait_ge(o_ready, 2 * m + 2)
                    if r == 1:
                        pe.wait_ge(on_ready, 2 * m + 1)
                    elif exists(m + 5):
                        pe.wait_ge(qk_ready, m + 6)
                    elif exists(m + 1):
                        pe.wait_ge(v_ready, m + 2)
                    else:
                        pe.wait_ge(on_ready, 2 * m)
                    for g in range(4):
                        last = nc.tensor.transpose(ps_q[:, g * P:(g + 1) * P], o[j % 2][:, g, r * P:(r + 1) * P],
                                                   t["ident"][:])
                    last.then_inc(oT_done, 1)

                def turn_max(q, j):
                    pe.wait_ge(mparts_ready, q + 1)
                    if exists(q - 3):
                        pe.wait_ge(z_ready, q - 2)
                    else:
                        wait(pe, mT_ready, q)
                    for r in range(2):
                        last = nc.tensor.matmul(ps_m[0:3 * H, r * P:(r + 1) * P],
                                                mparts[j % 2][:, r, :, :].rearrange("p a h -> p (a h)"),
                                                t["ident_b"][:], start=True, stop=True)
                    last.then_inc(mT_done, 1)

                def turn_back(m):
                    pe.wait_ge(on_ready, 2 * m + 2)
                    if exists(m + 2):
                        pe.wait_ge(mT_ready, m + 3)
                    else:
                        wait(pe, z_ready, m)
                    for r in range(2):
                        last = nc.tensor.transpose(ps_m[:, r * P:(r + 1) * P], on[:, r, :], t["ident"][:])
                    last.then_inc(back_done, 1)

                def project_out(m):
                    pe.wait_ge(onT_ready, m + 1)
                    for r in range(2):
                        last = nc.tensor.matmul(ps_m[:, r * D:(r + 1) * D], onT[:, r * P:(r + 1) * P], wo[:],
                                                start=True, stop=True)
                    last.then_inc(z_done, 1)

                pe.wait_ge(w_in, W_ALL)
                for q in range(4):
                    wait(pe, qk_ready, q)
                    project(q, q)
                pe.wait_ge(qk_ready, 4)
                values(0, 0)
                pe.wait_ge(filled, FILLS)
                pe.wait_ge(ones_filled, 4)
                for q in range(2):
                    for h in range(H):
                        by_queries(q, q, h)
                    if q == 0:
                        turn_max(0, 0)

                def between(m, j, g, k):
                    near = stages(m, j)
                    if (g, k) == (0, 0) and exists(m - 2):
                        turn_back(m - 2)
                    if (g, k) == (1, 0) and exists(m - 2):
                        project_out(m - 2)
                    if (g, k) == (2, 0) and exists(m + 1):
                        turn_max(*near(1))
                    if k >= 2:
                        weighed = (*near(0), g - 1) if g else (*near(-1), 3)
                        if exists(weighed[0]):
                            weigh(*weighed, k - 2)
                    if (g, k) == (0, 3) and exists(m + 4):
                        pe.wait_ge(v_ready, m + 1)
                        project(*near(4))
                    if k == 3 and g in (1, 2) and exists(m - 1):
                        turn_o(*near(-1), g - 1)
                    if (g, k) == (3, 3) and exists(m + 1):
                        if exists(m - 1):
                            pe.wait_ge(on_ready, 2 * m)
                        else:
                            pe.wait_ge(qk_ready, m + 5)
                        values(*near(1))

                def step(m, j):
                    near = stages(m, j)
                    for g in range(4):
                        for k in range(4):
                            if exists(m):
                                by_keys(m, j, 4 * g + k)
                            if exists(m + 2):
                                by_queries(*near(2), 4 * g + k)
                            between(m, j, g, k)

                rounds(pe, step)


HEADS_A, DH_A = 16, 64
PAIRS_A = HEADS_A // 2
QKV = HEADS_A * DH_A
SCALE_A = DH_A ** -0.5


def layer1_route(nc, t, d, a):
    with ExitStack() as ctx:
        def sb(name, shape, dt):
            return ctx.enter_context(nc.sbuf_tensor(name, shape, dt))

        def pb(name, shape, dt):
            return ctx.enter_context(nc.psum_tensor(name, shape, dt))

        def sem(name):
            return ctx.enter_context(semaphore(nc, t, "r1_" + name))

        xn, s = t["xn"], t["s"]
        g1, b1 = sb("ln1_g", [P, D], F32), sb("ln1_b", [P, D], F32)
        gw, gb = sb("gw1", [P, P], F32), sb("gb1", [P, EXPERTS], F32)
        xT = sb("x1T", [P, 2, 512], F32)
        prob = sb("prob1", [P, TILES, EXPERTS], F32)
        best, total = sb("best1", [P, TILES], F32), sb("total1s", [P, TILES], F32)
        norm = Norm(nc, sem, sb, "n2")
        ps = pb("ps_x1", [P, 2, 512], F32)
        n_tiles = expert_tiles(2 * TOKENS)
        r = route_buffers(sb, pb, 2, n_tiles, dict(slot=t["slot1"], expert=t["expert1"]), "1")
        ps_g = pb("ps_g1", [P, 2, 512], F32)

        w_in, w_zero, x1_ready, x1_out = sem("w_in"), sem("w_zero"), sem("x1_ready"), sem("x1_out")
        tr_done, xT_ready, g_done, g_ready = sem("tr_done"), sem("xT_ready"), sem("g_done"), sem("g_ready")
        shifted, exp_ready = sem("shifted"), sem("exp_ready")
        shifted_x, normed = sem("shifted_x"), sem("normed")
        a_in, w_hi_ready = sem("a_in"), sem("w_hi_ready")
        chosen_ready, counted, routed = sem("chosen"), sem("counted"), sem("routed")
        dve_step = sem("dve_step")
        GROUPS = TILES // 4

        with nc.Block() as block:

            @block.sync
            def _(sp):
                sp.wait_ge(w_zero, 1)
                sp.dma_start(gw[:, 0:EXPERTS], d["gate1"]).then_inc(w_in, 16)
                for m, n in ((gb, "gate1_b"), (g1, "ln1_g"), (b1, "ln1_b")):
                    sp.dma_start(m[:], d[n].to_broadcast([P, m.shape[1]])).then_inc(w_in, 16)
                for n in ("w", "wo", "bq", "bk"):
                    sp.dma_start(a[n][:], d["a_" + n]).then_inc(a_in, 16)
                for n, source in (("bv", "a_bv"), ("bo", "a_bo"), ("ghost", "ghost")):
                    sp.dma_start(a[n][:], d[source].to_broadcast([P, a[n].shape[1]])).then_inc(a_in, 16)
                for c in range(CHUNKS):
                    sp.wait_ge(x1_ready, c + 1)
                    sp.dma_start(d["x1_rows"].rearrange("(t p) d -> p t d", p=P)[:, c * CT:(c + 1) * CT, :],
                                 xn[:, c * CT:(c + 1) * CT, :]).then_inc(x1_out, 16)
                sp.wait_ge(x1_out, 16 * CHUNKS)

            @block.gpsimd
            def _(pool):
                nc.gpsimd.memset(gw[:], 0.0).then_inc(w_zero, 1)
                pool.wait_ge(w_in, 64)
                for c in range(CHUNKS):
                    q = slice(c * CT, (c + 1) * CT)
                    nc.gpsimd.tensor_tensor(xn[:, q, :], xn[:, q, :], over(b1[:], CT, 1), ALU.add)\
                        .then_inc(shifted_x, 1)
                pool.wait_ge(w_hi_ready, 1)
                nc.gpsimd.tensor_tensor(a["w_lo"][:], a["w"][:], a["w_hi"][:], ALU.subtract)

            @block.scalar
            def _(act):
                for c in range(CHUNKS):
                    norm.scalar(act, c, s[:, c * CT:(c + 1) * CT, :], t["eps"][:])
                    for q in range(4 * c, 4 * c + 4):
                        act.wait_ge(tr_done, q + 1)
                        if q >= 2:
                            act.wait_ge(g_done, q - 1)
                        nc.scalar.activation(xT[:, q % 2, :], ps[:, q % 2, :], ACT.Copy).then_inc(xT_ready, 1)
                act.wait_ge(a_in, 16 * 7)
                nc.scalar.activation(a["w_hi"][:], a["w"][:], ACT.Copy).then_inc(w_hi_ready, 1)
                nc.scalar.activation(a["bq_s"][:], a["bq"][:], ACT.Copy, scale=SCALE_A)
                act.wait_ge(shifted, 1)
                nc.scalar.activation(prob[:], prob[:], ACT.Exp).then_inc(exp_ready, 1)

            @block.tensor
            def _(pe):
                pe.wait_ge(w_in, 64)
                pe.wait_ge(w_zero, 1)

                def gate(q):
                    pe.wait_ge(xT_ready, q + 1)
                    if q >= 2:
                        pe.wait_ge(g_ready, q - 1)
                    for i in range(4):
                        last = nc.tensor.matmul(ps_g[:, q % 2, i * P:(i + 1) * P], xT[:, q % 2, i * P:(i + 1) * P],
                                                gw[:], start=True, stop=True)
                    last.then_inc(g_done, 1)

                for q in range(GROUPS):
                    pe.wait_ge(x1_ready, q // 4 + 1)
                    if q >= 2:
                        pe.wait_ge(xT_ready, q - 1)
                    for i in range(4):
                        last = nc.tensor.transpose(ps[:, q % 2, i * P:(i + 1) * P], xn[:, 4 * q + i, :], t["ident"][:])
                    last.then_inc(tr_done, 1)
                    if q:
                        gate(q - 1)
                gate(GROUPS - 1)
                pe.wait_ge(chosen_ready, 1)
                route_counts(nc, pe, t, r, 2, counted)

            @block.vector
            def _(dve):
                link = Chain(dve, dve_step)
                dve.wait_ge(w_in, 64)

                def logits(q):
                    dve.wait_ge(g_done, q + 1)
                    nc.vector.tensor_tensor(prob[:, 4 * q:4 * q + 4, :],
                                            ps_g[:, q % 2, :].rearrange("p (i d) -> p i d", d=P)[:, :, 0:EXPERTS],
                                            over(gb[:], 4, 1), ALU.add).then_inc(g_ready, 1)

                norm.begin(link, 0, s[:, 0:CT, :])
                for c in range(CHUNKS):
                    q = slice(c * CT, (c + 1) * CT)
                    if c + 1 < CHUNKS:
                        norm.begin(link, c + 1, s[:, (c + 1) * CT:(c + 2) * CT, :])
                    norm.finish(link, c, s[:, q, :], s[:, q, :], normed)
                    dve.wait_ge(normed, c + 1)
                    link(nc.vector.tensor_tensor(s[:, q, :], s[:, q, :], over(g1[:], CT, 1), ALU.mult))
                    dve.wait_ge(shifted_x, c + 1)
                    nc.vector.tensor_tensor(xn[:, q, :], xn[:, q, :], s[:, q, :], ALU.add).then_inc(x1_ready, 1)
                    if c:
                        for g in range(4 * c - 4, 4 * c):
                            logits(g)
                for g in range(GROUPS - 4, GROUPS):
                    logits(g)
                dve.wait_ge(g_ready, GROUPS)
                link(nc.vector.tensor_reduce(best[:], prob[:], AX_X, ALU.max))
                nc.vector.tensor_tensor(prob[:], prob[:], over(best[:], EXPERTS, 2), ALU.subtract).then_inc(shifted, 1)
                dve.wait_ge(exp_ready, 1)
                link(nc.vector.tensor_reduce(total[:], prob[:], AX_X, ALU.add))
                link(nc.vector.reciprocal(total[:], total[:]))
                link(nc.vector.tensor_tensor(prob[:], prob[:], over(total[:], EXPERTS, 2), ALU.mult))
                first, second = r["chosen"][:, 0:TILES, :], r["chosen"][:, TILES:2 * TILES, :]
                work = r["total"][:, 0:TILES, :]
                first_of(nc, link, first, prob[:], best[:], work, t["rank8"][:], TILES)
                link(nc.vector.tensor_tensor(work, prob[:], first, ALU.mult))
                link(nc.vector.tensor_reduce(t["weight1"][:, 0:TILES], work, AX_X, ALU.add))
                rest = r["total"][:, TILES:2 * TILES, :]
                link(nc.vector.scalar_tensor_tensor(rest, first, -2.0, prob[:], ALU.mult, ALU.add))
                first_of(nc, link, second, rest, best[:], work, t["rank8"][:], TILES, chosen_ready)
                link(nc.vector.tensor_tensor(work, prob[:], second, ALU.mult))
                link(nc.vector.tensor_reduce(t["weight1"][:, TILES:2 * TILES], work, AX_X, ALU.add))
                route(nc, dve, link, t, r, 2, n_tiles, counted, routed)




def causal_weights(sb):
    return dict(
        w=sb("a_w", [P, 3 * QKV], F32), w_hi=sb("a_w_hi", [P, 3 * QKV], F32R), w_lo=sb("a_w_lo", [P, 3 * QKV], F32R),
        wo=sb("a_wo", [P, PAIRS_A, D], F32), bq=sb("a_bq", [P, PAIRS_A], F32), bq_s=sb("a_bq_s", [P, PAIRS_A], F32),
        bk=sb("a_bk", [P, PAIRS_A], F32), bv=sb("a_bv", [P, QKV], F32), bo=sb("a_bo", [P, D], F32),
        ghost=sb("a_ghost", [P, HEADS_A], F32))


def causal_attention(nc, t, d, c):
    with ExitStack() as ctx:
        def sb(name, shape, dt):
            return ctx.enter_context(nc.sbuf_tensor("a_" + name, shape, dt))

        def pb(name, shape, dt):
            return ctx.enter_context(nc.psum_tensor("a_" + name, shape, dt))

        def sem(name):
            return ctx.enter_context(semaphore(nc, t, "a_" + name))

        def many(n, make, name, *more):
            return [make(f"{name}{b}", *more) for b in range(n)]

        T, N, HP = SEQ, BATCH, PAIRS_A
        w_hi, w_lo, wo, bq_s, bk, bv, bo, ghost = (
            c[n] for n in ("w_hi", "w_lo", "wo", "bq_s", "bk", "bv", "bo", "ghost"))
        slab = many(2, sb, "slab", [P, T], F32)
        slab_hi, slab_lo = many(2, sb, "slab_hi", [P, T], F32R), many(2, sb, "slab_lo", [P, T], F32R)
        qT, kT = many(2, sb, "qT", [P, T], F32), many(2, sb, "kT", [P, T], F32)
        v = sb("v", [P, 2, QKV], F32)
        nmax, sums = many(2, sb, "nmax", [P, 2, 2], F32), many(2, sb, "sums", [P, 2, 2], F32)
        total, rec = sb("total", [P, 2, 2], F32), sb("rec", [P, 2, 2], F32)
        prob, probT = many(4, sb, "prob", [P, 2, 3 * P], F32), many(2, sb, "probT", [P, 2, 3 * P], F32)
        o = many(2, sb, "o", [P, HP, T], F32)
        ps_s = many(2, pb, "ps_s", [P, 2, 512], F32)
        ps_q, ps_t, ps_o = pb("ps_q", [P, 512], F32), pb("ps_t", [P, 2, 512], F32), pb("ps_o", [P, 512], F32)

        slab_in = many(2, sem, "slab_in")
        slab_hi_ready, slab_lo_ready = sem("slab_hi_ready"), sem("slab_lo_ready")
        qk_done, qk_ready = sem("qk_done"), sem("qk_ready")
        v_done, v_ready = sem("v_done"), sem("v_ready")
        s_done, max_ready, exp_ready = sem("s_done"), sem("max_ready"), sem("exp_ready")
        totalled, rec_ready, divided = sem("totalled"), sem("rec_ready"), sem("divided")
        t_done, o_done, o_ready = sem("t_done"), sem("o_done"), sem("o_ready")
        probT_act, probT_dve = sem("probT_act"), sem("probT_dve")
        z_done, z_ready, scattered, placed = sem("z_done"), sem("z_ready"), sem("scattered"), sem("placed")
        TURN, WEIGH, OUT = 2, 3, 4

        def exists(m):
            return not isinstance(m, int) or 0 <= m < N

        def ago(m, b, p, k):
            return (m, b, p - k) if p >= k else (m - 1, 1 - b, p - k + HP)

        def loop(eng, pair):
            def step(m, b, more):
                for p in range(HP):
                    pair(m, b, p)

            pipelined(eng, N, step)
            for p in range(OUT + 1):
                pair(N, 0, p)

        def chunk_at(m, b, p):
            if p in (2, 3):
                return m, b, p
            if p in (6, 7):
                return m + 1, 1 - b, p - 6
            return -1, 0, 0

        def slab_wait(eng, m, b):
            eng.wait_ge(slab_in[b], 16 * ((m - b) // 2 + 1) if isinstance(m, int) else 8 * (m - b) + 16)

        with nc.Block() as block:

            @block.sync
            def _(sp):
                def load(q, b):
                    wait(sp, slab_lo_ready, q - 1)
                    sp.dma_start(slab[b][:], d["xnT"][:, bass.ds(q * T, T)]).then_inc(slab_in[b], 16)

                load(0, 0)
                load(1, 1)

                def step(m, b, more):
                    if more >= 2:
                        load(m + 2, b)

                pipelined(sp, N, step)

            @block.gpsimd
            def _(pool):
                for a in range(2):
                    if a:
                        pool.wait_ge(scattered, 16 * TILES)
                        nc.gpsimd.iota(t["row"][:, :, PLACE].bitcast(I32), pattern=[[P, TILES]], base=TOKENS,
                                       channel_multiplier=1).then_inc(placed, 1)
                    nc.gpsimd.tensor_copy(t["row"][:, :, WEIGHT], t["weight1"][:, a * TILES:(a + 1) * TILES])\
                        .then_inc(placed, 1)
                    pool.wait_ge(placed, 1 + 2 * a)
                    for i in range(TILES):
                        slot = t["slot1"][:, a * TILES + i:a * TILES + i + 1]
                        pool.indirect_dma_start(d["rows1"], bass.IndirectOffsetOnAxis(slot, 0), t["row"][:, i, :], None)\
                            .then_inc(scattered, 16)
                pool.wait_ge(scattered, 32 * TILES)

            @block.scalar
            def _(act):
                def queries_keys(m, b, p):
                    act.wait_ge(qk_done, HP * m + p + 1)
                    wait(act, s_done, HP * m + p - 1)
                    nc.scalar.activation(qT[p % 2][:], ps_q[:, 0:T], ACT.Identity, bias=bq_s[:, p:p + 1], scale=SCALE_A)
                    nc.scalar.activation(kT[p % 2][:], ps_q[:, T:2 * T], ACT.Identity, bias=bk[:, p:p + 1])\
                      .then_inc(qk_ready, 1)

                def exps(m, b, p):
                    act.wait_ge(max_ready, HP * m + p + 1)
                    wait(act, t_done, HP * m + p - 3)
                    wait(act, totalled, HP * m + p - 1)
                    for h in range(2):
                        for q in range(2):
                            cols = slice(q * P, (2 * q + 1) * P)
                            last = nc.scalar.activation(prob[p % 4][:, h, cols], ps_s[p % 2][:, h, cols], ACT.Exp,
                                                        bias=nmax[p % 2][:, q, h:h + 1],
                                                        accum_out=sums[p % 2][:, q, h:h + 1])
                    last.then_inc(exp_ready, 1)

                def turned(m, b, p):
                    act.wait_ge(t_done, HP * m + p + 1)
                    wait(act, o_done, HP * m + p - 1)
                    nc.scalar.activation(probT[p % 2][:, 1, :], ps_t[:, 1, 0:3 * P], ACT.Copy).then_inc(probT_act, 1)

                def take(m, b, p):
                    act.wait_ge(o_done, HP * m + p + 1)
                    wait(act, z_done, m - 1)
                    nc.scalar.activation(o[b][:, p, :], ps_o[:, 0:T], ACT.Copy).then_inc(o_ready, 1)

                def high_part(m, b):
                    slab_wait(act, m, b)
                    wait(act, qk_done, HP * (m - 1))
                    nc.scalar.activation(slab_hi[b][:], slab[b][:], ACT.Copy).then_inc(slab_hi_ready, 1)

                high_part(0, 0)
                queries_keys(0, 0, 0)

                def pair(m, b, p):
                    after, old = (m, b, p + 1) if p + 1 < HP else (m + 1, 1 - b, 0), ago(m, b, p, WEIGH)
                    if exists(after[0]):
                        queries_keys(*after)
                    if exists(m):
                        exps(m, b, p)
                    turn = ago(m, b, p, TURN)
                    if exists(turn[0]):
                        turned(*turn)
                    if exists(old[0]):
                        take(*old)
                    if p == 3 and exists(m + 1):
                        high_part(m + 1, 1 - b)

                loop(act, pair)

            @block.vector
            def _(dve):
                def values(m, b, n):
                    dve.wait_ge(v_done, 4 * m + n + 1)
                    wait(dve, o_done, HP * (m - 1) + 4 * (n // 2 + 1))
                    half, r = n // 2, n % 2
                    cols = slice(half * 512, (half + 1) * 512)
                    nc.vector.tensor_tensor(v[:, r, cols], ps_q[:], bv[:, cols], ALU.add).then_inc(v_ready, 1)

                def maxima(m, b, p):
                    dve.wait_ge(s_done, HP * m + p + 1)
                    wait(dve, exp_ready, HP * m + p - 1)
                    for q in range(2):
                        last = nc.vector.tensor_reduce(nmax[p % 2][:, q, :], ps_s[p % 2][:, :, q * P:(2 * q + 1) * P],
                                                       AX_X, ALU.max, negate=True)
                    last.then_inc(max_ready, 1)

                def invert(m, b, p):
                    dve.wait_ge(exp_ready, HP * m + p + 1)
                    wait(dve, rec_ready, HP * m + p)
                    nc.vector.tensor_tensor(total[:], sums[p % 2][:], over(ghost[:, 2 * p:2 * p + 2], 2, 1),
                                            ALU.add).then_inc(totalled, 1)
                    dve.wait_ge(totalled, HP * m + p + 1)
                    wait(dve, divided, HP * m + p)
                    nc.vector.reciprocal(rec[:], total[:]).then_inc(rec_ready, 1)
                    dve.wait_ge(rec_ready, HP * m + p + 1)
                    for q in range(2):
                        cols = prob[p % 4][:, :, q * P:(2 * q + 1) * P]
                        last = nc.vector.tensor_tensor(cols, cols, over(rec[:, q, :], (q + 1) * P, 2), ALU.mult)
                    last.then_inc(divided, 1)

                def turned(m, b, p):
                    dve.wait_ge(t_done, HP * m + p + 1)
                    wait(dve, o_done, HP * m + p - 1)
                    nc.vector.tensor_copy(probT[p % 2][:, 0, :], ps_t[:, 0, 0:3 * P]).then_inc(probT_dve, 1)

                def output(m):
                    dve.wait_ge(z_done, m + 1)
                    nc.vector.tensor_tensor(t["s"][:, bass.ds(2 * m, 2), :],
                                            ps_q[:, 0:2 * D].rearrange("p (r c) -> p r c", c=D),
                                            over(bo[:], 2, 1), ALU.add).then_inc(z_ready, 1)

                def low_part(m, b):
                    dve.wait_ge(slab_hi_ready, m + 1)
                    nc.vector.tensor_tensor(slab_lo[b][:], slab[b][:], slab_hi[b][:], ALU.subtract)\
                        .then_inc(slab_lo_ready, 1)

                low_part(0, 0)
                for n in range(2):
                    values(0, 0, n)

                def pair(m, b, p):
                    turn, before = ago(m, b, p, TURN), ago(m, b, p, 1)
                    if exists(m):
                        maxima(m, b, p)
                    if exists(before[0]):
                        invert(*before)
                    if exists(turn[0]):
                        turned(*turn)
                    chunk = chunk_at(m, b, p)
                    if exists(chunk[0]):
                        values(*chunk)
                    if p == OUT and exists(m + 1):
                        low_part(m + 1, 1 - b)
                    if p == OUT and exists(m - 1):
                        output(m - 1)

                loop(dve, pair)

            @block.tensor
            def _(pe):
                def project(m, b, p):
                    for z in range(2):
                        cols = slice(z * QKV + p * P, z * QKV + (p + 1) * P)
                        last = three_passes(nc, ps_q[:, z * T:(z + 1) * T], w_hi[:, cols], w_lo[:, cols],
                                            slab_hi[b][:], slab_lo[b][:])
                    last.then_inc(qk_done, 1)

                def values(m, b, n):
                    half, r = n // 2, n % 2
                    rows, cols = slice(r * P, (r + 1) * P), slice(2 * QKV + half * 512, 2 * QKV + (half + 1) * 512)
                    three_passes(nc, ps_q[:], slab_hi[b][:, rows], slab_lo[b][:, rows], w_hi[:, cols], w_lo[:, cols])\
                        .then_inc(v_done, 1)

                def scores(m, b, p):
                    pe.wait_ge(qk_ready, HP * m + p + 1)
                    wait(pe, exp_ready, HP * m + p - 1)
                    out = ps_s[p % 2]
                    for q in range(2):
                        for h in range(2):
                            rows = slice(64 * h, 64 * h + 64)
                            nc.tensor.matmul(out[:, h, q * P:(2 * q + 1) * P], qT[p % 2][rows, q * P:(q + 1) * P],
                                             kT[p % 2][rows, 0:(q + 1) * P], start=True, stop=False)
                            last = nc.tensor.matmul(out[:, h, 2 * q * P:(2 * q + 1) * P], t["ident_b"][:],
                                                    t["future_q"][:], start=False, stop=True)
                    last.then_inc(s_done, 1)

                def turn(m, b, p):
                    pe.wait_ge(divided, HP * m + p + 1)
                    wait(pe, probT_act, HP * m + p)
                    wait(pe, probT_dve, HP * m + p)
                    for h in range(2):
                        for n in range(3):
                            cols = slice(n * P, (n + 1) * P)
                            last = nc.tensor.transpose(ps_t[:, h, cols], prob[p % 4][:, h, cols], t["ident"][:])
                    last.then_inc(t_done, 1)

                def weigh(m, b, p):
                    pe.wait_ge(probT_act, HP * m + p + 1)
                    pe.wait_ge(probT_dve, HP * m + p + 1)
                    if p % 4 == 0:
                        pe.wait_ge(v_ready, 4 * m + 2 + p // 2)
                    wait(pe, o_ready, HP * m + p)
                    for keys in range(2):
                        for h in range(2):
                            head = 2 * p + h
                            last = nc.tensor.matmul(ps_o[64 * h:64 * h + 64, keys * P:T],
                                                    v[:, keys, head * 64:(head + 1) * 64],
                                                    probT[p % 2][:, h, 2 * P:3 * P] if keys else probT[p % 2][:, h, 0:T],
                                                    start=(keys == 0), stop=(keys == 1))
                    last.then_inc(o_done, 1)

                def project_out(m, b):
                    pe.wait_ge(o_ready, HP * m + HP)
                    for r in range(2):
                        for p in range(HP):
                            last = nc.tensor.matmul(ps_q[:, r * D:(r + 1) * D], o[b][:, p, r * P:(r + 1) * P],
                                                    wo[:, p, :], start=(p == 0), stop=(p == HP - 1))
                    last.then_inc(z_done, 1)

                pe.wait_ge(slab_lo_ready, 1)
                project(0, 0, 0)
                for n in range(2):
                    if n == 0:
                        pe.wait_ge(qk_ready, 1)
                    else:
                        pe.wait_ge(v_ready, 1)
                    values(0, 0, n)

                def pair(m, b, p):
                    after, before = (m, b, p + 1) if p + 1 < HP else (m + 1, 1 - b, 0), ago(m, b, p, 1)
                    if exists(m):
                        scores(m, b, p)
                    if exists(after[0]):
                        made = chunk_at(*before)
                        if isinstance(m, int) and (m, p) == (0, 0):
                            made = (0, 0, 1)
                        if exists(made[0]):
                            pe.wait_ge(v_ready, 4 * made[0] + made[2] + 1)
                        if before[2] == OUT:
                            wait(pe, z_ready, m)
                        project(*after)
                    turned, weighed = ago(m, b, p, TURN), ago(m, b, p, WEIGH)
                    if exists(turned[0]):
                        turn(*turned)
                    if exists(weighed[0]):
                        weigh(*weighed)
                    chunk = chunk_at(m, b, p)
                    if exists(chunk[0]):
                        pe.wait_ge(qk_ready, HP * m + p + 2)
                        if p == 6:
                            pe.wait_ge(slab_lo_ready, m + 2)
                        values(*chunk)
                    if p == OUT and exists(m - 1):
                        if exists(after[0]):
                            pe.wait_ge(qk_ready, HP * m + p + 2)
                        project_out(m - 1, 1 - b)

                loop(pe, pair)


def layer1_join(nc, t, d):
    with ExitStack() as ctx:
        def sb(name, shape, dt):
            return ctx.enter_context(nc.sbuf_tensor(name, shape, dt))

        def sem(name):
            return ctx.enter_context(semaphore(nc, t, "j1_" + name))

        s = t["s"]
        x, x1 = sb("x_again", [P, TILES, D], F32), sb("x1_again", [P, 2, CT, D], F32)
        y = [sb(f"y_best{a}", [P, TILES, D], F32) for a in range(2)]
        g2, b2 = sb("ln2_g", [P, D], F32), sb("ln2_b", [P, D], F32)
        norm = Norm(nc, sem, sb, "n3")
        w_in, x_in, x1_in = sem("w_in"), [sem(f"x_in{c}") for c in range(CHUNKS)], [sem("x1_in0"), sem("x1_in1")]
        got = [sem(f"got{c}") for c in range(CHUNKS)]
        inner, gated, done, out_done = sem("inner"), sem("gated"), sem("done"), sem("out_done")
        dve_step, shifted_x1, normed = sem("dve_step"), sem("shifted_x1"), sem("normed")
        product, done_last = sem("product"), sem("done_last")

        def rows(name, c):
            return d[name].rearrange("(t p) d -> p t d", p=P)[:, c * CT:(c + 1) * CT, :]

        with nc.Block() as block:

            @block.sync
            def _(sp):
                for m, n in ((g2, "ln2_g"), (b2, "ln2_b")):
                    sp.dma_start(m[:], d[n].to_broadcast([P, D])).then_inc(w_in, 16)
                for c in range(CHUNKS):
                    for a in range(2):
                        sp.dma_start(y[a][:, c * CT:(c + 1) * CT, :],
                                     d["outs1"][a * TOKENS:(a + 1) * TOKENS, :]
                                     .rearrange("(t p) d -> p t d", p=P)[:, c * CT:(c + 1) * CT, :])\
                          .then_inc(got[c], 16)
                    if c < 2:
                        sp.dma_start(x1[:, c % 2, :, :], rows("x1_rows", c)).then_inc(x1_in[c % 2], 16)
                for c in range(CHUNKS):
                    sp.dma_start(x[:, c * CT:(c + 1) * CT, :], rows("x_rows", c)).then_inc(x_in[c], 16)
                for c in range(2, CHUNKS):
                    sp.wait_ge(inner, c - 1)
                    sp.dma_start(x1[:, c % 2, :, :], rows("x1_rows", c)).then_inc(x1_in[c % 2], 16)
                for c in range(CHUNKS):
                    if c < CHUNKS - 1:
                        sp.wait_ge(done, c + 1)
                    else:
                        sp.wait_ge(done_last, 1)
                    sp.dma_start(rows("out", c), x[:, c * CT:(c + 1) * CT, :]).then_inc(out_done, 16)
                sp.wait_ge(out_done, 16 * CHUNKS)

            @block.gpsimd
            def _(pool):
                pool.wait_ge(w_in, 32)
                part = lambda a, c: a[:, c * CT:(c + 1) * CT, :]

                def last_sum(c):
                    pool.wait_ge(x_in[c], 16)
                    pool.wait_ge(product, c + 1)
                    nc.gpsimd.tensor_tensor(part(x, c), part(x, c), part(y[0], c), ALU.add).then_inc(done, 1)

                for c in range(CHUNKS):
                    pool.wait_ge(x1_in[c % 2], 16 * (c // 2 + 1))
                    nc.gpsimd.tensor_tensor(x1[:, c % 2, :, :], x1[:, c % 2, :, :], over(b2[:], CT, 1), ALU.add)\
                        .then_inc(shifted_x1, 1)
                    if c >= 2:
                        last_sum(c - 2)
                last_sum(CHUNKS - 2)

            @block.scalar
            def _(act):
                part = lambda c: y[0][:, c * CT:(c + 1) * CT, :]
                norm.scalar(act, 0, part(0), t["eps"][:])
                for c in range(CHUNKS):
                    if c + 1 < CHUNKS:
                        norm.scalar(act, c + 1, part(c + 1), t["eps"][:])
                    act.wait_ge(inner, c + 1)
                    nc.scalar.activation(part(c), part(c), ACT.Silu).then_inc(gated, 1)

            @block.vector
            def _(dve):
                link = Chain(dve, dve_step)
                dve.wait_ge(w_in, 32)
                part = lambda a, c: a[:, c * CT:(c + 1) * CT, :]

                def mix(c):
                    dve.wait_ge(got[c], 32)
                    link(nc.vector.tensor_tensor(part(y[0], c), part(y[0], c), part(y[1], c), ALU.add))
                    norm.begin(link, c, part(y[0], c))

                def gate(c):
                    dve.wait_ge(gated, c + 1)
                    nc.vector.tensor_tensor(part(y[0], c), part(y[0], c), part(s, c), ALU.mult).then_inc(product, 1)

                mix(0)
                for c in range(CHUNKS):
                    if c + 1 < CHUNKS:
                        mix(c + 1)
                    norm.finish(link, c, part(y[0], c), part(y[0], c), normed)
                    dve.wait_ge(normed, c + 1)
                    link(nc.vector.tensor_tensor(part(y[0], c), part(y[0], c), over(g2[:], CT, 1), ALU.mult))
                    dve.wait_ge(shifted_x1, c + 1)
                    nc.vector.tensor_tensor(part(y[0], c), part(y[0], c), x1[:, c % 2, :, :], ALU.add).then_inc(inner, 1)
                    if c:
                        gate(c - 1)
                gate(CHUNKS - 1)
                dve.wait_ge(product, CHUNKS)
                dve.wait_ge(x_in[CHUNKS - 1], 16)
                nc.vector.tensor_tensor(part(x, CHUNKS - 1), part(x, CHUNKS - 1), part(y[0], CHUNKS - 1),
                                        ALU.add).then_inc(done_last, 1)


def shared(sb):
    return dict(
        semaphores=[], ident=sb("ident", [P, P], F32), ident_b=sb("ident_b", [P, P], BF16), ones=sb("ones", [P, P], F32),
        before=sb("before", [P, P], F32), zero_b=sb("zero_b", [P, P], BF16),
        future_q=sb("future_q", [P, P], BF16), future_k=sb("future_k", [P, P], BF16),
        rank8=sb("rank8", [P, EXPERTS], F32), tile_no=sb("tile_no", [1, expert_tiles(2 * TOKENS)], F32),
        eps=sb("eps", [P, 1], F32), zero_i=sb("zero_i", [P, 2], I32), zero_f=sb("zero_f", [P, 1], F32),
        slot0=sb("slot0", [P, TILES], I32), expert0=sb("expert0", [1, expert_tiles(TOKENS)], I32),
        slot1=sb("slot1", [P, 2 * TILES], I32), expert1=sb("expert1", [1, expert_tiles(2 * TOKENS)], I32),
        weight1=sb("weight1", [P, 2 * TILES], F32), s=sb("s", [P, TILES, D], F32))


def program(nc, d):
    def dram(name, *shape):
        d[name] = nc.dram_tensor("scratch_" + name, shape, F32, kind="Internal").ap()

    for tag, rows in (("0", TOKENS), ("1", 2 * TOKENS)):
        slots = expert_tiles(rows) * SLOTS
        dram("rows" + tag, slots, ROW)
        dram("outs" + tag, rows + slots, D)
    dram("xnT", D, TOKENS)
    dram("x_rows", TOKENS, D)
    dram("x1_rows", TOKENS, D)
    with ExitStack() as ctx:
        def sb(name, shape, dt):
            return ctx.enter_context(nc.sbuf_tensor(name, shape, dt))

        t = shared(sb)
        constants(nc, t)
        with nc.sbuf_tensor("row", [P, TILES, ROW], F32) as row:
            t["row"], t["xn"] = row, row[:, :, 0:D]
            with nc.sbuf_tensor("x", [P, TILES, D], F32) as x:
                t["x"] = x
                layer0_front(nc, t, d)
                experts(nc, t, d, "0", expert_tiles(TOKENS), ACT.Relu, t["expert0"], False)
                layer0_join(nc, t, d)
                clear(nc, t)
            small_attention(nc, t, d)
            with ExitStack() as held:
                a = causal_weights(lambda name, shape, dt: held.enter_context(nc.sbuf_tensor(name, shape, dt)))
                layer1_route(nc, t, d, a)
                causal_attention(nc, t, d, a)
            clear(nc, t)
        experts(nc, t, d, "1", expert_tiles(2 * TOKENS), ACT.Gelu, t["expert1"], True)
        layer1_join(nc, t, d)


def layout(i):
    import numpy as np

    def experts_pack(w1T, w2T, b1, b2):
        e = w1T.shape[0]
        w2 = w2T.reshape(e, HC, P, D).transpose(0, 2, 1, 3).reshape(e, P, HC * D)
        return np.ascontiguousarray(np.concatenate(
            [w1T, w2, b1.reshape(e, HC, P).transpose(0, 2, 1), np.broadcast_to(b2[:, None, :], (e, P, D))], axis=2))

    def by_channel(a):
        return c(a.reshape(-1, HEADS_B, DH_B).transpose(0, 2, 1).reshape(a.shape[0], -1))

    c = np.ascontiguousarray
    return {
        "x": c(i["L0_attn_x"].reshape(TOKENS, D)),
        "A": c(i["L0_attn_A"]), "AT": c(i["L0_attn_A"].T), "BmT": c(i["L0_attn_Bm"].T),
        "CT": c(i["L0_attn_C"].T), "W_inT": c(i["L0_attn_W_in"].T), "b_in": c(i["L0_attn_b_in"].reshape(N_STATE, 1)),
        "D": c(i["L0_attn_D"].reshape(1, D)),
        "gate0T": c(i["L0_ffn_gate_w"].T), "gate0_b": c(i["L0_ffn_gate_b"].reshape(1, EXPERTS)),
        "w0": experts_pack(i["L0_ffn_w1"].transpose(0, 2, 1), i["L0_ffn_w2"].transpose(0, 2, 1), i["L0_ffn_b1"],
                           i["L0_ffn_b2"]),
        **{"f_" + n: by_channel(i["L1_ffn_" + n]) for n in ("Wq", "Wk")},
        **{"f_" + n: c(i["L1_ffn_" + n]) for n in ("Wv", "Wo")},
        "gate1": c(i["L1_ffn_gate_w"]), "gate1_b": c(i["L1_ffn_gate_b"].reshape(1, EXPERTS)),
        **{n: c(i["L1_ffn_" + n].reshape(1, D)) for n in ("ln1_g", "ln1_b", "ln2_g", "ln2_b")},
        "w1": experts_pack(i["L1_ffn_W1"], i["L1_ffn_W2"], i["L1_ffn_b1"], i["L1_ffn_b2"]),
        "a_w": c(i["L1_attn_Wqkv_w"].T),
        "a_wo": c(i["L1_attn_Wo_w"].T.reshape(PAIRS_A, P, D).transpose(1, 0, 2)),
        "a_bq": c(i["L1_attn_Wqkv_b"][0:QKV].reshape(PAIRS_A, P).T),
        "a_bk": c(i["L1_attn_Wqkv_b"][QKV:2 * QKV].reshape(PAIRS_A, P).T),
        "a_bv": c(i["L1_attn_Wqkv_b"][2 * QKV:].reshape(1, QKV)), "a_bo": c(i["L1_attn_Wo_b"].reshape(1, D)),
        "ghost": c(i["L1_attn_ghost"].reshape(1, HEADS_A)),
        **{"f_" + n: by_channel(i["L1_ffn_" + n].reshape(1, D)).reshape(D, 1) for n in ("bq", "bk")},
        "f_bv": c(i["L1_ffn_bv"].reshape(1, D)), "f_bo": c(i["L1_ffn_bo"].reshape(1, D)),
    }


def kernel(**inputs):
    import numpy as np
    import concourse.bacc as bacc
    from concourse.bass_utils import run_bass_kernel_spmd

    nc = bacc.Bacc("TRN2", target_bir_lowering=False, num_devices=1)
    arrays, d = {}, {}
    for name, a in layout(inputs).items():
        arrays["in_" + name] = a
        d[name] = nc.dram_tensor("in_" + name, a.shape, mybir.dt.from_np(a.dtype), kind="ExternalInput").ap()
    d["out"] = nc.dram_tensor("out_rows", (TOKENS, D), F32, kind="ExternalOutput").ap()
    program(nc, d)
    ran = run_bass_kernel_spmd(nc, [arrays], core_ids=[0])
    return ran.results[0]["out_rows"].reshape(BATCH, SEQ, D)
```
